# Optimizing a Trainium2 kernel written in Bass

```python
import numpy as np
import jax
import jax.numpy as jnp

def _softmax(x, axis=-1):
    return jax.nn.softmax(x, axis=axis)

def _gelu(x):
    return jax.nn.gelu(x, approximate=True)

def _silu(x):
    return jax.nn.silu(x)

def _sigmoid(x):
    return jax.nn.sigmoid(x)

def _layernorm(x, axis=-1, eps=1e-05):
    m = jnp.mean(x, axis=axis, keepdims=True)
    v = jnp.var(x, axis=axis, keepdims=True)
    return (x - m) / jnp.sqrt(v + eps)

def _scatter_add(tgt, idx, src, axis=0):
    return tgt.at[idx].add(src)

def _segment_sum(src, seg, n):
    return jax.ops.segment_sum(src, seg, n)
kernel_name = 'mk_decoder_preln_d1_seqx_r8_8033e1'

def setup_inputs(seed: int=0):
    np.random.seed(seed)
    _w = jnp.asarray

    def _rec_inputs():
        import jax
        import jax.numpy as jnp
        _rk = jax.random.key(seed)
        x = -0.0002928 + 1 * jax.random.normal(jax.random.fold_in(_rk, 1), (8, 256, 128), jnp.float32)
        _lenS = 256 - jax.random.randint(jax.random.fold_in(_rk, 7), (8,), 0, max(1, 256 // 4) + 1, jnp.int32)
        _lenS2 = 1601 - jax.random.randint(jax.random.fold_in(_rk, 8), (8,), 0, max(1, 1601 // 4) + 1, jnp.int32)
        _ctx_1024P = jax.random.normal(jax.random.fold_in(_rk, 11), (8, 16, 128), jnp.float32)
        _ctx_1024c = jax.random.dirichlet(jax.random.fold_in(_rk, 511), 0.3 * jnp.ones((16,), jnp.float32), (8, 1601))
        _ctx_1024t = jnp.einsum('bsk,bkd->bsd', _ctx_1024c, _ctx_1024P)
        _ctx_1024t = _ctx_1024t * jax.lax.rsqrt(jnp.mean(jnp.square(_ctx_1024t)) + 1e-12) * 0.953939
        ctx_1024 = -1.39393e-06 + 0.999914 * (_ctx_1024t + 0.3 * jax.random.normal(jax.random.fold_in(_rk, 611), (8, 1601, 128), jnp.float32))
        fside_BxS2_0 = jax.random.uniform(jax.random.fold_in(_rk, 12), (8, 1601), jnp.float32, 0.0, 0.999833)
        return (x, ctx_1024, fside_BxS2_0)
    x, ctx_1024, fside_BxS2_0 = _rec_inputs()

    def _L0_attn_setup():
        import jax, jax.numpy as jnp
        import numpy as np
        D_MODEL = 128
        N_HEADS = 16
        D_K = D_MODEL // N_HEADS

        def _rope_cache(T, dtype):
            half = D_K // 2
            freq = 1.0 / 10000.0 ** (2.0 * jnp.arange(half, dtype=dtype) / D_K)
            angles = jnp.arange(T, dtype=dtype)[:, None] * freq[None, :]
            return (jnp.cos(angles), jnp.sin(angles))

        def _apply_rope(x, cos, sin):
            half = x.shape[-1] // 2
            x1, x2 = (x[..., :half], x[..., half:])
            return jnp.concatenate([x1 * cos - x2 * sin, x1 * sin + x2 * cos], axis=-1)
        key = jax.random.key(seed)
        ks = jax.random.split(key, 9)
        s = 0.02
        return {'x': jax.random.normal(ks[0], (4, 256, D_MODEL), dtype=jnp.float32), 'WQ_w': jax.random.normal(ks[1], (D_MODEL, D_MODEL), dtype=jnp.float32) * s, 'WQ_b': jax.random.normal(ks[2], (D_MODEL,), dtype=jnp.float32) * s, 'WK_w': jax.random.normal(ks[3], (D_MODEL, D_MODEL), dtype=jnp.float32) * s, 'WK_b': jax.random.normal(ks[4], (D_MODEL,), dtype=jnp.float32) * s, 'WV_w': jax.random.normal(ks[5], (D_MODEL, D_MODEL), dtype=jnp.float32) * s, 'WV_b': jax.random.normal(ks[6], (D_MODEL,), dtype=jnp.float32) * s, 'Wo_w': jax.random.normal(ks[7], (D_MODEL, D_MODEL), dtype=jnp.float32) * s, 'Wo_b': jax.random.normal(ks[8], (D_MODEL,), dtype=jnp.float32) * s}
    _L0_attn_all = _L0_attn_setup()
    _L0_attn_in = {k: v for k, v in _L0_attn_all.items() if k in ('WQ_w', 'WQ_b', 'WK_w', 'WK_b', 'WV_w', 'WV_b', 'Wo_w', 'Wo_b')}
    del _L0_attn_all

    def _L0_xattn_setup():
        import jax, jax.numpy as jnp
        import numpy as np
        D_MODEL = 128
        N_HEADS = 16
        D_K = D_MODEL // N_HEADS

        def _split_heads(x):
            B, S, _ = x.shape
            return x.reshape(B, S, N_HEADS, D_K).transpose(0, 2, 1, 3)
        key = jax.random.key(seed)
        ks = jax.random.split(key, 12)
        B, S = (2, 256)
        scale = 1.0 / np.sqrt(D_MODEL)
        inp = {'query': jax.random.normal(ks[0], (B, S, D_MODEL), jnp.float32), 'key': jax.random.normal(ks[1], (B, S, D_MODEL), jnp.float32), 'value': jax.random.normal(ks[2], (B, S, D_MODEL), jnp.float32), 'weights': jax.random.uniform(ks[3], (B, S), jnp.float32), 'wq': jax.random.normal(ks[4], (D_MODEL, D_MODEL), jnp.float32) * scale, 'bq': jnp.zeros((D_MODEL,), jnp.float32), 'wk': jax.random.normal(ks[5], (D_MODEL, D_MODEL), jnp.float32) * scale, 'bk': jnp.zeros((D_MODEL,), jnp.float32), 'wv': jax.random.normal(ks[6], (D_MODEL, D_MODEL), jnp.float32) * scale, 'bv': jnp.zeros((D_MODEL,), jnp.float32), 'wo': jax.random.normal(ks[7], (D_MODEL, D_MODEL), jnp.float32) * scale, 'bo': jnp.zeros((D_MODEL,), jnp.float32)}
        return inp
    _L0_xattn_all = _L0_xattn_setup()
    _L0_xattn_in = {k: v for k, v in _L0_xattn_all.items() if k in ('wq', 'bq', 'wk', 'bk', 'wv', 'bv', 'wo', 'bo')}
    del _L0_xattn_all

    def _L0_ffn_setup():
        import jax, jax.numpy as jnp
        import numpy as np
        B, S, D, E, F, K = (4, 256, 128, 8, 256, 2)
        key = jax.random.key(seed)
        k0, k1, k2, k3, k4 = jax.random.split(key, 5)
        x = jax.random.normal(k0, (B, S, D), dtype=jnp.float32)
        bound = 1.0 / np.sqrt(D)
        gate_w = jax.random.uniform(k1, (E, D), jnp.float32, -bound, bound)
        w_gate = jax.random.normal(k2, (E, D, F), dtype=jnp.float32) * 0.02
        w_up = jax.random.normal(k3, (E, D, F), dtype=jnp.float32) * 0.02
        w_down = jax.random.normal(k4, (E, F, D), dtype=jnp.float32) * 0.02
        return {'x': x, 'gate_w': gate_w, 'w_gate': w_gate, 'w_up': w_up, 'w_down': w_down}
    _L0_ffn_all = _L0_ffn_setup()
    _L0_ffn_in = {k: v for k, v in _L0_ffn_all.items() if k in ('gate_w', 'w_gate', 'w_up', 'w_down')}
    del _L0_ffn_all
    return {'x': x, 'ctx_1024': ctx_1024, 'fside_BxS2_0': fside_BxS2_0, 'L0_attn_WQ_w': _L0_attn_in['WQ_w'], 'L0_attn_WQ_b': _L0_attn_in['WQ_b'], 'L0_attn_WK_w': _L0_attn_in['WK_w'], 'L0_attn_WK_b': _L0_attn_in['WK_b'], 'L0_attn_WV_w': _L0_attn_in['WV_w'], 'L0_attn_WV_b': _L0_attn_in['WV_b'], 'L0_attn_Wo_w': _L0_attn_in['Wo_w'], 'L0_attn_Wo_b': _L0_attn_in['Wo_b'], 'L0_xattn_wq': _L0_xattn_in['wq'], 'L0_xattn_bq': _L0_xattn_in['bq'], 'L0_xattn_wk': _L0_xattn_in['wk'], 'L0_xattn_bk': _L0_xattn_in['bk'], 'L0_xattn_wv': _L0_xattn_in['wv'], 'L0_xattn_bv': _L0_xattn_in['bv'], 'L0_xattn_wo': _L0_xattn_in['wo'], 'L0_xattn_bo': _L0_xattn_in['bo'], 'L0_ffn_gate_w': _L0_ffn_in['gate_w'], 'L0_ffn_w_gate': _L0_ffn_in['w_gate'], 'L0_ffn_w_up': _L0_ffn_in['w_up'], 'L0_ffn_w_down': _L0_ffn_in['w_down']}

def reference(x, ctx_1024, fside_BxS2_0, L0_attn_WQ_w, L0_attn_WQ_b, L0_attn_WK_w, L0_attn_WK_b, L0_attn_WV_w, L0_attn_WV_b, L0_attn_Wo_w, L0_attn_Wo_b, L0_xattn_wq, L0_xattn_bq, L0_xattn_wk, L0_xattn_bk, L0_xattn_wv, L0_xattn_bv, L0_xattn_wo, L0_xattn_bo, L0_ffn_gate_w, L0_ffn_w_gate, L0_ffn_w_up, L0_ffn_w_down):
    import jax
    import jax.numpy as jnp

    def _L0_attn_ref(x, WQ_w, WQ_b, WK_w, WK_b, WV_w, WV_b, Wo_w, Wo_b):
        import jax, jax.numpy as jnp
        import numpy as np
        D_MODEL = 128
        N_HEADS = 16
        D_K = D_MODEL // N_HEADS

        def _rope_cache(T, dtype):
            half = D_K // 2
            freq = 1.0 / 10000.0 ** (2.0 * jnp.arange(half, dtype=dtype) / D_K)
            angles = jnp.arange(T, dtype=dtype)[:, None] * freq[None, :]
            return (jnp.cos(angles), jnp.sin(angles))

        def _apply_rope(x, cos, sin):
            half = x.shape[-1] // 2
            x1, x2 = (x[..., :half], x[..., half:])
            return jnp.concatenate([x1 * cos - x2 * sin, x1 * sin + x2 * cos], axis=-1)
        B, T, D = x.shape

        def proj(w, b):
            y = jnp.einsum('btd,ed->bte', x, w) + b
            return y.reshape(B, T, N_HEADS, D_K).transpose(0, 2, 1, 3)
        q = proj(WQ_w, WQ_b)
        k = proj(WK_w, WK_b)
        v = proj(WV_w, WV_b)
        cos, sin = _rope_cache(T, x.dtype)
        q = _apply_rope(q, cos, sin)
        k = _apply_rope(k, cos, sin)
        scores = jnp.einsum('bhqd,bhkd->bhqk', q, k) / jnp.sqrt(jnp.asarray(D_K, x.dtype))
        causal = jnp.tril(jnp.ones((T, T), dtype=bool))
        scores = jnp.where(causal[None, None, :, :], scores, -jnp.inf)
        attn = jax.nn.softmax(scores, axis=-1)
        out = jnp.einsum('bhqk,bhkd->bhqd', attn, v)
        out = out.transpose(0, 2, 1, 3).reshape(B, T, D)
        return jnp.einsum('btd,ed->bte', out, Wo_w) + Wo_b

    def _L0_xattn_ref(query, key, value, weights, wq, bq, wk, bk, wv, bv, wo, bo):
        import jax, jax.numpy as jnp
        import numpy as np
        D_MODEL = 128
        N_HEADS = 16
        D_K = D_MODEL // N_HEADS

        def _split_heads(x):
            B, S, _ = x.shape
            return x.reshape(B, S, N_HEADS, D_K).transpose(0, 2, 1, 3)
        Q = _split_heads(query @ wq + bq)
        K = _split_heads(key @ wk + bk)
        V = _split_heads(value @ wv + bv)
        scores = jnp.einsum('bhqd,bhkd->bhqk', Q, K) / np.sqrt(D_K)
        log_w = jnp.log(weights + 1e-20)[:, None, None, :]
        attn = jax.nn.softmax(scores + log_w, axis=-1)
        out = jnp.einsum('bhqk,bhkd->bhqd', attn, V)
        B, H, S, Dk = out.shape
        out = out.transpose(0, 2, 1, 3).reshape(B, S, D_MODEL)
        return out @ wo + bo

    def _L0_ffn_ref(x, gate_w, w_gate, w_up, w_down):
        import jax, jax.numpy as jnp
        import numpy as np
        B, S, D, E, F, K = (4, 256, 128, 8, 256, 2)
        b, s, d = x.shape
        e = gate_w.shape[0]
        xf = x.reshape(-1, d)
        n = xf.shape[0]
        logits = xf @ gate_w.T
        scores = jax.nn.softmax(logits, axis=-1)
        topk_w, topk_idx = jax.lax.top_k(scores, K)
        topk_w = topk_w / (topk_w.sum(axis=-1, keepdims=True) + 1e-20)
        cw = jnp.zeros((n, e), dtype=xf.dtype).at[jnp.arange(n)[:, None], topk_idx].add(topk_w)
        h = jax.nn.silu(jnp.einsum('nd,edf->enf', xf, w_gate)) * jnp.einsum('nd,edf->enf', xf, w_up)
        outs = jnp.einsum('enf,efd->end', h, w_down)
        y = jnp.einsum('ne,end->nd', cw, outs)
        return y.reshape(b, s, d)
    x = x + _L0_attn_ref(_layernorm(x, axis=-1), L0_attn_WQ_w, L0_attn_WQ_b, L0_attn_WK_w, L0_attn_WK_b, L0_attn_WV_w, L0_attn_WV_b, L0_attn_Wo_w, L0_attn_Wo_b)
    x = x + _L0_xattn_ref(_layernorm(x, axis=-1), ctx_1024, ctx_1024, fside_BxS2_0, L0_xattn_wq, L0_xattn_bq, L0_xattn_wk, L0_xattn_bk, L0_xattn_wv, L0_xattn_bv, L0_xattn_wo, L0_xattn_bo)
    x = x + _L0_ffn_ref(_layernorm(x, axis=-1), L0_ffn_gate_w, L0_ffn_w_gate, L0_ffn_w_up, L0_ffn_w_down)
    return x

_drawn_inputs = setup_inputs


def setup_inputs(seed=0):
    import zlib

    import numpy as np

    out = dict(_drawn_inputs(seed))
    spreads = {'L0_xattn_bq': (0.0, 0.355),
     'L0_xattn_bk': (0.0, 0.8),
     'L0_xattn_bv': (0.0, 0.1),
     'L0_xattn_bo': (0.0, 0.1)}
    factors = {'fside_BxS2_0': 2.698,
     'L0_attn_WQ_w': 8.0,
     'L0_attn_WQ_b': 8.0,
     'L0_attn_WK_w': 8.0,
     'L0_attn_WK_b': 8.0,
     'L0_attn_WV_w': 8.0,
     'L0_attn_WV_b': 8.0,
     'L0_attn_Wo_w': 7.003,
     'L0_attn_Wo_b': 3.057,
     'L0_ffn_gate_w': 8.0,
     'L0_ffn_w_gate': 8.0,
     'L0_ffn_w_up': 8.0,
     'L0_ffn_w_down': 8.0}
    for name, (base, spread) in spreads.items():
        noise = np.random.default_rng([zlib.crc32(name.encode()), seed]).standard_normal(out[name].shape)
        drawn = base * np.exp(spread * noise) if base else spread * noise
        out[name] = jnp.asarray(drawn.astype(out[name].dtype))
    for name, factor in factors.items():
        out[name] = (out[name] * factor).astype(out[name].dtype)
    return out
```

```python
from contextlib import ExitStack

import numpy as np

import concourse.bass as bass
from concourse import mybir

F32 = mybir.dt.float32
BF16 = mybir.dt.bfloat16
ALU = mybir.AluOpType
ACT = mybir.ActivationFunctionType
AX = mybir.AxisListType

B, T, D, H = 8, 256, 128, 16
DK = D // H
S2 = 1601
E, F = 8, 256
N = B * T
P = 128
NT = N // P
TT = T // P
EPS = 1e-5
SCALE = DK ** -0.5
MASKED = -1e30

G = 4
GJ = 2 * G
KT = -(-S2 // P)
LAST = S2 - (KT - 1) * P
CH = 4
CW = [S2 // CH + (i < S2 % CH) for i in range(CH)]
CO = [sum(CW[:i]) for i in range(CH)]
VW = DK + 1

K_PART = [1, 2, 1, 2, 1, 3]
Q_PART = [1, 1, 2, 2, 3, 1]
NPROD = len(K_PART)
TOP = 3
PROWS = NPROD * DK
MP = 3
KROWS = MP + PROWS

LOG_SHIFT = 20

CK = 512
NC = N // CK
CT = CK // P


def sems(nc, ctx, names):
    return [ctx.enter_context(nc.semaphore(n)) for n in names.split()]


def context_stage(nc, io, scr, banks, kp, vb, lp, stored, stored_log):
    NST = NPROD + 1
    with ExitStack() as ctx:
        def sb(name, shape, dt=F32):
            return ctx.enter_context(nc.sbuf_tensor("c_" + name, shape, dt))
        wk, wv, bk, bv = sb("wk", [D, D]), sb("wv", [D, D]), sb("bk", [D, 1]), sb("bv", [P, D])
        cx = [sb(f"ctx{i}", [D, S2]) for i in range(2)]
        rest = [sb(f"rest{i}", [D, S2]) for i in range(2)]
        fw, lw, lrest = sb("fw", [B, S2]), sb("lw", [B, S2]), sb("lrest", [B, S2])
        lbias = sb("lbias", [B, 1])
        (w_in, fw_in, proj, k_first, k_rest, k_second, k_third, v_done, ones_set, log_steps) = sems(
            nc, ctx, "c_w_in c_fw_in c_proj c_k_first c_k_rest c_k_second c_k_third c_v_done "
                     "c_ones_set c_log_steps")
        ctx_in = sems(nc, ctx, "c_ctx_in0 c_ctx_in1")
        PB = 2 * CH
        with nc.Block() as block:

            @block.sync
            def _(sp):
                for dst, src in ((wk, io["xwk"]), (bk, io["xbk"]), (wv, io["xwv"]), (bv, io["xbv"])):
                    sp.dma_start(dst[:], src).then_inc(w_in, 16)
                for i in range(2):
                    sp.dma_start(cx[i][:], io["ctxT"][:, i * S2:(i + 1) * S2]).then_inc(ctx_in[i], 16)
                    sp.sem_inc(stored[i], 16 * NST)
                sp.dma_start(fw[:], io["weights"]).then_inc(fw_in, 16)

                def store(b, i):
                    sp.wait_ge(k_third, b + 1)
                    for r in range(NPROD):
                        one = slice(b, b + 1) if isinstance(b, int) else bass.ds(b, 1)
                        sp.dma_start(scr["ks"][one, :, MP + DK * r:MP + DK * (r + 1), :, :]
                                     .rearrange("o c r n k -> (o c) (r n) k"),
                                     kp[i][K_PART[r] - 1][:]).then_inc(stored[i], 16)
                    sp.wait_ge(v_done, CH * (b + 1))
                    sp.dma_start(scr["v"][one].rearrange("o p v -> (o p) v"),
                                 vb[i][:].rearrange("p g t v -> p (g t v)"))\
                      .then_inc(stored[i], 16)

                with sp.Fori(0, B // 2 - 1) as it:
                    for i in range(2):
                        b = it * 2 + i
                        sp.wait_ge(proj, PB * (b + 1))
                        sp.dma_start(cx[i][:], io["ctxT"][:, bass.ds((b + 2) * S2, S2)])\
                          .then_inc(ctx_in[i], 16)
                        store(b, i)
                for i in range(2):
                    store(B - 2 + i, i)
                sp.wait_ge(log_steps, 7)
                for j in range(MP):
                    for par in range(2):
                        sp.dma_start(scr["ks"][:, par, j, :, :],
                                     lp[j][:].unsqueeze(1).broadcast_to([B, GJ, S2]))\
                          .then_inc(stored_log, 16)

            @block.tensor
            def _(pe):
                pe.wait_ge(w_in, 64)

                def batch(b, i, it, first):
                    pe.wait_ge(ctx_in[i], it * 16 + 16)
                    for c in range(CH):
                        if not first:
                            pe.wait_ge(k_rest, CH * (b - 1) + c + 1)
                        pe.matmul(banks[c][:, 0:CW[c]], wk[:], cx[i][:, CO[c]:CO[c] + CW[c]],
                                  start=True, stop=True).then_inc(proj, 1)
                    for c in range(CH):
                        if not first:
                            pe.wait_ge(v_done, CH * (b - 1) + c + 1)
                        for n, t in enumerate(range(CT * c, min(CT * (c + 1), KT))):
                            m = P if t < KT - 1 else LAST
                            mm = pe.matmul(banks[CH + c][0:m, n * D:(n + 1) * D],
                                           cx[i][:, t * P:t * P + m], wv[:], start=True, stop=True)
                        mm.then_inc(proj, 1)

                batch(0, 0, 0, True)
                batch(1, 1, 0, False)
                with pe.Fori(1, B // 2) as it:
                    for i in range(2):
                        batch(it * 2 + i, i, it, False)

            @block.scalar
            def _(act):
                act.wait_ge(w_in, 64)
                act.wait_ge(fw_in, 16)
                act.wait_ge(ones_set, 1)
                act.activation(lw[:], fw[:], ACT.Ln, bias=lbias[:], scale=float(2 ** LOG_SHIFT))\
                   .then_inc(log_steps, 1)

                def batch(b, i, it):
                    act.wait_ge(stored[i], 16 * NST * (it + 1))
                    for c in range(CH):
                        act.wait_ge(proj, PB * b + c + 1)
                        act.activation(kp[i][0][:, CO[c]:CO[c] + CW[c]], banks[c][:, 0:CW[c]],
                                       ACT.Identity, bias=bk[:]).then_inc(k_first, 1)
                    act.wait_ge(k_rest, CH * (b + 1))
                    act.copy(kp[i][1][:], rest[i][:]).then_inc(k_second, 1)

                with act.Fori(0, B // 2) as it:
                    for i in range(2):
                        batch(it * 2 + i, i, it)

            @block.vector
            def _(dve):
                dve.memset(lbias[:], 1e-20 * 2 ** LOG_SHIFT).then_inc(ones_set, 1)
                for i in range(2):
                    dve.memset(vb[i][:], 1.0).then_inc(ones_set, 1)
                dve.wait_ge(ones_set, 3)
                dve.wait_ge(log_steps, 1)
                dve.tensor_scalar(lw[:], lw[:], -LOG_SHIFT * float(np.log(2.0)), None, ALU.add)\
                   .then_inc(log_steps, 1)
                dve.wait_ge(log_steps, 2)
                dve.tensor_copy(lp[0][:], lw[:]).then_inc(log_steps, 1)
                dve.wait_ge(log_steps, 3)
                dve.tensor_tensor(lrest[:], lw[:], lp[0][:], ALU.subtract).then_inc(log_steps, 1)
                dve.wait_ge(log_steps, 4)
                dve.tensor_copy(lp[1][:], lrest[:]).then_inc(log_steps, 1)
                dve.wait_ge(log_steps, 5)
                dve.tensor_tensor(lrest[:], lrest[:], lp[1][:], ALU.subtract).then_inc(log_steps, 1)
                dve.wait_ge(log_steps, 6)
                dve.tensor_copy(lp[2][:], lrest[:]).then_inc(log_steps, 1)

                def batch(b, i, it):
                    for c in range(CH):
                        dve.wait_ge(k_first, CH * b + c + 1)
                        o = slice(CO[c], CO[c] + CW[c])
                        dve.scalar_tensor_tensor(out=rest[i][:, o], in0=banks[c][:, 0:CW[c]],
                                                 scalar=bk[:], in1=kp[i][0][:, o], op0=ALU.add,
                                                 op1=ALU.subtract).then_inc(k_rest, 1)
                    dve.wait_ge(stored[i], 16 * NST * (it + 1))
                    for c in range(CH):
                        dve.wait_ge(proj, PB * b + CH + c + 1)
                        nt = min(CT, KT - CT * c)
                        m = P if c < CH - 1 else LAST
                        for g in range(G):
                            ins = dve.tensor_tensor(
                                vb[i][0:m, g, CT * c:CT * c + nt, :]
                                .rearrange("p t (h v) -> p t h v", h=4)[:, :, :, 0:DK],
                                banks[CH + c][0:m, 0:nt * D]
                                .rearrange("p (t e) -> p t e", e=D)[:, :, 32 * g:32 * g + 32]
                                .rearrange("p t (h d) -> p t h d", h=4),
                                bv[0:m, 32 * g:32 * g + 32].rearrange("p (h d) -> p h d", h=4)
                                .unsqueeze(1).broadcast_to([m, nt, 4, DK]), ALU.add)
                        ins.then_inc(v_done, 1)
                    dve.wait_ge(k_second, b + 1)
                    dve.tensor_tensor(kp[i][2][:], rest[i][:], kp[i][1][:], ALU.subtract)\
                       .then_inc(k_third, 1)

                dve.wait_ge(w_in, 64)
                with dve.Fori(0, B // 2) as it:
                    for i in range(2):
                        batch(it * 2 + i, i, it)


class Norm:

    def __init__(self, nc, ctx, tag):
        self.st = ctx.enter_context(nc.sbuf_tensor(tag + "stats", [P, NT, 6], F32))
        self.mv = ctx.enter_context(nc.sbuf_tensor(tag + "meanvar", [P, NT, 2], F32))
        self.rs = ctx.enter_context(nc.sbuf_tensor(tag + "rstd", [P, NT, 2], F32))
        self.eps = ctx.enter_context(nc.sbuf_tensor(tag + "eps", [P, 1], F32))
        self.stats, self.rooted, self.ready, self.turned, self.out = sems(
            nc, ctx, " ".join(tag + n for n in "stats_s rooted_s ready_s turned_s out_s".split()))


def norm_vector(dve, nm, x, xn):
    dve.memset(nm.eps[:], EPS).then_inc(nm.stats, 1)
    for t in range(NT):
        dve.bn_stats(nm.st[:, t, :], x[:, t, :]).then_inc(nm.stats, 1)
    for t in range(NT):
        dve.wait_ge(nm.stats, 2 + t)
        dve.bn_aggr(nm.mv[:, t, :], nm.st[:, t, :]).then_inc(nm.stats, 1)
    dve.wait_ge(nm.rooted, 1)
    dve.reciprocal(nm.rs[:, :, 1], nm.rs[:, :, 0]).then_inc(nm.rooted, 1)
    dve.wait_ge(nm.rooted, 2)
    for t in range(NT):
        dve.tensor_scalar(xn[:, t, :], x[:, t, :], nm.mv[:, t, 0:1], nm.rs[:, t, 1:2],
                          ALU.subtract, ALU.mult).then_inc(nm.ready, 1)


def norm_scalar_root(act, nm):
    act.wait_ge(nm.stats, 1 + 2 * NT)
    act.activation(nm.rs[:, :, 0], nm.mv[:, :, 1], ACT.Sqrt, bias=nm.eps[:]).then_inc(nm.rooted, 1)


def norm_scalar_out(act, nm, bank2, xnT, c):
    act.wait_ge(nm.turned, c + 1)
    act.copy(xnT[:, c * CK:(c + 1) * CK], bank2[c % 2]).then_inc(nm.out, 1)


def norm_tensor(pe, nm, xn, ident, bank2, c):
    pe.wait_ge(nm.ready, CT * (c + 1))
    if c >= 2:
        pe.wait_ge(nm.out, c - 1)
    for t in range(CT):
        mm = pe.transpose(bank2[c % 2][:, t * P:(t + 1) * P], xn[:, CT * c + t, :], ident[:])
    mm.then_inc(nm.turned, 1)


def self_projection_stage(nc, io, scr, banks, x, xn, xnT, v_all, ident, identb, cst_in, stored_self):
    with ExitStack() as ctx:
        def sb(name, shape, dt=F32):
            return ctx.enter_context(nc.sbuf_tensor("p_" + name, shape, dt))
        names = ["q", "q_swap", "k", "k_swap"]
        w = {n: sb("w" + n, [D, D]) for n in names}
        bias = {n: sb("b" + n, [D, 1]) for n in names}
        wv, bv, bo = sb("wv", [D, D]), sb("bv", [P, D]), sb("bo", [P, D])
        rot = {n: sb("rot" + n, [D, T]) for n in names}
        turned = [[sb(f"t{n}{i}", [D, CK]) for i in range(2)] for n in "qk"]
        part = [[sb(f"part{n}{j}", [D, N], BF16) for j in range(3)] for n in "qk"]
        rest = [sb(f"rest{n}", [D, CK]) for n in "qk"]
        nm = Norm(nc, ctx, "p_n_")
        (w_in, x_in, proj, drained, tmp, whole, first, rest_s, second, third, biased) = sems(
            nc, ctx, "p_w_in p_x_in p_proj p_drained p_tmp p_whole p_first p_rest p_second p_third "
                     "p_biased")
        NW = 4 * 3 + 2
        PC = 5
        with nc.Block() as block:

            @block.sync
            def _(sp):
                sp.dma_start(x[:], io["x"].rearrange("(t p) d -> p t d", p=P)).then_inc(x_in, 16)
                sp.dma_start(bo[:], io["sbo"]).then_inc(x_in, 16)
                sp.dma_start(ident[:], io["ident"]).then_inc(cst_in, 16)
                for n in names:
                    sp.dma_start(w[n][:], io["w_" + n]).then_inc(w_in, 16)
                    sp.dma_start(bias[n][:], io["b_" + n]).then_inc(w_in, 16)
                    sp.dma_start(rot[n][:], io["rot_" + n]).then_inc(w_in, 16)
                sp.dma_start(wv[:], io["swv"]).then_inc(w_in, 16)
                sp.dma_start(bv[:], io["sbv"]).then_inc(w_in, 16)
                for half in range(2):
                    sp.wait_ge(third, 2 * 2 * (half + 1))
                    b0, nb = half * B // 2, B // 2
                    for which, dst, parts in ((0, "qs_self", Q_PART), (1, "ks_self", K_PART)):
                        for r in range(NPROD):
                            src = part[which][parts[r] - 1]
                            sp.dma_start(
                                scr[dst][:, DK * r:DK * (r + 1), :, b0 * T:(b0 + nb) * T]
                                .rearrange("c r n t -> c (r n) t"),
                                src[:, b0 * T:(b0 + nb) * T]).then_inc(stored_self, 16)
                sp.wait_ge(stored_self, 16 * 2 * 2 * NPROD)

            @block.tensor
            def _(pe):
                pe.wait_ge(cst_in, 16)
                for c in range(NC):
                    norm_tensor(pe, nm, xn, ident, banks[5:7], c)
                    if c == 0:
                        pe.wait_ge(w_in, 16 * NW)
                    pe.wait_ge(nm.out, c + 1)
                    for i, n in enumerate(names):
                        if c:
                            pe.wait_ge(drained, PC * (c - 1) + i + 1)
                        pe.matmul(banks[i], w[n][:], xnT[:, c * CK:(c + 1) * CK],
                                  start=True, stop=True).then_inc(proj, 1)
                    if c:
                        pe.wait_ge(drained, PC * c)
                    for t in range(CT):
                        mm = pe.matmul(banks[4][:, t * D:(t + 1) * D],
                                       xnT[:, c * CK + t * P:c * CK + (t + 1) * P], wv[:],
                                       start=True, stop=True)
                    mm.then_inc(proj, 1)

            @block.scalar
            def _(act):
                norm_scalar_root(act, nm)
                norm_scalar_out(act, nm, banks[5:7], xnT, 0)
                for c in range(NC):
                    if c + 1 < NC:
                        norm_scalar_out(act, nm, banks[5:7], xnT, c + 1)
                    o = slice(c * CK, (c + 1) * CK)
                    for i in range(2):
                        act.wait_ge(whole, 2 * c + i + 1)
                        act.copy(part[i][0][:, o], turned[i][0][:]).then_inc(first, 1)
                    for i in range(2):
                        act.wait_ge(rest_s, 2 * c + i + 1)
                        act.copy(part[i][1][:, o], rest[i][:]).then_inc(second, 1)

            @block.gpsimd
            def _(pool):
                pool.memset(v_all[:], 1.0).then_inc(biased, 1)
                pool.wait_ge(nm.ready, NT)
                pool.wait_ge(x_in, 32)
                pool.tensor_tensor(x[:], x[:], bo[:].unsqueeze(1).broadcast_to([P, NT, D]), ALU.add)\
                    .then_inc(biased, 1)

            @block.vector
            def _(dve):
                dve.wait_ge(x_in, 32)
                norm_vector(dve, nm, x, xn)
                dve.wait_ge(cst_in, 16)
                dve.tensor_copy(identb[:], ident[:])
                dve.wait_ge(w_in, 16 * NW)
                dve.wait_ge(biased, 1)
                steps = 0
                for c in range(NC):
                    o = slice(c * CK, (c + 1) * CK)
                    for i in range(2):
                        if c:
                            dve.wait_ge(first, 2 * (c - 1) + i + 1)
                        for s in range(2):
                            n = names[2 * i + s]
                            dve.wait_ge(proj, PC * c + 2 * i + s + 1)
                            dve.scalar_tensor_tensor(
                                out=turned[i][s][:].rearrange("p (b t) -> p b t", t=T),
                                in0=banks[2 * i + s].rearrange("p (b t) -> p b t", t=T),
                                scalar=bias[n][:],
                                in1=rot[n][:].unsqueeze(1).broadcast_to([P, CK // T, T]),
                                op0=ALU.add, op1=ALU.mult).then_inc(drained, 1)
                        dve.wait_ge(drained, PC * c + 2 * i + 2)
                        dve.tensor_tensor(turned[i][0][:], turned[i][0][:], turned[i][1][:], ALU.add)\
                           .then_inc(whole, 1)
                    dve.wait_ge(proj, PC * c + 5)
                    dve.tensor_tensor(
                        v_all[:, CT * c:CT * (c + 1), :, 0:DK],
                        banks[4].rearrange("p (t h d) -> p t h d", t=CT, h=H),
                        bv[:].rearrange("p (h d) -> p h d", h=H).unsqueeze(1)
                        .broadcast_to([P, CT, H, DK]), ALU.add).then_inc(drained, 1)
                    for i in range(2):
                        dve.wait_ge(first, 2 * c + i + 1)
                        dve.tensor_tensor(rest[i][:], turned[i][0][:], part[i][0][:, o], ALU.subtract)\
                           .then_inc(rest_s, 1)
                    for i in range(2):
                        dve.wait_ge(second, 2 * c + i + 1)
                        dve.tensor_tensor(part[i][2][:, o], rest[i][:], part[i][1][:, o], ALU.subtract)\
                           .then_inc(third, 1)


SU = 2 * G
SA = 12
SRING = SA + 1 + G + 1


def self_banks():
    return [(par, 1, 2 * i, 2) for i in range(G) for par in range(2)] + \
           [(par, 0, 4 * i, 4) for i in range(2) for par in range(2)]


def self_ring(u, first, last):
    jobs = []
    if u == 1 and not first:
        jobs.append(("denominators", G - 1))
    if u == 2 and not first:
        jobs.append(("output", 0))
    if u in (3, 5, 7):
        jobs.append(("denominators", (u - 3) // 2))
    if not last and 2 <= u <= 4:
        jobs += [("scores", a) for a in range(4 * (u - 2), 4 * (u - 1))]
    if not last and u == 6:
        jobs.append(("maxima", 0))
    return jobs


def over_pairs(eng, batch):
    batch(0, 0, 0, True, False)
    with eng.Fori(0, B // 2 - 1) as i:
        batch(i * 2 + 1, 1, i, False, False)
        batch(i * 2 + 2, 0, i + 1, False, False)
    batch(B - 1, 1, B // 2 - 1, False, True)


def self_attention_stage(nc, io, scr, ring, S4, U, x, v_all, identb):
    with ExitStack() as ctx:
        def sb(name, shape, dt=F32):
            return ctx.enter_context(nc.sbuf_tensor("s_" + name, shape, dt))
        kb = [sb(f"k{i}", [P, GJ, T], BF16) for i in range(2)]
        qb = [sb(f"q{i}", [P, GJ, T], BF16) for i in range(2)]
        vv = [sb(f"v{i}", [P, TT, H, VW]) for i in range(2)]
        mask32 = sb("mask32", [P, 2, P])
        mask = sb("mask", [P, 2, 4, P], BF16)
        sel, wo = sb("sel", [P, P]), sb("wo", [P, G, D])
        probs = sb("probs", [P, 4, 2, 2 * T])
        nmax, nrest, zero = (sb(n, [P, 2, 2 * GJ]) for n in ("nmax", "nrest", "zero"))
        mparts = sb("mparts", [P, 2, MP, 2 * GJ], BF16)
        mrows = sb("mrows", [4 * MP * GJ, P], BF16)
        ub = [sb(f"u{i}", [P, T]) for i in range(2)]
        rec = [sb(f"rec{i}", [P, T]) for i in range(2)]
        y = sb("y", [P, G, T])
        (w_in, set_up, filled, drained, scored, exped, valued, evac, normed, msplit, m0, m1) = sems(
            nc, ctx, "s_w_in s_set_up s_ring_filled s_ring_drained s_scored s_exped s_valued s_evac "
                     "s_normed s_msplit s_max_in0 s_max_in1")
        m_in = [m0, m1]
        load_in = sems(nc, ctx, "s_load_in0 s_load_in1")
        S = S4.rearrange("p (u c w) -> p u c w", u=2, c=2)
        MC = 2 * GJ * MP
        NL = 5

        def base(b, first):
            return SA + 1 if first else (b - 1) * SRING + SA + 1 + SRING - 2

        AFTER = (B - 2) * SRING + SA + 1 + SRING - 2 + 5

        with nc.Block() as block:

            @block.sync
            def _(sp):
                sp.dma_start(mask32[:], io["masks"]).then_inc(w_in, 16)
                sp.dma_start(sel[:], io["sel"]).then_inc(w_in, 16)
                sp.dma_start(wo[:], io["swo"]).then_inc(w_in, 16)
                sp.wait_ge(set_up, 6)

                def load(b, s):
                    for par in range(2):
                        for dst, name in ((kb, "ks_self"), (qb, "qs_self")):
                            toks = slice(b * T, (b + 1) * T) if isinstance(b, int) else bass.ds(b * T, T)
                            sp.dma_start(dst[s][64 * par:64 * par + PROWS, :, :],
                                         scr[name][par, :, :, toks])\
                              .then_inc(load_in[s], 16)
                    vsrc = v_all[:, TT * b:TT * (b + 1)] if isinstance(b, int) else \
                        v_all[:, bass.ds(b * TT, TT)]
                    sp.dma_start(vv[s][:].rearrange("p t h v -> p (t h v)"),
                                 vsrc.rearrange("p t h v -> p (t h v)")).then_inc(load_in[s], 16)

                def maxima_rows(use, s):
                    sp.wait_ge(drained, use + 1)
                    for par in range(2):
                        sp.dma_start(qb[s][64 * par + PROWS:64 * par + PROWS + MP, :, :]
                                     .rearrange("p j q -> p (j q)"),
                                     mrows[MC * par:MC * (par + 1), :]).then_inc(m_in[s], 16)

                load(0, 0)
                load(1, 1)
                maxima_rows(SA, 0)

                def batch(b, s, half, first, last):
                    if not first and not last:
                        sp.wait_ge(valued, SU * b)
                        load(b + 1, 1 - s)
                    n = base(b, first)
                    for u in range(SU):
                        for kind, a in self_ring(u, first, last):
                            if kind == "maxima":
                                maxima_rows(n, 1 - s)
                            n = n + 1

                over_pairs(sp, batch)

            @block.tensor
            def _(pe):
                pe.wait_ge(w_in, 48)
                pe.wait_ge(set_up, 6)

                def scores_rows(use, r, s, a, wait):
                    par, qt, gj, cnt = self_banks()[a]
                    if wait:
                        pe.wait_ge(drained, use - 2)
                    keys = (qt + 1) * P
                    rows = slice(64 * par, 64 * par + TOP * DK)
                    for n in range(cnt):
                        pe.matmul(ring[r][:, n * keys:(n + 1) * keys],
                                  qb[s][rows, gj + n, qt * P:(qt + 1) * P], kb[s][rows, gj + n, 0:keys],
                                  start=(n == 0), stop=False, skip_group_check=True)
                    out = ring[r][:].rearrange("p (n k) -> p n k", n=cnt)[:, :, qt * P:keys]
                    pe.matmul(out, identb[:], mask[:, 0, 0:cnt, :], start=False, stop=True,
                              skip_group_check=True).then_inc(filled, 1)

                def turn_maxima(use, r, nsplit):
                    pe.wait_ge(msplit, nsplit)
                    pe.wait_ge(drained, use - 2)
                    pe.transpose(ring[r][:].bitcast(BF16)[0:2 * MC, 0:P],
                                 mparts[:].rearrange("p c m n -> p (c m n)"), identb[:])\
                      .then_inc(filled, 1)

                def denominators(use, r, group, gn):
                    pe.wait_ge(evac, gn + 1)
                    pe.wait_ge(drained, use - 2)
                    pe.matmul(ring[r][:, 0:T], sel[:], ub[group % 2][:], start=True, stop=True)\
                      .then_inc(filled, 1)

                def output(use, r, groups):
                    pe.wait_ge(normed, groups)
                    pe.wait_ge(drained, use - 2)
                    for t in range(TT):
                        for g in range(G):
                            mm = pe.matmul(ring[r][:, t * D:(t + 1) * D], y[:, g, t * P:(t + 1) * P],
                                           wo[:, g, :], start=(g == 0), stop=(g == G - 1))
                    mm.then_inc(filled, 1)

                def values(n, u, s, gn):
                    g, kt = u // 2, u % 2
                    pe.wait_ge(exped, n + 1)
                    if kt == 0 and gn is not None:
                        pe.wait_ge(evac, gn)
                    for par in range(2):
                        for j in range(2):
                            t, w = 2 * par + j, T - kt * P
                            mm = pe.matmul(U[32 * t:32 * t + VW, kt * P:T],
                                           vv[s][:, kt, 4 * g + 2 * j + par, :],
                                           probs[:, u % 4, par, j * w:(j + 1) * w],
                                           start=(kt == 0), stop=(kt == 1), skip_group_check=True)
                    mm.then_inc(valued, 1)

                pe.wait_ge(load_in[0], 16 * NL)
                for a in range(SA):
                    scores_rows(a, a % 3, 0, a, a >= 3)
                turn_maxima(SA, SA % 3, 4)

                def batch(b, s, half, first, last):
                    n0, rb = b * SU, (SA + 1 if first else SA + 1 + SRING - 2)
                    use, k = base(b, first), 0
                    for u in range(SU):
                        g, kt = u // 2, u % 2
                        if u == 0:
                            pe.wait_ge(load_in[s], (half + 1) * 16 * NL)
                            pe.wait_ge(m_in[s], (half + 1) * 32)
                        if not (first and u < 2):
                            pe.wait_ge(exped, n0 + u - 1)
                        w = T - kt * P
                        for par in range(2):
                            rows = slice(64 * par, 64 * par + PROWS + MP)
                            for j in range(2):
                                pe.matmul(S[:, u % 2, par, j * w:(j + 1) * w],
                                          kb[s][rows, 2 * g + j, kt * P:(kt + 1) * P],
                                          qb[s][rows, 2 * g + j, kt * P:T],
                                          start=(j == 0), stop=False, skip_group_check=True)
                        for par in range(2):
                            mm = pe.matmul(
                                S[:, u % 2, par, 0:2 * w].rearrange("p (j q) -> p j q", j=2)[:, :, 0:P],
                                identb[:], mask[:, 1, 0:2, :], start=False, stop=True,
                                skip_group_check=True)
                        mm.then_inc(scored, 1)
                        for kind, a in self_ring(u, first, last):
                            r = (rb + k) % 3
                            if kind == "scores":
                                if a == 0:
                                    pe.wait_ge(load_in[1 - s], (half + (1 + s)) * 16 * NL)
                                scores_rows(use + k, r, 1 - s, a, True)
                            elif kind == "maxima":
                                turn_maxima(use + k, r, (b + 2) * 4)
                            elif kind == "denominators":
                                gn = b * G + a - (G if u == 1 else 0)
                                denominators(use + k, r, a, gn)
                            else:
                                output(use + k, r, b * G)
                            k += 1
                        if u > 0:
                            values(n0 + u - 1, u - 1, s, None if first and u == 1 else b * G + (u - 1) // 2)
                        elif not first:
                            values(n0 - 1, SU - 1, 1 - s, None)

                over_pairs(pe, batch)
                values(B * SU - 1, SU - 1, 1, None)
                denominators(AFTER, AFTER % 3, G - 1, B * G - 1)
                output(AFTER + 1, (AFTER + 1) % 3, B * G)

            @block.scalar
            def _(act):
                def evacuate(group, gn, wait):
                    act.wait_ge(valued, gn * 2 + 2)
                    if wait:
                        act.wait_ge(normed, gn - 1)
                    act.copy(ub[group % 2][:], U[:, 0:T]).then_inc(evac, 1)

                def batch(b, s, half, first, last):
                    for u in range(SU):
                        n = b * SU + u
                        act.wait_ge(scored, n + 1)
                        if not (first and u < 4):
                            act.wait_ge(valued, n - 3)
                        w = 2 * (T - (u % 2) * P)
                        act.activation(probs[:, u % 4, :, 0:w], S[:, u % 2, :, 0:w], ACT.Exp)\
                           .then_inc(exped, 1)
                        if u % 2 == 0 and not (first and u == 0):
                            group = u // 2 - 1
                            evacuate(group % G, b * G + group, not (first and u < 6))

                over_pairs(act, batch)
                evacuate(G - 1, B * G - 1, True)

            @block.gpsimd
            def _(pool):
                for i in range(2):
                    pool.memset(kb[i][:], 1.0).then_inc(set_up, 1)

                def split(b, use):
                    pool.wait_ge(drained, use)
                    pool.tensor_tensor(mparts[:, :, 0, :], nmax[:], zero[:], ALU.add).then_inc(msplit, 1)
                    pool.wait_ge(msplit, b * 4 + 1)
                    pool.tensor_tensor(nrest[:], nmax[:], mparts[:, :, 0, :], ALU.subtract)\
                        .then_inc(msplit, 1)
                    pool.wait_ge(msplit, b * 4 + 2)
                    pool.tensor_tensor(mparts[:, :, 1, :], nrest[:], zero[:], ALU.add).then_inc(msplit, 1)
                    pool.wait_ge(msplit, b * 4 + 3)
                    pool.tensor_tensor(mparts[:, :, 2, :], nrest[:], mparts[:, :, 1, :], ALU.subtract)\
                        .then_inc(msplit, 1)

                pool.memset(zero[:], 0.0).then_inc(set_up, 1)
                pool.wait_ge(set_up, 6)
                split(0, SA)

                def batch(b, s, half, first, last):
                    n = base(b, first)
                    for u in range(SU):
                        for kind, a in self_ring(u, first, last):
                            n = n + 1
                            if kind == "scores" and a == SA - 1:
                                split(b + 1, n)

                over_pairs(pool, batch)

            @block.vector
            def _(dve):
                dve.memset(U[:], 0.0).then_inc(set_up, 1)
                dve.wait_ge(w_in, 48)
                for i in range(2):
                    dve.tensor_copy(mask[:, i, :, :], mask32[:, i, :].unsqueeze(1)
                                    .broadcast_to([P, 4, P])).then_inc(set_up, 1)

                def row_max(use, r, a):
                    par, qt, gj, cnt = self_banks()[a]
                    dve.wait_ge(filled, use + 1)
                    out = nmax[:, par, :].rearrange("p (n q) -> p n q", q=TT)[:, gj:gj + cnt, qt]
                    dve.tensor_reduce(out, ring[r][:].rearrange("p (n k) -> p n k", n=cnt), AX.X,
                                      ALU.max, negate=True).then_inc(drained, 1)

                def maxima_out(use, r, s, half, wait):
                    dve.wait_ge(filled, use + 1)
                    if wait:
                        dve.wait_ge(m_in[s], (half + 1) * 32)
                    dve.tensor_copy(mrows[:], ring[r][:].bitcast(BF16)[0:2 * MC, 0:P])\
                       .then_inc(drained, 1)

                def normalize(use, r, group):
                    dve.wait_ge(filled, use + 1)
                    dve.reciprocal(rec[group % 2][:], ring[r][:, 0:T]).then_inc(drained, 1)
                    dve.wait_ge(drained, use + 1)
                    dve.tensor_tensor(y[:, group, :], ub[group % 2][:], rec[group % 2][:], ALU.mult)\
                       .then_inc(normed, 1)

                def residual(use, r, b):
                    dve.wait_ge(filled, use + 1)
                    tiles = x[:, TT * b:TT * (b + 1), :] if isinstance(b, int) else \
                        x[:, bass.ds(b * TT, TT), :]
                    dve.tensor_tensor(tiles, ring[r][:, 0:TT * D].rearrange("p (t d) -> p t d", t=TT),
                                      tiles, ALU.add).then_inc(drained, 1)

                for a in range(SA):
                    row_max(a, a % 3, a)
                maxima_out(SA, SA % 3, 0, 0, False)

                def batch(b, s, half, first, last):
                    use, rb, k = base(b, first), (SA + 1 if first else SA + 1 + SRING - 2), 0
                    for u in range(SU):
                        for kind, a in self_ring(u, first, last):
                            r = (rb + k) % 3
                            if kind == "scores":
                                row_max(use + k, r, a)
                            elif kind == "maxima":
                                maxima_out(use + k, r, s, half, True)
                            elif kind == "denominators":
                                normalize(use + k, r, a)
                            else:
                                residual(use + k, r, b - 1)
                            k += 1

                over_pairs(dve, batch)
                normalize(AFTER, AFTER % 3, G - 1)
                residual(AFTER + 1, (AFTER + 1) % 3, B - 1)


def query_stage(nc, io, scr, banks, x, xn, xnT, ident, stored_q):
    with ExitStack() as ctx:
        def sb(name, shape, dt=F32):
            return ctx.enter_context(nc.sbuf_tensor("q_" + name, shape, dt))
        w, bias, sbias, bo = sb("w", [D, D]), sb("b", [D, 1]), sb("sb", [D, 1]), sb("bo", [P, D])
        whole = sb("whole", [D, N])
        part = [sb(f"part{j}", [D, N], BF16) for j in range(3)]
        rest = [sb(f"rest{i}", [D, CK]) for i in range(2)]
        nm = Norm(nc, ctx, "q_n_")
        (w_in, scaled, proj, first, whole_s, rest_s, second, third, biased) = sems(
            nc, ctx, "q_w_in q_scaled q_proj q_first q_whole q_rest q_second q_third q_biased")
        with nc.Block() as block:

            @block.sync
            def _(sp):
                for dst, src in ((w, io["xwq"]), (bias, io["xbq"]), (bo, io["xbo"])):
                    sp.dma_start(dst[:], src).then_inc(w_in, 16)
                for half in range(2):
                    sp.wait_ge(third, 2 * (half + 1))
                    b0, nb = half * B // 2, B // 2
                    for r in range(NPROD):
                        sp.dma_start(
                            scr["qs"][:, DK * r:DK * (r + 1), :, b0 * T:(b0 + nb) * T]
                            .rearrange("c r n t -> c (r n) t"),
                            part[Q_PART[r] - 1][:, b0 * T:(b0 + nb) * T]).then_inc(stored_q, 16)
                sp.wait_ge(stored_q, 16 * 2 * NPROD)

            @block.tensor
            def _(pe):
                for c in range(NC):
                    norm_tensor(pe, nm, xn, ident, banks[5:7], c)
                    if c == 0:
                        pe.wait_ge(w_in, 48)
                    pe.wait_ge(nm.out, c + 1)
                    pe.matmul(banks[c], w[:], xnT[:, c * CK:(c + 1) * CK],
                              start=True, stop=True).then_inc(proj, 1)

            @block.scalar
            def _(act):
                norm_scalar_root(act, nm)
                norm_scalar_out(act, nm, banks[5:7], xnT, 0)
                for c in range(NC):
                    if c + 1 < NC:
                        norm_scalar_out(act, nm, banks[5:7], xnT, c + 1)
                    o = slice(c * CK, (c + 1) * CK)
                    act.wait_ge(whole_s, c + 1)
                    act.copy(part[0][:, o], whole[:, o]).then_inc(first, 1)
                    act.wait_ge(rest_s, c + 1)
                    act.copy(part[1][:, o], rest[c % 2][:]).then_inc(second, 1)

            @block.gpsimd
            def _(pool):
                pool.wait_ge(nm.ready, NT)
                pool.wait_ge(w_in, 48)
                pool.tensor_tensor(x[:], x[:], bo[:].unsqueeze(1).broadcast_to([P, NT, D]), ALU.add)\
                    .then_inc(biased, 1)

            @block.vector
            def _(dve):
                norm_vector(dve, nm, x, xn)
                dve.wait_ge(w_in, 48)
                dve.tensor_scalar(sbias[:], bias[:], SCALE, None, ALU.mult).then_inc(scaled, 1)
                dve.wait_ge(scaled, 1)
                for c in range(NC):
                    o = slice(c * CK, (c + 1) * CK)
                    dve.wait_ge(proj, c + 1)
                    dve.tensor_scalar(whole[:, o], banks[c], SCALE, sbias[:], ALU.mult, ALU.add)\
                       .then_inc(whole_s, 1)
                    dve.wait_ge(first, c + 1)
                    dve.tensor_tensor(rest[c % 2][:], whole[:, o], part[0][:, o], ALU.subtract)\
                       .then_inc(rest_s, 1)
                    dve.wait_ge(second, c + 1)
                    dve.tensor_tensor(part[2][:, o], rest[c % 2][:], part[1][:, o], ALU.subtract)\
                       .then_inc(third, 1)


XA = 2 * 2 * TT * CH
NG = B * G


def cross_banks():
    return [(j, qt, c, par) for j in range(2) for qt in range(TT) for c in range(CH) for par in range(2)]


def cross_ring(g, kt, first, last):
    jobs = []
    if kt == 1 and not (last and g == G - 1):
        jobs.append(("maxima", 0))
    if kt == 2 and not (first and g == 0):
        jobs.append(("denominators", 0))
    if kt == 3 and g == 0 and not first:
        jobs += [("output", t) for t in range(TT)]
    if not (last and g >= G - 2):
        jobs += [("scores", a) for a in range(XA * kt // KT, XA * (kt + 1) // KT)]
    return jobs


def cross_uses(first, last):
    return sum(len(cross_ring(g, kt, first, last)) for g in range(G) for kt in range(KT))


def over_batches(eng, batch):
    batch(0, True, False)
    with eng.Fori(1, B - 1) as b:
        batch(b, False, False)
    batch(B - 1, False, True)


def cross_attention_stage(nc, io, scr, ring, S4, U, x, identb, stored, stored_log):
    with ExitStack() as ctx:
        def sb(name, shape, dt=F32):
            return ctx.enter_context(nc.sbuf_tensor("x_" + name, shape, dt))
        kb = [sb(f"k{i}", [P, 2, S2], BF16) for i in range(G)]
        qb = [sb(f"q{i}", [P, 2, T], BF16) for i in range(G)]
        vv = [sb(f"v{i}", [P, KT, 4, VW]) for i in range(G)]
        sel, wo = sb("sel", [P, P]), sb("wo", [P, G, D])
        probs = sb("probs", [P, 4, 2, 2 * T])
        pmax = sb("pmax", [P, 2, 2 * TT, CH])
        nmax, nrest, zero = (sb(n, [P, 2, 2 * TT]) for n in ("nmax", "nrest", "zero"))
        mparts = sb("mparts", [P, 2, MP, 2 * TT], BF16)
        mrows = sb("mrows", [4 * MP * TT, P], BF16)
        ub = [sb(f"u{i}", [P, T]) for i in range(2)]
        rec = [sb(f"rec{i}", [P, T]) for i in range(2)]
        y = sb("y", [P, G, T])
        (w_in, set_up, filled, drained, maxed, scored, exped, valued, evac, normed, msplit) = sems(
            nc, ctx, "x_w_in x_set_up x_ring_filled x_ring_drained x_maxed x_scored x_exped x_valued "
                     "x_evac x_normed x_msplit")
        m_in = sems(nc, ctx, "x_max_in0 x_max_in1 x_max_in2 x_max_in3")
        load_in = sems(nc, ctx, "x_load_in0 x_load_in1 x_load_in2 x_load_in3")
        S = S4.rearrange("p (u c w) -> p u c w", u=2, c=2)
        MC = 2 * TT * MP
        NL = 5
        QTOP = MP + PROWS
        UNITS = G * KT

        PRO = 2 * XA + 1
        U0, UM, UL = cross_uses(True, False), cross_uses(False, False), cross_uses(False, True)
        assert UM % 3 == 0

        def base(b, first):
            return PRO if first else (b - 1) * UM + PRO + U0

        def start_bank(first):
            return PRO if first else PRO + U0

        AFTER = PRO + U0 + (B - 2) * UM + UL

        with nc.Block() as block:

            @block.sync
            def _(sp):
                sp.dma_start(sel[:], io["sel"]).then_inc(w_in, 16)
                sp.dma_start(wo[:], io["xwo"]).then_inc(w_in, 16)
                sp.wait_ge(set_up, 2 * G + 2)
                for i in range(2):
                    sp.wait_ge(stored[i], 16 * (NPROD + 1) * (B // 2 + 1))
                sp.wait_ge(stored_log, 16 * 2 * MP)

                def load(b, g):
                    one = slice(b, b + 1) if isinstance(b, int) else bass.ds(b, 1)
                    toks = slice(b * T, (b + 1) * T) if isinstance(b, int) else bass.ds(b * T, T)
                    for par in range(2):
                        sp.dma_start(kb[g][64 * par:64 * par + KROWS, :, :],
                                     scr["ks"][one, par, :, 2 * g:2 * g + 2, :]
                                     .rearrange("o r j k -> (o r) j k"))\
                          .then_inc(load_in[g], 16)
                        sp.dma_start(qb[g][64 * par + MP:64 * par + QTOP, :, :],
                                     scr["qs"][par, :, 2 * g:2 * g + 2, toks])\
                          .then_inc(load_in[g], 16)
                    sp.dma_start(vv[g][:].rearrange("p t h v -> p (t h v)"),
                                 scr["v"][one, :, g * KT * 4 * VW:(g + 1) * KT * 4 * VW]
                                 .rearrange("o p v -> (o p) v")).then_inc(load_in[g], 16)

                def maxima_rows(use, g):
                    sp.wait_ge(drained, use + 1)
                    for par in range(2):
                        sp.dma_start(qb[g][64 * par + QTOP:64 * par + QTOP + MP, :, :]
                                     .rearrange("p j q -> p (j q)"),
                                     mrows[MC * par:MC * (par + 1), :]).then_inc(m_in[g], 16)

                for g in range(G - 1):
                    load(0, g)
                maxima_rows(XA, 0)
                load(0, G - 1)

                def batch(b, first, last):
                    n = base(b, first)
                    for g in range(G):
                        if not (first and g == 0) and not (last and g > 0):
                            sp.wait_ge(valued, b * UNITS + g * KT)
                            load(b if g == 0 else b + 1, (g - 1) % G)
                        for kt in range(KT):
                            for kind, a in cross_ring(g, kt, first, last):
                                if kind == "maxima":
                                    maxima_rows(n, (g + 1) % G)
                                n = n + 1

                over_batches(sp, batch)

            @block.tensor
            def _(pe):
                pe.wait_ge(w_in, 32)
                pe.wait_ge(set_up, 2 * G + 2)

                def scores_rows(use, r, g, a, wait):
                    j, qt, c, par = cross_banks()[a]
                    if wait:
                        pe.wait_ge(drained, use - 2)
                    rows = slice(64 * par, 64 * par + MP + TOP * DK)
                    pe.matmul(ring[r][:, 0:CW[c]], qb[g][rows, j, qt * P:(qt + 1) * P],
                              kb[g][rows, j, CO[c]:CO[c] + CW[c]], start=True, stop=True)\
                      .then_inc(filled, 1)

                def turn_maxima(use, r, groups):
                    pe.wait_ge(msplit, groups * 4)
                    pe.wait_ge(drained, use - 2)
                    pe.transpose(ring[r][:].bitcast(BF16)[0:2 * MC, 0:P],
                                 mparts[:].rearrange("p c m n -> p (c m n)"), identb[:])\
                      .then_inc(filled, 1)

                def denominators(use, r, g, groups):
                    pe.wait_ge(evac, groups)
                    pe.wait_ge(drained, use - 2)
                    pe.matmul(ring[r][:, 0:T], sel[:], ub[g % 2][:], start=True, stop=True)\
                      .then_inc(filled, 1)

                def output(use, r, groups, t):
                    pe.wait_ge(normed, groups)
                    pe.wait_ge(drained, use - 2)
                    for g in range(G):
                        mm = pe.matmul(ring[r][:, 0:D], y[:, g, t * P:(t + 1) * P],
                                       wo[:, g, :], start=(g == 0), stop=(g == G - 1))
                    mm.then_inc(filled, 1)

                def values(n, g, kt, groups):
                    pe.wait_ge(exped, n + 1)
                    if kt == 0 and groups is not None:
                        pe.wait_ge(evac, groups)
                    m = P if kt < KT - 1 else LAST
                    for par in range(2):
                        for j in range(2):
                            t = 2 * par + j
                            mm = pe.matmul(U[32 * t:32 * t + VW, 0:T], vv[g][0:m, kt, 2 * j + par, :],
                                           probs[0:m, (g * KT + kt) % 4, par, j * T:(j + 1) * T],
                                           start=(kt == 0), stop=(kt == KT - 1), skip_group_check=True)
                    mm.then_inc(valued, 1)

                pe.wait_ge(load_in[0], 16 * NL)
                for a in range(XA):
                    scores_rows(a, a % 3, 0, a, a >= 3)
                turn_maxima(XA, XA % 3, 1)
                pe.wait_ge(load_in[1], 16 * NL)
                for a in range(XA):
                    scores_rows(XA + 1 + a, (XA + 1 + a) % 3, 1, a, True)

                def batch(b, first, last):
                    use, k = base(b, first), 0
                    for g in range(G):
                        pe.wait_ge(m_in[g], (b + 1) * 32)
                        for kt in range(KT):
                            u = g * KT + kt
                            if not (first and u < 2):
                                pe.wait_ge(exped, b * UNITS + u - 1)
                            m = P if kt < KT - 1 else LAST
                            for j in range(2):
                                for par in range(2):
                                    rows = slice(64 * par, 64 * par + QTOP + MP)
                                    mm = pe.matmul(S[0:m, u % 2, par, j * T:(j + 1) * T],
                                                   kb[g][rows, j, kt * P:kt * P + m],
                                                   qb[g][rows, j, :], start=True, stop=True,
                                                   skip_group_check=True)
                            mm.then_inc(scored, 1)
                            for kind, a in cross_ring(g, kt, first, last):
                                r = (start_bank(first) + k) % 3
                                if kind == "scores":
                                    if a == 0:
                                        pe.wait_ge(load_in[(g + 2) % G],
                                                   (b + 1 + (g + 2) // G) * (16 * NL))
                                    scores_rows(use + k, r, (g + 2) % G, a, True)
                                elif kind == "maxima":
                                    turn_maxima(use + k, r, b * G + g + 2)
                                elif kind == "denominators":
                                    denominators(use + k, r, (g - 1) % G, b * G + g)
                                else:
                                    output(use + k, r, b * G, a)
                                k += 1
                            if u > 0:
                                pg, pk = divmod(u - 1, KT)
                                values(b * UNITS + u - 1, pg, pk, None if first and pg == 0 else b * G + pg)
                            elif not first:
                                values(b * UNITS - 1, G - 1, KT - 1, None)

                over_batches(pe, batch)
                values(B * UNITS - 1, G - 1, KT - 1, None)
                denominators(AFTER, AFTER % 3, G - 1, NG)
                for t in range(TT):
                    output(AFTER + 1 + t, (AFTER + 1 + t) % 3, NG, t)

            @block.scalar
            def _(act):
                def evacuate(g, units, groups):
                    act.wait_ge(valued, units)
                    if groups is not None:
                        act.wait_ge(normed, groups)
                    act.copy(ub[g % 2][:], U[:, 0:T]).then_inc(evac, 1)

                def batch(b, first, last):
                    for u in range(UNITS):
                        g, kt = divmod(u, KT)
                        m = P if kt < KT - 1 else LAST
                        act.wait_ge(scored, b * UNITS + u + 1)
                        if not (first and u < 4):
                            act.wait_ge(valued, b * UNITS + u - 3)
                        act.activation(probs[0:m, u % 4, :, :], S[0:m, u % 2, :, :], ACT.Exp)\
                           .then_inc(exped, 1)
                        if kt == 0 and not (first and g == 0):
                            evacuate((g - 1) % G, b * UNITS + u, None if first and g < 3 else b * G + g - 2)

                over_batches(act, batch)
                evacuate(G - 1, B * UNITS, NG - 2)

            @block.gpsimd
            def _(pool):
                for i in range(G):
                    pool.memset(kb[i][:], 1.0).then_inc(set_up, 1)
                    pool.memset(qb[i][:], 1.0).then_inc(set_up, 1)

                def split(groups):
                    pool.wait_ge(maxed, groups + 1)
                    pool.tensor_tensor(mparts[:, :, 0, :], nmax[:], zero[:], ALU.add).then_inc(msplit, 1)
                    pool.wait_ge(msplit, groups * 4 + 1)
                    pool.tensor_tensor(nrest[:], nmax[:], mparts[:, :, 0, :], ALU.subtract)\
                        .then_inc(msplit, 1)
                    pool.wait_ge(msplit, groups * 4 + 2)
                    pool.tensor_tensor(mparts[:, :, 1, :], nrest[:], zero[:], ALU.add).then_inc(msplit, 1)
                    pool.wait_ge(msplit, groups * 4 + 3)
                    pool.tensor_tensor(mparts[:, :, 2, :], nrest[:], mparts[:, :, 1, :], ALU.subtract)\
                        .then_inc(msplit, 1)

                pool.memset(zero[:], 0.0).then_inc(set_up, 1)
                pool.wait_ge(set_up, 2 * G + 2)
                split(0)
                split(1)
                with pool.Fori(2, NG) as group:
                    split(group)

            @block.vector
            def _(dve):
                dve.memset(U[:], 0.0).then_inc(set_up, 1)

                def row_max(use, r, a, groups):
                    j, qt, c, par = cross_banks()[a]
                    if a == 0 and groups is not None:
                        dve.wait_ge(maxed, groups)
                    dve.wait_ge(filled, use + 1)
                    dve.tensor_reduce(pmax[:, par, 2 * j + qt, c:c + 1], ring[r][:, 0:CW[c]], AX.X,
                                      ALU.max).then_inc(drained, 1)
                    if a == XA - 1:
                        dve.wait_ge(drained, use + 1)
                        dve.tensor_reduce(nmax[:], pmax[:], AX.X, ALU.max, negate=True)\
                           .then_inc(maxed, 1)

                def maxima_out(use, r, last_slot, loads):
                    dve.wait_ge(filled, use + 1)
                    if loads is not None:
                        dve.wait_ge(m_in[last_slot], loads * 32)
                    dve.tensor_copy(mrows[:], ring[r][:].bitcast(BF16)[0:2 * MC, 0:P])\
                       .then_inc(drained, 1)

                def normalize(use, r, g):
                    dve.wait_ge(filled, use + 1)
                    dve.reciprocal(rec[g % 2][:], ring[r][:, 0:T]).then_inc(drained, 1)
                    dve.wait_ge(drained, use + 1)
                    dve.tensor_tensor(y[:, g, :], ub[g % 2][:], rec[g % 2][:], ALU.mult).then_inc(normed, 1)

                def residual(use, r, b, t):
                    dve.wait_ge(filled, use + 1)
                    tile = x[:, TT * b + t, :] if isinstance(b, int) else \
                        x[:, bass.ds(b * TT + t, 1), :].rearrange("p o d -> p (o d)")
                    dve.tensor_tensor(tile, ring[r][:, 0:D], tile, ALU.add).then_inc(drained, 1)

                for a in range(XA):
                    row_max(a, a % 3, a, None)
                maxima_out(XA, XA % 3, 0, None)
                for a in range(XA):
                    row_max(XA + 1 + a, (XA + 1 + a) % 3, a, 1)

                def batch(b, first, last):
                    use, k = base(b, first), 0
                    for g in range(G):
                        for kt in range(KT):
                            for kind, a in cross_ring(g, kt, first, last):
                                r = (start_bank(first) + k) % 3
                                if kind == "scores":
                                    row_max(use + k, r, a, b * G + g + 2)
                                elif kind == "maxima":
                                    maxima_out(use + k, r, g, b + 1)
                                elif kind == "denominators":
                                    normalize(use + k, r, (g - 1) % G)
                                else:
                                    residual(use + k, r, b - 1, a)
                                k += 1

                over_batches(dve, batch)
                normalize(AFTER, AFTER % 3, G - 1)
                for t in range(TT):
                    residual(AFTER + 1 + t, (AFTER + 1 + t) % 3, B - 1, t)


FT = F // P
HU = E * FT


def expert_stage(nc, io, scr, banks, x, xn, xnT, ident, out):
    with ExitStack() as ctx:
        def sb(name, shape, dt=F32):
            return ctx.enter_context(nc.sbuf_tensor("e_" + name, shape, dt))
        wr, rank = sb("wr", [D, E]), sb("rank", [P, E])
        wg, wu, wd = sb("wg", [D, E, F]), sb("wu", [D, E, F]), sb("wd", [P, E, FT, D])
        names = "logit p q chosen1 chosen2 score cw"
        r = {n: sb("r_" + n, [P, NT, E]) for n in names.split()}
        s = {n: sb("s_" + n, [P, NT]) for n in "top sum inv first second best den".split()}
        cwT = sb("cwT", [E, N])
        cwb = sb("cwb", [P, E, N])
        xc = [sb(f"xc{i}", [D, CK]) for i in range(2)]
        act_out = [sb(f"silu{i}", [P, CK]) for i in range(2)]
        hid = [sb(f"hid{i}", [P, CK]) for i in range(4)]
        yT = sb("yT", [D, CK])
        res = sb("res", [P, NT, D])
        nm = Norm(nc, ctx, "e_n_")
        (w_in, logits, shifted, exped, step, cw_turned, cw_out, cw_st, scaled, up, silued, hidden,
         downed, summed, y_out, y_turned, added, stored_out) = sems(
            nc, ctx, "e_w_in e_logits e_shifted e_exped e_step e_cw_turned e_cw_out e_cw_st e_scaled "
                     "e_up e_silued e_hidden e_downed e_summed e_y_out e_y_turned e_added e_stored_out")
        cw_in = sems(nc, ctx, " ".join(f"e_cw_in{c}" for c in range(NC)))
        def tiles(a, c):
            return a[:, CT * c:CT * (c + 1), :] if isinstance(c, int) else a[:, bass.ds(c * CT, CT), :]

        gate, upb = banks[0:2], banks[2:4]
        yb, tb = banks[4], banks[5]

        with nc.Block() as block:

            @block.sync
            def _(sp):
                for dst, src in ((wr, io["wr"]), (rank, io["rank"]), (wg, io["wg"]), (wu, io["wu"]),
                                 (wd, io["wd"])):
                    sp.dma_start(dst[:], src).then_inc(w_in, 16)
                for c in range(NC):
                    o = slice(c * CK, (c + 1) * CK)
                    sp.wait_ge(cw_out, c + 1)
                    sp.dma_start(scr["cw"][:, o], cwT[:, o]).then_inc(cw_st, 16)
                    sp.wait_ge(cw_st, 16 * (c + 1))
                    sp.dma_start(cwb[:, :, o], scr["cw"][:, o].partition_broadcast(P))\
                      .then_inc(cw_in[c], 16)

                def store(c):
                    sp.wait_ge(added, c + 1)
                    dst = out[c * CK:(c + 1) * CK, :] if isinstance(c, int) else out[bass.ds(c * CK, CK), :]
                    sp.dma_start(dst.rearrange("(t p) d -> p t d", p=P), tiles(res, c))\
                      .then_inc(stored_out, 16)

                with sp.Fori(0, NC) as c:
                    store(c)
                sp.wait_ge(stored_out, 16 * NC)

            @block.tensor
            def _(pe):
                for c in range(NC):
                    norm_tensor(pe, nm, xn, ident, banks[5:7], c)
                    pe.wait_ge(nm.out, c + 1)
                    if c == 0:
                        pe.wait_ge(w_in, 16 * 5)
                    for t in range(CT * c, CT * (c + 1)):
                        mm = pe.matmul(banks[0][:, t * E:(t + 1) * E], xnT[:, t * P:(t + 1) * P], wr[:],
                                       start=True, stop=True, skip_group_check=True)
                mm.then_inc(logits, 1)
                pe.wait_ge(step, RSTEPS)
                for c in range(NC):
                    for t in range(CT):
                        mm = pe.transpose(banks[1 + c][0:E, t * P:(t + 1) * P],
                                          r["cw"][:, CT * c + t, :], ident[:])
                    mm.then_inc(cw_turned, 1)
                pe.wait_ge(cw_out, NC)

                def hidden_units(c, k, first):
                    e, f = divmod(k, FT)
                    o = slice(c * CK, (c + 1) * CK) if isinstance(c, int) else bass.ds(c * CK, CK)
                    if not (first and k < 2):
                        pe.wait_ge(hidden, c * HU + k - 1)
                    pe.matmul(gate[k % 2], wg[:, e, f * P:(f + 1) * P], xnT[:, o], start=True, stop=True)\
                      .then_inc(up, 1)
                    pe.wait_ge(scaled, c * E + e + 1)
                    pe.matmul(upb[k % 2], wu[:, e, f * P:(f + 1) * P], xc[e % 2][:], start=True, stop=True)\
                      .then_inc(up, 1)

                def down(c, k, first):
                    e, f = divmod(k, FT)
                    pe.wait_ge(hidden, c * HU + k + 1)
                    if k == 0 and not first:
                        pe.wait_ge(y_out, c)
                    mm = pe.matmul(yb, wd[:, e, f, :], hid[k % 4][:], start=(k == 0), stop=(k == HU - 1))
                    mm.then_inc(downed, 1)

                def turn_back(c):
                    pe.wait_ge(y_out, c + 1)
                    for t in range(CT):
                        mm = pe.transpose(tb[:, t * D:(t + 1) * D], yT[:, t * P:(t + 1) * P], ident[:])
                    mm.then_inc(y_turned, 1)

                def piece(c, first):
                    for k in range(HU):
                        hidden_units(c, k, first)
                        if k == 3 and not first:
                            turn_back(c - 1)
                        if k >= 2:
                            down(c, k - 2, first)
                    down(c, HU - 2, first)
                    down(c, HU - 1, first)

                piece(0, True)
                with pe.Fori(1, NC) as c:
                    piece(c, False)
                turn_back(NC - 1)

            @block.scalar
            def _(act):
                norm_scalar_root(act, nm)
                for c in range(NC):
                    norm_scalar_out(act, nm, banks[5:7], xnT, c)
                act.wait_ge(shifted, 1)
                act.activation(r["p"][:], r["p"][:], ACT.Exp).then_inc(exped, 1)
                for c in range(NC):
                    act.wait_ge(cw_turned, c + 1)
                    act.copy(cwT[:, c * CK:(c + 1) * CK], banks[1 + c][0:E, :]).then_inc(cw_out, 1)

                def piece(c, first):
                    for k in range(HU):
                        if k == 2 and not first:
                            y_evacuate(c - 1)
                        act.wait_ge(up, 2 * (c * HU + k) + 1)
                        if not (first and k < 2):
                            act.wait_ge(hidden, c * HU + k - 1)
                        act.activation(act_out[k % 2][:], gate[k % 2], ACT.Silu).then_inc(silued, 1)

                def y_evacuate(c):
                    act.wait_ge(downed, (c + 1) * HU)
                    act.copy(yT[:], yb).then_inc(y_out, 1)

                piece(0, True)
                with act.Fori(1, NC) as c:
                    piece(c, False)
                y_evacuate(NC - 1)

            @block.gpsimd
            def _(pool):
                def piece(c, first):
                    for e in range(E):
                        if not (first and e < 2):
                            pool.wait_ge(up, 2 * FT * (c * E + e - 1))
                        o = slice(c * CK, (c + 1) * CK)
                        pool.tensor_tensor(xc[e % 2][:], xnT[:, o], cwb[:, e, o], ALU.mult)\
                            .then_inc(scaled, 1)

                for c in range(NC):
                    pool.wait_ge(cw_in[c], 16)
                    piece(c, c == 0)

            @block.vector
            def _(dve):
                norm_vector(dve, nm, x, xn)
                dve.wait_ge(w_in, 16 * 5)
                dve.wait_ge(logits, 1)
                n = [0]

                def then(ins):
                    n[0] += 1
                    ins.then_inc(step, 1)
                    dve.wait_ge(step, n[0])

                def wide(a):
                    return a[:].unsqueeze(2).broadcast_to([P, NT, E])

                ranks = rank[:].unsqueeze(1).broadcast_to([P, NT, E])
                then(dve.tensor_copy(r["logit"][:], banks[0][:, 0:NT * E].rearrange("p (t e) -> p t e", e=E)))
                then(dve.tensor_reduce(s["top"][:], r["logit"][:], AX.X, ALU.max))
                dve.tensor_tensor(r["p"][:], r["logit"][:], wide(s["top"]), ALU.subtract).then_inc(shifted, 1)
                dve.wait_ge(exped, 1)
                then(dve.tensor_reduce(s["sum"][:], r["p"][:], AX.X, ALU.add))
                then(dve.reciprocal(s["inv"][:], s["sum"][:]))
                then(dve.tensor_tensor(r["p"][:], r["p"][:], wide(s["inv"]), ALU.mult))
                left = "p"
                for top, chosen in (("first", "chosen1"), ("second", "chosen2")):
                    then(dve.tensor_reduce(s[top][:], r[left][:], AX.X, ALU.max))
                    then(dve.tensor_tensor(r["score"][:], r[left][:], wide(s[top]), ALU.is_equal))
                    then(dve.tensor_tensor(r["score"][:], r["score"][:], ranks, ALU.mult))
                    then(dve.tensor_reduce(s["best"][:], r["score"][:], AX.X, ALU.max))
                    then(dve.tensor_tensor(r[chosen][:], r["score"][:], wide(s["best"]), ALU.is_equal))
                    if left == "p":
                        then(dve.scalar_tensor_tensor(out=r["q"][:], in0=r[chosen][:], scalar=-2.0,
                                                      in1=r["p"][:], op0=ALU.mult, op1=ALU.add))
                        left = "q"
                then(dve.tensor_tensor(r["score"][:], r["chosen1"][:], r["chosen2"][:], ALU.add))
                then(dve.tensor_tensor(r["score"][:], r["score"][:], r["p"][:], ALU.mult))
                then(dve.tensor_tensor(s["den"][:], s["first"][:], s["second"][:], ALU.add))
                then(dve.tensor_scalar(s["den"][:], s["den"][:], 1e-20, None, ALU.add))
                then(dve.reciprocal(s["inv"][:], s["den"][:]))
                then(dve.tensor_tensor(r["cw"][:], r["score"][:], wide(s["inv"]), ALU.mult))
                assert n[0] == RSTEPS

                def piece(c, first):
                    for k in range(HU):
                        if k == 4 and not first:
                            add_back(c - 1)
                        dve.wait_ge(silued, c * HU + k + 1)
                        dve.wait_ge(up, 2 * (c * HU + k) + 2)
                        if not (first and k < 4):
                            dve.wait_ge(downed, c * HU + k - 3)
                        dve.tensor_tensor(hid[k % 4][:], upb[k % 2], act_out[k % 2][:], ALU.mult)\
                           .then_inc(hidden, 1)

                def add_back(c):
                    dve.wait_ge(y_turned, c + 1)
                    dve.tensor_tensor(tiles(res, c), tb.rearrange("p (t d) -> p t d", d=D),
                                      tiles(x, c), ALU.add).then_inc(added, 1)

                piece(0, True)
                with dve.Fori(1, NC) as c:
                    piece(c, False)
                add_back(NC - 1)


RSTEPS = 22


def decoder_layer(nc, io, out):
    with ExitStack() as ctx:
        def sb(name, shape, dt=F32):
            return ctx.enter_context(nc.sbuf_tensor(name, shape, dt))

        def scratch(name, shape, dt):
            return nc.dram_tensor(name, shape, dt, kind="Internal").ap()
        scr = {
            "ks": scratch("scr_ks", [B, 2, KROWS, GJ, S2], BF16),
            "qs": scratch("scr_qs", [2, PROWS, GJ, N], BF16),
            "v": scratch("scr_v", [B, P, G * KT * 4 * VW], F32),
            "ks_self": scratch("scr_ks_self", [2, PROWS, GJ, N], BF16),
            "qs_self": scratch("scr_qs_self", [2, PROWS, GJ, N], BF16),
            "cw": scratch("scr_cw", [E, N], F32),
        }
        x, xn, xnT = sb("x", [P, NT, D]), sb("xn", [P, NT, D]), sb("xnT", [D, N])
        ident, identb = sb("ident", [P, P]), sb("identb", [P, P], BF16)
        v_all = sb("v_all", [P, NT, H, VW])
        S4 = ctx.enter_context(nc.psum_tensor("S4", [P, 4 * 512], F32))
        ring = [ctx.enter_context(nc.psum_tensor(f"ring{i}", [P, 512], F32)) for i in range(3)]
        U = ctx.enter_context(nc.psum_tensor("U", [P, 512], F32))
        banks = [S4[:, 512 * i:512 * (i + 1)] for i in range(4)] + [r[:] for r in ring] + [U[:]]
        cst_in, stored0, stored1, stored_log, stored_self, stored_q = sems(
            nc, ctx, "cst_in stored_context0 stored_context1 stored_log stored_self stored_q")
        with ExitStack() as held:
            kp = [[held.enter_context(nc.sbuf_tensor(f"kpart{i}_{j}", [D, S2], BF16)) for j in range(3)]
                  for i in range(2)]
            vb = [held.enter_context(nc.sbuf_tensor(f"vbuf{i}", [P, G, KT, 4 * VW], F32))
                  for i in range(2)]
            lp = [held.enter_context(nc.sbuf_tensor(f"logpart{j}", [B, S2], BF16)) for j in range(MP)]
            context_stage(nc, io, scr, banks, kp, vb, lp, [stored0, stored1], stored_log)
            self_projection_stage(nc, io, scr, banks, x, xn, xnT, v_all, ident, identb, cst_in,
                                  stored_self)
            self_attention_stage(nc, io, scr, ring, S4[:], U, x, v_all, identb)
            query_stage(nc, io, scr, banks, x, xn, xnT, ident, stored_q)
            cross_attention_stage(nc, io, scr, ring, S4[:], U, x, identb, [stored0, stored1],
                                  stored_log)
        expert_stage(nc, io, scr, banks, x, xn, xnT, ident, out)


def _layouts(a):
    c = np.ascontiguousarray
    perm = np.array([(4 * g + 2 * j + par) * DK + d
                     for par in range(2) for d in range(DK) for g in range(G) for j in range(2)])
    swap = np.array([(e // DK) * DK + (e % DK + DK // 2) % DK for e in perm])
    spaced = np.array([[(32 * (2 * par + j) + d, (4 * g + 2 * j + par) * DK + d)
                        for par in range(2) for j in range(2) for d in range(DK)] for g in range(G)])

    def spread(w):
        o = np.zeros((P, G, D), w.dtype)
        for g in range(G):
            o[spaced[g, :, 0], g] = w[spaced[g, :, 1]]
        return o

    def row(b):
        return np.broadcast_to(b, (P, D))

    half = DK // 2
    freq = (1.0 / 10000.0 ** (2.0 * np.arange(half, dtype=np.float32) / DK)).astype(np.float32)
    ang = np.arange(T, dtype=np.float32)[:, None] * freq[None, :]
    d = perm % DK
    cos = np.cos(ang)[:, d % half].T.astype(np.float32)
    sin = (np.sin(ang)[:, d % half] * np.where(d < half, -1, 1)).T.astype(np.float32)
    hidden = np.where(np.arange(P)[None, :] > np.arange(P)[:, None], MASKED, 0).astype(np.float32)
    sel = np.zeros((P, P), np.float32)
    for t in range(4):
        sel[32 * t + DK, 32 * t:32 * t + 32] = 1
    scale = np.float32(SCALE)
    return {
        "x": a["x"].reshape(N, D),
        "ctxT": c(a["ctx_1024"].transpose(2, 0, 1).reshape(D, B * S2)),
        "weights": a["fside_BxS2_0"],
        "w_q": c(a["L0_attn_WQ_w"].T[:, perm]), "w_q_swap": c(a["L0_attn_WQ_w"].T[:, swap]),
        "w_k": c(a["L0_attn_WK_w"].T[:, perm]), "w_k_swap": c(a["L0_attn_WK_w"].T[:, swap]),
        "b_q": a["L0_attn_WQ_b"][perm, None], "b_q_swap": a["L0_attn_WQ_b"][swap, None],
        "b_k": a["L0_attn_WK_b"][perm, None], "b_k_swap": a["L0_attn_WK_b"][swap, None],
        "rot_q": cos * scale, "rot_q_swap": sin * scale, "rot_k": cos, "rot_k_swap": sin,
        "swv": c(a["L0_attn_WV_w"].T), "sbv": row(a["L0_attn_WV_b"]),
        "swo": spread(a["L0_attn_Wo_w"].T), "sbo": row(a["L0_attn_Wo_b"]),
        "xwq": c(a["L0_xattn_wq"][:, perm]), "xbq": a["L0_xattn_bq"][perm, None],
        "xwk": c(a["L0_xattn_wk"][:, perm]), "xbk": a["L0_xattn_bk"][perm, None],
        "xwv": a["L0_xattn_wv"], "xbv": row(a["L0_xattn_bv"]),
        "xwo": spread(a["L0_xattn_wo"]), "xbo": row(a["L0_xattn_bo"]),
        "wr": c(a["L0_ffn_gate_w"].T),
        "wg": c(a["L0_ffn_w_gate"].transpose(1, 0, 2)), "wu": c(a["L0_ffn_w_up"].transpose(1, 0, 2)),
        "wd": c(a["L0_ffn_w_down"].reshape(E, FT, P, D).transpose(2, 0, 1, 3)),
        "ident": np.eye(P, dtype=np.float32), "sel": sel,
        "masks": np.stack([hidden, hidden.T], 1),
        "rank": np.broadcast_to(np.arange(E, 0, -1).astype(np.float32), (P, E)),
    }


def kernel(**inputs):
    import concourse.bacc as bacc
    from concourse.bass_utils import run_bass_kernel_spmd

    nc = bacc.Bacc("TRN2", target_bir_lowering=False, num_devices=1)
    arrays, io = {}, {}
    for name, a in _layouts({k: np.asarray(v) for k, v in inputs.items()}).items():
        a = np.ascontiguousarray(a)
        arrays[f"in_{name}"] = a
        io[name] = nc.dram_tensor(f"in_{name}", a.shape, mybir.dt.from_np(a.dtype),
                                  kind="ExternalInput").ap()
    out = nc.dram_tensor("out", [N, D], F32, kind="ExternalOutput").ap()
    decoder_layer(nc, io, out)
    r = run_bass_kernel_spmd(nc, [arrays], core_ids=[0])
    return r.results[0]["out"].reshape(B, T, D)
```

```python
from contextlib import ExitStack

import numpy as np

import concourse.bass as bass
from concourse import mybir

F32 = mybir.dt.float32
BF16 = mybir.dt.bfloat16
ALU = mybir.AluOpType
ACT = mybir.ActivationFunctionType
AX = mybir.AxisListType

B, T, D, H = 8, 256, 128, 16
DK = D // H
S2 = 1601
E, F = 8, 256
N = B * T
P = 128
NT = N // P
TT = T // P
EPS = 1e-5
SCALE = DK ** -0.5
MASKED = -1e30

G = 4
GJ = 2 * G
KT = -(-S2 // P)
LAST = S2 - (KT - 1) * P
CH = 4
CW = [S2 // CH + (i < S2 % CH) for i in range(CH)]
CO = [sum(CW[:i]) for i in range(CH)]
VW = DK + 1

K_PART = [1, 2, 1, 2, 1, 3]
Q_PART = [1, 1, 2, 2, 3, 1]
NPROD = len(K_PART)
PROWS = NPROD * DK
MP = 3
KROWS = MP + PROWS

LOG_SHIFT = 20

CK = 512
NC = N // CK
CT = CK // P


def sems(nc, ctx, names):
    return [ctx.enter_context(nc.semaphore(n)) for n in names.split()]


def context_stage(nc, io, scr, banks, kp, vb, lp, stored, stored_log):
    NST = NPROD + 1
    with ExitStack() as ctx:
        def sb(name, shape, dt=F32):
            return ctx.enter_context(nc.sbuf_tensor("c_" + name, shape, dt))
        wk, wv, bk, bv = sb("wk", [D, D]), sb("wv", [D, D]), sb("bk", [D, 1]), sb("bv", [P, D])
        cx = [sb(f"ctx{i}", [D, S2]) for i in range(2)]
        rest = [sb(f"rest{i}", [D, S2]) for i in range(2)]
        fw, lw, lrest = sb("fw", [B, S2]), sb("lw", [B, S2]), sb("lrest", [B, S2])
        lbias = sb("lbias", [B, 1])
        (w_in, fw_in, proj, k_first, k_rest, k_second, k_third, v_done, ones_set, log_steps) = sems(
            nc, ctx, "c_w_in c_fw_in c_proj c_k_first c_k_rest c_k_second c_k_third c_v_done "
                     "c_ones_set c_log_steps")
        ctx_in = sems(nc, ctx, "c_ctx_in0 c_ctx_in1")
        PB = 2 * CH
        with nc.Block() as block:

            @block.sync
            def _(sp):
                for dst, src in ((wk, io["xwk"]), (bk, io["xbk"]), (wv, io["xwv"]), (bv, io["xbv"])):
                    sp.dma_start(dst[:], src).then_inc(w_in, 16)
                for i in range(2):
                    sp.dma_start(cx[i][:], io["ctxT"][:, i * S2:(i + 1) * S2]).then_inc(ctx_in[i], 16)
                    sp.sem_inc(stored[i], 16 * NST)
                sp.dma_start(fw[:], io["weights"]).then_inc(fw_in, 16)

                def store(b, i):
                    sp.wait_ge(k_third, b + 1)
                    for r in range(NPROD):
                        one = slice(b, b + 1) if isinstance(b, int) else bass.ds(b, 1)
                        sp.dma_start(scr["ks"][one, :, MP + DK * r:MP + DK * (r + 1), :, :]
                                     .rearrange("o c r n k -> (o c) (r n) k"),
                                     kp[i][K_PART[r] - 1][:]).then_inc(stored[i], 16)
                    sp.wait_ge(v_done, CH * (b + 1))
                    sp.dma_start(scr["v"][one].rearrange("o p v -> (o p) v"),
                                 vb[i][:].rearrange("p g t v -> p (g t v)"))\
                      .then_inc(stored[i], 16)

                with sp.Fori(0, B // 2 - 1) as it:
                    for i in range(2):
                        b = it * 2 + i
                        sp.wait_ge(proj, PB * (b + 1))
                        sp.dma_start(cx[i][:], io["ctxT"][:, bass.ds((b + 2) * S2, S2)])\
                          .then_inc(ctx_in[i], 16)
                        store(b, i)
                for i in range(2):
                    store(B - 2 + i, i)
                sp.wait_ge(log_steps, 7)
                for j in range(MP):
                    for par in range(2):
                        sp.dma_start(scr["ks"][:, par, j, :, :],
                                     lp[j][:].unsqueeze(1).broadcast_to([B, GJ, S2]))\
                          .then_inc(stored_log, 16)

            @block.tensor
            def _(pe):
                pe.wait_ge(w_in, 64)

                def batch(b, i, it, first):
                    pe.wait_ge(ctx_in[i], it * 16 + 16)
                    for c in range(CH):
                        if not first:
                            pe.wait_ge(k_rest, CH * (b - 1) + c + 1)
                        pe.matmul(banks[c][:, 0:CW[c]], wk[:], cx[i][:, CO[c]:CO[c] + CW[c]],
                                  start=True, stop=True).then_inc(proj, 1)
                    for c in range(CH):
                        if not first:
                            pe.wait_ge(v_done, CH * (b - 1) + c + 1)
                        for n, t in enumerate(range(CT * c, min(CT * (c + 1), KT))):
                            m = P if t < KT - 1 else LAST
                            mm = pe.matmul(banks[CH + c][0:m, n * D:(n + 1) * D],
                                           cx[i][:, t * P:t * P + m], wv[:], start=True, stop=True)
                        mm.then_inc(proj, 1)

                batch(0, 0, 0, True)
                batch(1, 1, 0, False)
                with pe.Fori(1, B // 2) as it:
                    for i in range(2):
                        batch(it * 2 + i, i, it, False)

            @block.scalar
            def _(act):
                act.wait_ge(w_in, 64)
                act.wait_ge(fw_in, 16)
                act.wait_ge(ones_set, 1)
                act.activation(lw[:], fw[:], ACT.Ln, bias=lbias[:], scale=float(2 ** LOG_SHIFT))\
                   .then_inc(log_steps, 1)

                def batch(b, i, it):
                    act.wait_ge(stored[i], 16 * NST * (it + 1))
                    for c in range(CH):
                        act.wait_ge(proj, PB * b + c + 1)
                        act.activation(kp[i][0][:, CO[c]:CO[c] + CW[c]], banks[c][:, 0:CW[c]],
                                       ACT.Identity, bias=bk[:]).then_inc(k_first, 1)
                    act.wait_ge(k_rest, CH * (b + 1))
                    act.copy(kp[i][1][:], rest[i][:]).then_inc(k_second, 1)

                with act.Fori(0, B // 2) as it:
                    for i in range(2):
                        batch(it * 2 + i, i, it)

            @block.vector
            def _(dve):
                dve.memset(lbias[:], 1e-20 * 2 ** LOG_SHIFT).then_inc(ones_set, 1)
                for i in range(2):
                    dve.memset(vb[i][:], 1.0).then_inc(ones_set, 1)
                dve.wait_ge(ones_set, 3)
                dve.wait_ge(log_steps, 1)
                dve.tensor_scalar(lw[:], lw[:], -LOG_SHIFT * float(np.log(2.0)), None, ALU.add)\
                   .then_inc(log_steps, 1)
                dve.wait_ge(log_steps, 2)
                dve.tensor_copy(lp[0][:], lw[:]).then_inc(log_steps, 1)
                dve.wait_ge(log_steps, 3)
                dve.tensor_tensor(lrest[:], lw[:], lp[0][:], ALU.subtract).then_inc(log_steps, 1)
                dve.wait_ge(log_steps, 4)
                dve.tensor_copy(lp[1][:], lrest[:]).then_inc(log_steps, 1)
                dve.wait_ge(log_steps, 5)
                dve.tensor_tensor(lrest[:], lrest[:], lp[1][:], ALU.subtract).then_inc(log_steps, 1)
                dve.wait_ge(log_steps, 6)
                dve.tensor_copy(lp[2][:], lrest[:]).then_inc(log_steps, 1)

                def batch(b, i, it):
                    for c in range(CH):
                        dve.wait_ge(k_first, CH * b + c + 1)
                        o = slice(CO[c], CO[c] + CW[c])
                        dve.scalar_tensor_tensor(out=rest[i][:, o], in0=banks[c][:, 0:CW[c]],
                                                 scalar=bk[:], in1=kp[i][0][:, o], op0=ALU.add,
                                                 op1=ALU.subtract).then_inc(k_rest, 1)
                    dve.wait_ge(stored[i], 16 * NST * (it + 1))
                    for c in range(CH):
                        dve.wait_ge(proj, PB * b + CH + c + 1)
                        nt = min(CT, KT - CT * c)
                        m = P if c < CH - 1 else LAST
                        for g in range(G):
                            ins = dve.tensor_tensor(
                                vb[i][0:m, g, CT * c:CT * c + nt, :]
                                .rearrange("p t (h v) -> p t h v", h=4)[:, :, :, 0:DK],
                                banks[CH + c][0:m, 0:nt * D]
                                .rearrange("p (t e) -> p t e", e=D)[:, :, 32 * g:32 * g + 32]
                                .rearrange("p t (h d) -> p t h d", h=4),
                                bv[0:m, 32 * g:32 * g + 32].rearrange("p (h d) -> p h d", h=4)
                                .unsqueeze(1).broadcast_to([m, nt, 4, DK]), ALU.add)
                        ins.then_inc(v_done, 1)
                    dve.wait_ge(k_second, b + 1)
                    dve.tensor_tensor(kp[i][2][:], rest[i][:], kp[i][1][:], ALU.subtract)\
                       .then_inc(k_third, 1)

                dve.wait_ge(w_in, 64)
                with dve.Fori(0, B // 2) as it:
                    for i in range(2):
                        batch(it * 2 + i, i, it)


class Norm:

    def __init__(self, nc, ctx, tag):
        self.st = ctx.enter_context(nc.sbuf_tensor(tag + "stats", [P, NT, 6], F32))
        self.mv = ctx.enter_context(nc.sbuf_tensor(tag + "meanvar", [P, NT, 2], F32))
        self.rs = ctx.enter_context(nc.sbuf_tensor(tag + "rstd", [P, NT, 2], F32))
        self.eps = ctx.enter_context(nc.sbuf_tensor(tag + "eps", [P, 1], F32))
        self.stats, self.rooted, self.ready, self.turned, self.out = sems(
            nc, ctx, " ".join(tag + n for n in "stats_s rooted_s ready_s turned_s out_s".split()))


def norm_vector(dve, nm, x, xn):
    dve.memset(nm.eps[:], EPS).then_inc(nm.stats, 1)
    for t in range(NT):
        dve.bn_stats(nm.st[:, t, :], x[:, t, :]).then_inc(nm.stats, 1)
    for t in range(NT):
        dve.wait_ge(nm.stats, 2 + t)
        dve.bn_aggr(nm.mv[:, t, :], nm.st[:, t, :]).then_inc(nm.stats, 1)
    dve.wait_ge(nm.rooted, 1)
    dve.reciprocal(nm.rs[:, :, 1], nm.rs[:, :, 0]).then_inc(nm.rooted, 1)
    dve.wait_ge(nm.rooted, 2)
    for t in range(NT):
        dve.tensor_scalar(xn[:, t, :], x[:, t, :], nm.mv[:, t, 0:1], nm.rs[:, t, 1:2],
                          ALU.subtract, ALU.mult).then_inc(nm.ready, 1)


def norm_scalar_root(act, nm):
    act.wait_ge(nm.stats, 1 + 2 * NT)
    act.activation(nm.rs[:, :, 0], nm.mv[:, :, 1], ACT.Sqrt, bias=nm.eps[:]).then_inc(nm.rooted, 1)


def norm_scalar_out(act, nm, bank2, xnT, c):
    act.wait_ge(nm.turned, c + 1)
    act.copy(xnT[:, c * CK:(c + 1) * CK], bank2[c % 2]).then_inc(nm.out, 1)


def norm_tensor(pe, nm, xn, ident, bank2, c):
    pe.wait_ge(nm.ready, CT * (c + 1))
    if c >= 2:
        pe.wait_ge(nm.out, c - 1)
    for t in range(CT):
        mm = pe.transpose(bank2[c % 2][:, t * P:(t + 1) * P], xn[:, CT * c + t, :], ident[:])
    mm.then_inc(nm.turned, 1)


def self_projection_stage(nc, io, scr, banks, x, xn, xnT, v_all, ident, identb, cst_in, stored_self):
    with ExitStack() as ctx:
        def sb(name, shape, dt=F32):
            return ctx.enter_context(nc.sbuf_tensor("p_" + name, shape, dt))
        names = ["q", "q_swap", "k", "k_swap"]
        w = {n: sb("w" + n, [D, D]) for n in names}
        bias = {n: sb("b" + n, [D, 1]) for n in names}
        wv, bv, bo = sb("wv", [D, D]), sb("bv", [P, D]), sb("bo", [P, D])
        rot = {n: sb("rot" + n, [D, T]) for n in names}
        turned = [[sb(f"t{n}{i}", [D, CK]) for i in range(2)] for n in "qk"]
        part = [[sb(f"part{n}{j}", [D, N], BF16) for j in range(3)] for n in "qk"]
        rest = [sb(f"rest{n}", [D, CK]) for n in "qk"]
        nm = Norm(nc, ctx, "p_n_")
        (w_in, x_in, proj, drained, tmp, whole, first, rest_s, second, third, biased) = sems(
            nc, ctx, "p_w_in p_x_in p_proj p_drained p_tmp p_whole p_first p_rest p_second p_third "
                     "p_biased")
        NW = 4 * 3 + 2
        PC = 5
        with nc.Block() as block:

            @block.sync
            def _(sp):
                sp.dma_start(x[:], io["x"].rearrange("(t p) d -> p t d", p=P)).then_inc(x_in, 16)
                sp.dma_start(bo[:], io["sbo"]).then_inc(x_in, 16)
                sp.dma_start(ident[:], io["ident"]).then_inc(cst_in, 16)
                for n in names:
                    sp.dma_start(w[n][:], io["w_" + n]).then_inc(w_in, 16)
                    sp.dma_start(bias[n][:], io["b_" + n]).then_inc(w_in, 16)
                    sp.dma_start(rot[n][:], io["rot_" + n]).then_inc(w_in, 16)
                sp.dma_start(wv[:], io["swv"]).then_inc(w_in, 16)
                sp.dma_start(bv[:], io["sbv"]).then_inc(w_in, 16)
                for half in range(2):
                    sp.wait_ge(third, 2 * 2 * (half + 1))
                    b0, nb = half * B // 2, B // 2
                    for which, dst, parts in ((0, "qs_self", Q_PART), (1, "ks_self", K_PART)):
                        for r in range(NPROD):
                            src = part[which][parts[r] - 1]
                            sp.dma_start(
                                scr[dst][:, DK * r:DK * (r + 1), :, b0 * T:(b0 + nb) * T]
                                .rearrange("c r n t -> c (r n) t"),
                                src[:, b0 * T:(b0 + nb) * T]).then_inc(stored_self, 16)
                sp.wait_ge(stored_self, 16 * 2 * 2 * NPROD)

            @block.tensor
            def _(pe):
                pe.wait_ge(cst_in, 16)
                for c in range(NC):
                    norm_tensor(pe, nm, xn, ident, banks[5:7], c)
                    if c == 0:
                        pe.wait_ge(w_in, 16 * NW)
                    pe.wait_ge(nm.out, c + 1)
                    for i, n in enumerate(names):
                        if c:
                            pe.wait_ge(drained, PC * (c - 1) + i + 1)
                        pe.matmul(banks[i], w[n][:], xnT[:, c * CK:(c + 1) * CK],
                                  start=True, stop=True).then_inc(proj, 1)
                    if c:
                        pe.wait_ge(drained, PC * c)
                    for t in range(CT):
                        mm = pe.matmul(banks[4][:, t * D:(t + 1) * D],
                                       xnT[:, c * CK + t * P:c * CK + (t + 1) * P], wv[:],
                                       start=True, stop=True)
                    mm.then_inc(proj, 1)

            @block.scalar
            def _(act):
                norm_scalar_root(act, nm)
                norm_scalar_out(act, nm, banks[5:7], xnT, 0)
                for c in range(NC):
                    if c + 1 < NC:
                        norm_scalar_out(act, nm, banks[5:7], xnT, c + 1)
                    o = slice(c * CK, (c + 1) * CK)
                    for i in range(2):
                        act.wait_ge(whole, 2 * c + i + 1)
                        act.copy(part[i][0][:, o], turned[i][0][:]).then_inc(first, 1)
                    for i in range(2):
                        act.wait_ge(rest_s, 2 * c + i + 1)
                        act.copy(part[i][1][:, o], rest[i][:]).then_inc(second, 1)

            @block.gpsimd
            def _(pool):
                pool.memset(v_all[:], 1.0).then_inc(biased, 1)
                pool.wait_ge(nm.ready, NT)
                pool.wait_ge(x_in, 32)
                pool.tensor_tensor(x[:], x[:], bo[:].unsqueeze(1).broadcast_to([P, NT, D]), ALU.add)\
                    .then_inc(biased, 1)

            @block.vector
            def _(dve):
                dve.wait_ge(x_in, 32)
                norm_vector(dve, nm, x, xn)
                dve.wait_ge(cst_in, 16)
                dve.tensor_copy(identb[:], ident[:])
                dve.wait_ge(w_in, 16 * NW)
                dve.wait_ge(biased, 1)
                steps = 0
                for c in range(NC):
                    o = slice(c * CK, (c + 1) * CK)
                    for i in range(2):
                        if c:
                            dve.wait_ge(first, 2 * (c - 1) + i + 1)
                        for s in range(2):
                            n = names[2 * i + s]
                            dve.wait_ge(proj, PC * c + 2 * i + s + 1)
                            dve.scalar_tensor_tensor(
                                out=turned[i][s][:].rearrange("p (b t) -> p b t", t=T),
                                in0=banks[2 * i + s].rearrange("p (b t) -> p b t", t=T),
                                scalar=bias[n][:],
                                in1=rot[n][:].unsqueeze(1).broadcast_to([P, CK // T, T]),
                                op0=ALU.add, op1=ALU.mult).then_inc(drained, 1)
                        dve.wait_ge(drained, PC * c + 2 * i + 2)
                        dve.tensor_tensor(turned[i][0][:], turned[i][0][:], turned[i][1][:], ALU.add)\
                           .then_inc(whole, 1)
                    dve.wait_ge(proj, PC * c + 5)
                    dve.tensor_tensor(
                        v_all[:, CT * c:CT * (c + 1), :, 0:DK],
                        banks[4].rearrange("p (t h d) -> p t h d", t=CT, h=H),
                        bv[:].rearrange("p (h d) -> p h d", h=H).unsqueeze(1)
                        .broadcast_to([P, CT, H, DK]), ALU.add).then_inc(drained, 1)
                    for i in range(2):
                        dve.wait_ge(first, 2 * c + i + 1)
                        dve.tensor_tensor(rest[i][:], turned[i][0][:], part[i][0][:, o], ALU.subtract)\
                           .then_inc(rest_s, 1)
                    for i in range(2):
                        dve.wait_ge(second, 2 * c + i + 1)
                        dve.tensor_tensor(part[i][2][:, o], rest[i][:], part[i][1][:, o], ALU.subtract)\
                           .then_inc(third, 1)


def tensor_sums(pe, filled, evac, drained, use, bank, u, groups, ident):
    pe.wait_ge(evac, groups)
    pe.wait_ge(drained, use - 2)
    for t in range(TT):
        mm = pe.transpose(bank[:, t * P:(t + 1) * P], u[:, t * P:(t + 1) * P], ident[:])
    mm.then_inc(filled, 1)


def tensor_turn(pe, filled, drained, use, last_sums, tiles, bank, y, ident):
    pe.wait_ge(drained, last_sums + 1)
    pe.wait_ge(drained, use - 2)
    for n, t in enumerate(tiles):
        mm = pe.transpose(bank[:, n * P:(n + 1) * P], y[:, t, :], ident[:])
    mm.then_inc(filled, 1)


def tensor_output(pe, filled, drained, use, turned, tiles, bank, yT, wo):
    pe.wait_ge(drained, turned + 1)
    pe.wait_ge(drained, use - 2)
    for n, t in enumerate(tiles):
        mm = pe.matmul(bank[:, n * D:(n + 1) * D], yT[:, t, :], wo[:], start=True, stop=True)
    mm.then_inc(filled, 1)


def vector_sums(dve, filled, normed, drained, use, group, g, bank, rec, y):
    sums = bank[:, 0:TT * P].rearrange("p (q h c) -> p q h c", q=TT, h=4)
    dve.wait_ge(filled, use + 1)
    dve.reciprocal(rec[:], sums[:, :, :, DK]).then_inc(normed, 1)
    dve.wait_ge(normed, group + 1)
    dve.tensor_tensor(y[:, :, 4 * DK * g:4 * DK * (g + 1)].rearrange("p q (h d) -> p q h d", h=4),
                      sums[:, :, :, 0:DK], rec[:].unsqueeze(3).broadcast_to([P, TT, 4, DK]),
                      ALU.mult).then_inc(drained, 1)


def vector_turn(dve, filled, drained, use, tiles, bank, yT):
    dve.wait_ge(filled, use + 1)
    dve.tensor_copy(yT[:, tiles[0]:tiles[-1] + 1, :],
                    bank[:, 0:len(tiles) * P].rearrange("p (t q) -> p t q", q=P)).then_inc(drained, 1)


def vector_output(dve, filled, drained, use, tiles, bank, x, b):
    n = len(tiles)
    part = x[:, TT * b + tiles[0]:TT * b + tiles[0] + n, :] if isinstance(b, int) else \
        x[:, bass.ds(b * TT + tiles[0], n), :]
    dve.wait_ge(filled, use + 1)
    dve.tensor_tensor(part, bank[:, 0:n * D].rearrange("p (t d) -> p t d", t=n), part, ALU.add)\
       .then_inc(drained, 1)


SU = 2 * G
SA = 12
SRING = SA + 1 + G + 2 * TT


def self_banks():
    return [(par, 1, 2 * i, 2) for i in range(G) for par in range(2)] + \
           [(par, 0, 4 * i, 4) for i in range(2) for par in range(2)]


def self_ring(u, first, last):
    jobs = []
    if u == 1 and not first:
        jobs.append(("sums", G - 1))
    if u in (2, 3) and not first:
        jobs += [(("turn", "output")[u - 2], [t]) for t in range(TT)]
    if u in (3, 5, 7):
        jobs.append(("sums", (u - 3) // 2))
    if not last and 2 <= u <= 4:
        jobs += [("scores", a) for a in range(4 * (u - 2), 4 * (u - 1))]
    if not last and u == 6:
        jobs.append(("maxima", 0))
    return jobs


def over_pairs(eng, batch):
    batch(0, 0, 0, True, False)
    with eng.Fori(0, B // 2 - 1) as i:
        batch(i * 2 + 1, 1, i, False, False)
        batch(i * 2 + 2, 0, i + 1, False, False)
    batch(B - 1, 1, B // 2 - 1, False, True)


def self_attention_stage(nc, io, scr, ring, S4, U, x, v_all, ident, identb):
    with ExitStack() as ctx:
        def sb(name, shape, dt=F32):
            return ctx.enter_context(nc.sbuf_tensor("s_" + name, shape, dt))
        kb = [sb(f"k{i}", [P, GJ, T], BF16) for i in range(2)]
        qb = [sb(f"q{i}", [P, 2, GJ, T], BF16) for i in range(2)]
        vv = [sb(f"v{i}", [P, TT, H, VW]) for i in range(2)]
        mask32 = sb("mask32", [P, 2, P])
        mask = sb("mask", [P, 2, 4, P], BF16)
        wo = sb("wo", [D, D])
        probs = sb("probs", [P, 4, 2, 2 * T])
        nmax, nrest, zero = (sb(n, [P, 2, 2 * GJ]) for n in ("nmax", "nrest", "zero"))
        mparts = sb("mparts", [P, 2, MP, 2 * GJ], BF16)
        mrows = sb("mrows", [4 * MP * GJ, P], BF16)
        ub = [sb(f"u{i}", [P, T]) for i in range(2)]
        rec = [sb(f"rec{i}", [P, TT, 4]) for i in range(2)]
        y = sb("y", [P, TT, D])
        yT = sb("yT", [D, TT, P])
        (w_in, set_up, filled, drained, scored, exped, valued, evac, normed, msplit, m0, m1) = sems(
            nc, ctx, "s_w_in s_set_up s_ring_filled s_ring_drained s_scored s_exped s_valued s_evac "
                     "s_normed s_msplit s_max_in0 s_max_in1")
        m_in = [m0, m1]
        load_in = sems(nc, ctx, "s_load_in0 s_load_in1")
        S = S4.rearrange("p (u c w) -> p u c w", u=2, c=2)
        MC = 2 * GJ * MP
        NL = 4

        def base(b, first):
            return SA + 1 if first else (b - 1) * SRING + SA + 1 + SRING - 1 - 2 * TT

        AFTER = base(B - 1, False) + G + 2 * TT

        with nc.Block() as block:

            @block.sync
            def _(sp):
                sp.dma_start(mask32[:], io["masks"]).then_inc(w_in, 16)
                sp.dma_start(wo[:], io["swo"]).then_inc(w_in, 16)
                sp.wait_ge(set_up, 8)

                def load(b, s):
                    toks = slice(b * T, (b + 1) * T) if isinstance(b, int) else bass.ds(b * T, T)
                    sp.dma_start(kb[s][0:2 * PROWS, :, :],
                                 scr["ks_self"][:, :, :, toks].rearrange("c r n t -> (c r) n t"))\
                      .then_inc(load_in[s], 16)
                    for par in range(2):
                        sp.dma_start(qb[s][PROWS * par:PROWS * (par + 1), par, :, :],
                                     scr["qs_self"][par, :, :, toks]).then_inc(load_in[s], 16)
                    vsrc = v_all[:, TT * b:TT * (b + 1)] if isinstance(b, int) else \
                        v_all[:, bass.ds(b * TT, TT)]
                    sp.dma_start(vv[s][:].rearrange("p t h v -> p (t h v)"),
                                 vsrc.rearrange("p t h v -> p (t h v)")).then_inc(load_in[s], 16)

                def maxima_rows(use, s):
                    sp.wait_ge(drained, use + 1)
                    for par in range(2):
                        row = 2 * PROWS + MP * par
                        sp.dma_start(qb[s][row:row + MP, par, :, :].rearrange("p j q -> p (j q)"),
                                     mrows[MC * par:MC * (par + 1), :]).then_inc(m_in[s], 16)

                load(0, 0)
                load(1, 1)
                maxima_rows(SA, 0)

                def batch(b, s, half, first, last):
                    if not first and not last:
                        sp.wait_ge(valued, SU * b)
                        load(b + 1, 1 - s)
                    n = base(b, first)
                    for u in range(SU):
                        for kind, a in self_ring(u, first, last):
                            if kind == "maxima":
                                maxima_rows(n, 1 - s)
                            n = n + 1

                over_pairs(sp, batch)

            @block.tensor
            def _(pe):
                pe.wait_ge(w_in, 32)
                pe.wait_ge(set_up, 8)

                def scores_rows(use, r, s, a, wait):
                    par, qt, gj, cnt = self_banks()[a]
                    if wait:
                        pe.wait_ge(drained, use - 2)
                    keys = (qt + 1) * P
                    rows = slice(0, 2 * PROWS)
                    for n in range(cnt):
                        pe.matmul(ring[r][:, n * keys:(n + 1) * keys],
                                  qb[s][rows, par, gj + n, qt * P:(qt + 1) * P],
                                  kb[s][rows, gj + n, 0:keys],
                                  start=(n == 0), stop=False, skip_group_check=True)
                    out = ring[r][:].rearrange("p (n k) -> p n k", n=cnt)[:, :, qt * P:keys]
                    pe.matmul(out, identb[:], mask[:, 0, 0:cnt, :], start=False, stop=True,
                              skip_group_check=True).then_inc(filled, 1)

                def turn_maxima(use, r, nsplit):
                    pe.wait_ge(msplit, nsplit)
                    pe.wait_ge(drained, use - 2)
                    pe.transpose(ring[r][:].bitcast(BF16)[0:2 * MC, 0:P],
                                 mparts[:].rearrange("p c m n -> p (c m n)"), identb[:])\
                      .then_inc(filled, 1)

                def values(n, u, s, gn):
                    g, kt = u // 2, u % 2
                    pe.wait_ge(exped, n + 1)
                    if kt == 0 and gn is not None:
                        pe.wait_ge(evac, gn)
                    for par in range(2):
                        for j in range(2):
                            t, w = 2 * j + par, T - kt * P
                            mm = pe.matmul(U[32 * t:32 * t + VW, kt * P:T],
                                           vv[s][:, kt, 4 * g + t, :],
                                           probs[:, u % 4, j, par * w:(par + 1) * w],
                                           start=(kt == 0), stop=(kt == 1), skip_group_check=True)
                    mm.then_inc(valued, 1)

                pe.wait_ge(load_in[0], 16 * NL)
                for a in range(SA):
                    scores_rows(a, a % 3, 0, a, a >= 3)
                turn_maxima(SA, SA % 3, 4)

                def batch(b, s, half, first, last):
                    n0, rb = b * SU, (SA + 1 if first else SA + SRING - 2 * TT)
                    use, k, last_sums, turned = base(b, first), 0, None, {}
                    for u in range(SU):
                        g, kt = u // 2, u % 2
                        if u == 0:
                            pe.wait_ge(load_in[s], (half + 1) * 16 * NL)
                            pe.wait_ge(m_in[s], (half + 1) * 32)
                        if not (first and u < 2):
                            pe.wait_ge(exped, n0 + u - 1)
                        w = T - kt * P
                        rows = slice(0, 2 * (PROWS + MP))
                        for j in range(2):
                            pe.matmul(S[:, u % 2, j, 0:2 * w],
                                      kb[s][rows, 2 * g + j, kt * P:(kt + 1) * P],
                                      qb[s][rows, :, 2 * g + j, kt * P:T],
                                      start=True, stop=False, skip_group_check=True)
                            mm = pe.matmul(
                                S[:, u % 2, j, 0:2 * w].rearrange("p (c q) -> p c q", c=2)[:, :, 0:P],
                                identb[:], mask[:, 1, 0:2, :], start=False, stop=True,
                                skip_group_check=True)
                        mm.then_inc(scored, 1)
                        for kind, a in self_ring(u, first, last):
                            r = (rb + k) % 3
                            if kind == "scores":
                                if a == 0:
                                    pe.wait_ge(load_in[1 - s], (half + (1 + s)) * 16 * NL)
                                scores_rows(use + k, r, 1 - s, a, True)
                            elif kind == "maxima":
                                turn_maxima(use + k, r, (b + 2) * 4)
                            elif kind == "sums":
                                if u == 1:
                                    last_sums = use + k
                                tensor_sums(pe, filled, evac, drained, use + k, ring[r], ub[a % 2],
                                            b * G + a + 1 - (G if u == 1 else 0), ident)
                            elif kind == "turn":
                                turned[a[0]] = use + k
                                tensor_turn(pe, filled, drained, use + k, last_sums, a, ring[r], y, ident)
                            else:
                                tensor_output(pe, filled, drained, use + k, turned[a[0]], a, ring[r],
                                              yT, wo)
                            k += 1
                        if u > 0:
                            values(n0 + u - 1, u - 1, s, None if first and u == 1 else b * G + (u - 1) // 2)
                        elif not first:
                            values(n0 - 1, SU - 1, 1 - s, None)

                over_pairs(pe, batch)
                values(B * SU - 1, SU - 1, 1, None)
                tensor_sums(pe, filled, evac, drained, AFTER, ring[AFTER % 3],
                            ub[(G - 1) % 2], B * G, ident)
                for t in range(TT):
                    n = AFTER + 1 + t
                    tensor_turn(pe, filled, drained, n, AFTER, [t], ring[n % 3], y, ident)
                for t in range(TT):
                    n = AFTER + 1 + TT + t
                    tensor_output(pe, filled, drained, n, n - TT, [t], ring[n % 3], yT, wo)

            @block.scalar
            def _(act):
                def evacuate(group, gn, wait):
                    act.wait_ge(valued, gn * 2 + 2)
                    if wait:
                        act.wait_ge(normed, gn - 1)
                    act.copy(ub[group % 2][:], U[:, 0:T]).then_inc(evac, 1)

                def batch(b, s, half, first, last):
                    for u in range(SU):
                        n = b * SU + u
                        act.wait_ge(scored, n + 1)
                        if not (first and u < 4):
                            act.wait_ge(valued, n - 3)
                        w = 2 * (T - (u % 2) * P)
                        act.activation(probs[:, u % 4, :, 0:w], S[:, u % 2, :, 0:w], ACT.Exp)\
                           .then_inc(exped, 1)
                        if u % 2 == 0 and not (first and u == 0):
                            group = u // 2 - 1
                            evacuate(group % G, b * G + group, not (first and u < 6))

                over_pairs(act, batch)
                evacuate(G - 1, B * G - 1, True)

            @block.gpsimd
            def _(pool):
                for i in range(2):
                    pool.memset(kb[i][:], 1.0).then_inc(set_up, 1)
                    pool.memset(qb[i][:], 0.0).then_inc(set_up, 1)

                def split(b, use):
                    pool.wait_ge(drained, use)
                    pool.tensor_tensor(mparts[:, :, 0, :], nmax[:], zero[:], ALU.add).then_inc(msplit, 1)
                    pool.wait_ge(msplit, b * 4 + 1)
                    pool.tensor_tensor(nrest[:], nmax[:], mparts[:, :, 0, :], ALU.subtract)\
                        .then_inc(msplit, 1)
                    pool.wait_ge(msplit, b * 4 + 2)
                    pool.tensor_tensor(mparts[:, :, 1, :], nrest[:], zero[:], ALU.add).then_inc(msplit, 1)
                    pool.wait_ge(msplit, b * 4 + 3)
                    pool.tensor_tensor(mparts[:, :, 2, :], nrest[:], mparts[:, :, 1, :], ALU.subtract)\
                        .then_inc(msplit, 1)

                pool.memset(zero[:], 0.0).then_inc(set_up, 1)
                pool.wait_ge(set_up, 8)
                split(0, SA)

                def batch(b, s, half, first, last):
                    n = base(b, first)
                    for u in range(SU):
                        for kind, a in self_ring(u, first, last):
                            n = n + 1
                            if kind == "scores" and a == SA - 1:
                                split(b + 1, n)

                over_pairs(pool, batch)

            @block.vector
            def _(dve):
                dve.memset(U[:], 0.0).then_inc(set_up, 1)
                dve.wait_ge(w_in, 32)
                for i in range(2):
                    dve.tensor_copy(mask[:, i, :, :], mask32[:, i, :].unsqueeze(1)
                                    .broadcast_to([P, 4, P])).then_inc(set_up, 1)

                def row_max(use, r, a):
                    par, qt, gj, cnt = self_banks()[a]
                    dve.wait_ge(filled, use + 1)
                    out = nmax[:, par, :].rearrange("p (n q) -> p n q", q=TT)[:, gj:gj + cnt, qt]
                    dve.tensor_reduce(out, ring[r][:].rearrange("p (n k) -> p n k", n=cnt), AX.X,
                                      ALU.max, negate=True).then_inc(drained, 1)

                def maxima_out(use, r, s, half, wait):
                    dve.wait_ge(filled, use + 1)
                    if wait:
                        dve.wait_ge(m_in[s], (half + 1) * 32)
                    dve.tensor_copy(mrows[:], ring[r][:].bitcast(BF16)[0:2 * MC, 0:P])\
                       .then_inc(drained, 1)

                for a in range(SA):
                    row_max(a, a % 3, a)
                maxima_out(SA, SA % 3, 0, 0, False)

                def batch(b, s, half, first, last):
                    use, rb, k = base(b, first), (SA + 1 if first else SA + SRING - 2 * TT), 0
                    for u in range(SU):
                        for kind, a in self_ring(u, first, last):
                            r = (rb + k) % 3
                            if kind == "scores":
                                row_max(use + k, r, a)
                            elif kind == "maxima":
                                maxima_out(use + k, r, s, half, True)
                            elif kind == "sums":
                                vector_sums(dve, filled, normed, drained, use + k,
                                            b * G + a - (G if u == 1 else 0), a, ring[r], rec[a % 2], y)
                            elif kind == "turn":
                                vector_turn(dve, filled, drained, use + k, a, ring[r], yT)
                            else:
                                vector_output(dve, filled, drained, use + k, a, ring[r], x, b - 1)
                            k += 1

                over_pairs(dve, batch)
                vector_sums(dve, filled, normed, drained, AFTER, B * G - 1, G - 1, ring[AFTER % 3],
                            rec[(G - 1) % 2], y)
                for t in range(TT):
                    n = AFTER + 1 + t
                    vector_turn(dve, filled, drained, n, [t], ring[n % 3], yT)
                for t in range(TT):
                    n = AFTER + 1 + TT + t
                    vector_output(dve, filled, drained, n, [t], ring[n % 3], x, B - 1)


def query_stage(nc, io, scr, banks, x, xn, xnT, ident, stored_q):
    with ExitStack() as ctx:
        def sb(name, shape, dt=F32):
            return ctx.enter_context(nc.sbuf_tensor("q_" + name, shape, dt))
        w, bias, sbias, bo = sb("w", [D, D]), sb("b", [D, 1]), sb("sb", [D, 1]), sb("bo", [P, D])
        whole = sb("whole", [D, N])
        part = [sb(f"part{j}", [D, N], BF16) for j in range(3)]
        rest = [sb(f"rest{i}", [D, CK]) for i in range(2)]
        nm = Norm(nc, ctx, "q_n_")
        (w_in, scaled, proj, first, whole_s, rest_s, second, third, biased) = sems(
            nc, ctx, "q_w_in q_scaled q_proj q_first q_whole q_rest q_second q_third q_biased")
        with nc.Block() as block:

            @block.sync
            def _(sp):
                for dst, src in ((w, io["xwq"]), (bias, io["xbq"]), (bo, io["xbo"])):
                    sp.dma_start(dst[:], src).then_inc(w_in, 16)
                for half in range(2):
                    sp.wait_ge(third, 2 * (half + 1))
                    b0, nb = half * B // 2, B // 2
                    for r in range(NPROD):
                        sp.dma_start(
                            scr["qs"][:, DK * r:DK * (r + 1), :, b0 * T:(b0 + nb) * T]
                            .rearrange("c r n t -> c (r n) t"),
                            part[Q_PART[r] - 1][:, b0 * T:(b0 + nb) * T]).then_inc(stored_q, 16)
                sp.wait_ge(stored_q, 16 * 2 * NPROD)

            @block.tensor
            def _(pe):
                for c in range(NC):
                    norm_tensor(pe, nm, xn, ident, banks[5:7], c)
                    if c == 0:
                        pe.wait_ge(w_in, 48)
                    pe.wait_ge(nm.out, c + 1)
                    pe.matmul(banks[c], w[:], xnT[:, c * CK:(c + 1) * CK],
                              start=True, stop=True).then_inc(proj, 1)

            @block.scalar
            def _(act):
                norm_scalar_root(act, nm)
                norm_scalar_out(act, nm, banks[5:7], xnT, 0)
                for c in range(NC):
                    if c + 1 < NC:
                        norm_scalar_out(act, nm, banks[5:7], xnT, c + 1)
                    o = slice(c * CK, (c + 1) * CK)
                    act.wait_ge(whole_s, c + 1)
                    act.copy(part[0][:, o], whole[:, o]).then_inc(first, 1)
                    act.wait_ge(rest_s, c + 1)
                    act.copy(part[1][:, o], rest[c % 2][:]).then_inc(second, 1)

            @block.gpsimd
            def _(pool):
                pool.wait_ge(nm.ready, NT)
                pool.wait_ge(w_in, 48)
                pool.tensor_tensor(x[:], x[:], bo[:].unsqueeze(1).broadcast_to([P, NT, D]), ALU.add)\
                    .then_inc(biased, 1)

            @block.vector
            def _(dve):
                norm_vector(dve, nm, x, xn)
                dve.wait_ge(w_in, 48)
                dve.tensor_scalar(sbias[:], bias[:], SCALE, None, ALU.mult).then_inc(scaled, 1)
                dve.wait_ge(scaled, 1)
                for c in range(NC):
                    o = slice(c * CK, (c + 1) * CK)
                    dve.wait_ge(proj, c + 1)
                    dve.tensor_scalar(whole[:, o], banks[c], SCALE, sbias[:], ALU.mult, ALU.add)\
                       .then_inc(whole_s, 1)
                    dve.wait_ge(first, c + 1)
                    dve.tensor_tensor(rest[c % 2][:], whole[:, o], part[0][:, o], ALU.subtract)\
                       .then_inc(rest_s, 1)
                    dve.wait_ge(second, c + 1)
                    dve.tensor_tensor(part[2][:, o], rest[c % 2][:], part[1][:, o], ALU.subtract)\
                       .then_inc(third, 1)


XA = 2 * 2 * TT * CH
NG = B * G


def cross_banks():
    return [(j, qt, c, par) for j in range(2) for qt in range(TT) for c in range(CH) for par in range(2)]


def cross_ring(g, kt, first, last):
    jobs = []
    if kt == 1 and not (last and g == G - 1):
        jobs.append(("maxima", 0))
    if kt == 2 and not (first and g == 0):
        jobs.append(("sums", 0))
    if kt in (3, 4) and g == 0 and not first:
        jobs.append((("turn", "output")[kt - 3], range(TT)))
    if not (last and g >= G - 2):
        jobs += [("scores", a) for a in range(XA * kt // KT, XA * (kt + 1) // KT)]
    return jobs


def cross_uses(first, last):
    return sum(len(cross_ring(g, kt, first, last)) for g in range(G) for kt in range(KT))


def over_batches(eng, batch):
    batch(0, True, False)
    with eng.Fori(1, B - 1) as b:
        batch(b, False, False)
    batch(B - 1, False, True)


def cross_attention_stage(nc, io, scr, ring, S4, U, x, ident, identb, stored, stored_log):
    with ExitStack() as ctx:
        def sb(name, shape, dt=F32):
            return ctx.enter_context(nc.sbuf_tensor("x_" + name, shape, dt))
        kb = [sb(f"k{i}", [P, 2, S2], BF16) for i in range(G)]
        qb = [sb(f"q{i}", [P, 2, 2, T], BF16) for i in range(G)]
        vv = [sb(f"v{i}", [P, KT, 4, VW]) for i in range(G)]
        wo = sb("wo", [D, D])
        probs = sb("probs", [P, 4, 2, 2 * T])
        pmax = sb("pmax", [P, 2, 2 * TT, CH])
        nmax, nrest, zero = (sb(n, [P, 2, 2 * TT]) for n in ("nmax", "nrest", "zero"))
        mparts = sb("mparts", [P, 2, MP, 2 * TT], BF16)
        mrows = sb("mrows", [4 * MP * TT, P], BF16)
        ub = [sb(f"u{i}", [P, T]) for i in range(2)]
        rec = [sb(f"rec{i}", [P, TT, 4]) for i in range(2)]
        y = sb("y", [P, TT, D])
        yT = sb("yT", [D, TT, P])
        (w_in, set_up, filled, drained, maxed, scored, exped, valued, evac, normed, msplit) = sems(
            nc, ctx, "x_w_in x_set_up x_ring_filled x_ring_drained x_maxed x_scored x_exped x_valued "
                     "x_evac x_normed x_msplit")
        m_in = sems(nc, ctx, "x_max_in0 x_max_in1 x_max_in2 x_max_in3")
        load_in = sems(nc, ctx, "x_load_in0 x_load_in1 x_load_in2 x_load_in3")
        S = S4.rearrange("p (u c w) -> p u c w", u=2, c=2)
        MC = 2 * TT * MP
        NL = 4
        UNITS = G * KT

        PRO = 2 * XA + 1
        WI = 1 + 2 * G
        U0, UM, UL = cross_uses(True, False), cross_uses(False, False), cross_uses(False, True)
        assert UM % 3 == 0

        def base(b, first):
            return PRO if first else (b - 1) * UM + PRO + U0

        def start_bank(first):
            return PRO if first else PRO + U0

        AFTER = PRO + U0 + (B - 2) * UM + UL

        with nc.Block() as block:

            @block.sync
            def _(sp):
                sp.dma_start(wo[:], io["xwo"]).then_inc(w_in, 16)
                sp.wait_ge(set_up, 2 * G + 2)
                for i in range(G):
                    for par in range(2):
                        sp.dma_start(qb[i][KROWS * par:KROWS * par + MP, par, :, :]
                                     .rearrange("p j q -> p (j q)"), kb[G - 1][0:MP, 0, 0:2 * T])\
                          .then_inc(w_in, 16)
                for i in range(2):
                    sp.wait_ge(stored[i], 16 * (NPROD + 1) * (B // 2 + 1))
                sp.wait_ge(stored_log, 16 * 2 * MP)

                def load(b, g):
                    one = slice(b, b + 1) if isinstance(b, int) else bass.ds(b, 1)
                    toks = slice(b * T, (b + 1) * T) if isinstance(b, int) else bass.ds(b * T, T)
                    sp.dma_start(kb[g][0:2 * KROWS, :, :],
                                 scr["ks"][one, :, :, 2 * g:2 * g + 2, :]
                                 .rearrange("o c r j k -> (o c r) j k")).then_inc(load_in[g], 16)
                    for par in range(2):
                        sp.dma_start(qb[g][KROWS * par + MP:KROWS * (par + 1), par, :, :],
                                     scr["qs"][par, :, 2 * g:2 * g + 2, toks])\
                          .then_inc(load_in[g], 16)
                    sp.dma_start(vv[g][:].rearrange("p t h v -> p (t h v)"),
                                 scr["v"][one, :, g * KT * 4 * VW:(g + 1) * KT * 4 * VW]
                                 .rearrange("o p v -> (o p) v")).then_inc(load_in[g], 16)

                def maxima_rows(use, g):
                    sp.wait_ge(drained, use + 1)
                    for par in range(2):
                        row = 2 * KROWS + MP * par
                        sp.dma_start(qb[g][row:row + MP, par, :, :].rearrange("p j q -> p (j q)"),
                                     mrows[MC * par:MC * (par + 1), :]).then_inc(m_in[g], 16)

                for g in range(G - 1):
                    load(0, g)
                maxima_rows(XA, 0)
                sp.wait_ge(w_in, 16 * WI)
                load(0, G - 1)

                def batch(b, first, last):
                    n = base(b, first)
                    for g in range(G):
                        if not (first and g == 0) and not (last and g > 0):
                            sp.wait_ge(valued, b * UNITS + g * KT)
                            load(b if g == 0 else b + 1, (g - 1) % G)
                        for kt in range(KT):
                            for kind, a in cross_ring(g, kt, first, last):
                                if kind == "maxima":
                                    maxima_rows(n, (g + 1) % G)
                                n = n + 1

                over_batches(sp, batch)

            @block.tensor
            def _(pe):
                pe.wait_ge(w_in, 16 * WI)
                pe.wait_ge(set_up, 2 * G + 2)

                def scores_rows(use, r, g, a, wait):
                    j, qt, c, par = cross_banks()[a]
                    if wait:
                        pe.wait_ge(drained, use - 2)
                    rows = slice(0, 2 * KROWS)
                    pe.matmul(ring[r][:, 0:CW[c]], qb[g][rows, par, j, qt * P:(qt + 1) * P],
                              kb[g][rows, j, CO[c]:CO[c] + CW[c]], start=True, stop=True)\
                      .then_inc(filled, 1)

                def turn_maxima(use, r, groups):
                    pe.wait_ge(msplit, groups * 4)
                    pe.wait_ge(drained, use - 2)
                    pe.transpose(ring[r][:].bitcast(BF16)[0:2 * MC, 0:P],
                                 mparts[:].rearrange("p c m n -> p (c m n)"), identb[:])\
                      .then_inc(filled, 1)

                def values(n, g, kt, groups):
                    pe.wait_ge(exped, n + 1)
                    if kt == 0 and groups is not None:
                        pe.wait_ge(evac, groups)
                    m = P if kt < KT - 1 else LAST
                    for par in range(2):
                        for j in range(2):
                            t = 2 * j + par
                            mm = pe.matmul(U[32 * t:32 * t + VW, 0:T], vv[g][0:m, kt, t, :],
                                           probs[0:m, (g * KT + kt) % 4, j, par * T:(par + 1) * T],
                                           start=(kt == 0), stop=(kt == KT - 1), skip_group_check=True)
                    mm.then_inc(valued, 1)

                pe.wait_ge(load_in[0], 16 * NL)
                for a in range(XA):
                    scores_rows(a, a % 3, 0, a, a >= 3)
                turn_maxima(XA, XA % 3, 1)
                pe.wait_ge(load_in[1], 16 * NL)
                for a in range(XA):
                    scores_rows(XA + 1 + a, (XA + 1 + a) % 3, 1, a, True)

                def batch(b, first, last):
                    use, k = base(b, first), 0
                    for g in range(G):
                        pe.wait_ge(m_in[g], (b + 1) * 32)
                        for kt in range(KT):
                            u = g * KT + kt
                            if not (first and u < 2):
                                pe.wait_ge(exped, b * UNITS + u - 1)
                            m = P if kt < KT - 1 else LAST
                            rows = slice(0, 2 * (KROWS + MP))
                            for j in range(2):
                                mm = pe.matmul(S[0:m, u % 2, j, :], kb[g][rows, j, kt * P:kt * P + m],
                                               qb[g][rows, :, j, :], start=True, stop=True)
                            mm.then_inc(scored, 1)
                            for kind, a in cross_ring(g, kt, first, last):
                                r = (start_bank(first) + k) % 3
                                if kind == "scores":
                                    if a == 0:
                                        pe.wait_ge(load_in[(g + 2) % G],
                                                   (b + 1 + (g + 2) // G) * (16 * NL))
                                    scores_rows(use + k, r, (g + 2) % G, a, True)
                                elif kind == "maxima":
                                    turn_maxima(use + k, r, b * G + g + 2)
                                elif kind == "sums":
                                    last_sums = use + k
                                    tensor_sums(pe, filled, evac, drained, use + k, ring[r],
                                                ub[(g - 1) % 2], b * G + g, ident)
                                elif kind == "turn":
                                    turned = use + k
                                    tensor_turn(pe, filled, drained, use + k, last_sums, a, ring[r], y,
                                                ident)
                                else:
                                    tensor_output(pe, filled, drained, use + k, turned, a, ring[r],
                                                  yT, wo)
                                k += 1
                            if u > 0:
                                pg, pk = divmod(u - 1, KT)
                                values(b * UNITS + u - 1, pg, pk, None if first and pg == 0 else b * G + pg)
                            elif not first:
                                values(b * UNITS - 1, G - 1, KT - 1, None)

                over_batches(pe, batch)
                values(B * UNITS - 1, G - 1, KT - 1, None)
                tensor_sums(pe, filled, evac, drained, AFTER, ring[AFTER % 3],
                            ub[(G - 1) % 2], NG, ident)
                n = AFTER + 1
                tensor_turn(pe, filled, drained, n, AFTER, range(TT), ring[n % 3], y, ident)
                tensor_output(pe, filled, drained, n + 1, n, range(TT), ring[(n + 1) % 3], yT, wo)

            @block.scalar
            def _(act):
                def evacuate(g, units, groups):
                    act.wait_ge(valued, units)
                    if groups is not None:
                        act.wait_ge(normed, groups)
                    act.copy(ub[g % 2][:], U[:, 0:T]).then_inc(evac, 1)

                def batch(b, first, last):
                    for u in range(UNITS):
                        g, kt = divmod(u, KT)
                        m = P if kt < KT - 1 else LAST
                        act.wait_ge(scored, b * UNITS + u + 1)
                        if not (first and u < 4):
                            act.wait_ge(valued, b * UNITS + u - 3)
                        act.activation(probs[0:m, u % 4, :, :], S[0:m, u % 2, :, :], ACT.Exp)\
                           .then_inc(exped, 1)
                        if kt == 0 and not (first and g == 0):
                            evacuate((g - 1) % G, b * UNITS + u, None if first and g < 3 else b * G + g - 2)

                over_batches(act, batch)
                evacuate(G - 1, B * UNITS, NG - 2)

            @block.gpsimd
            def _(pool):
                for i in range(G):
                    pool.memset(kb[i][:], 1.0).then_inc(set_up, 1)
                    pool.memset(qb[i][:], 0.0).then_inc(set_up, 1)

                def split(groups):
                    pool.wait_ge(maxed, groups + 1)
                    pool.tensor_tensor(mparts[:, :, 0, :], nmax[:], zero[:], ALU.add).then_inc(msplit, 1)
                    pool.wait_ge(msplit, groups * 4 + 1)
                    pool.tensor_tensor(nrest[:], nmax[:], mparts[:, :, 0, :], ALU.subtract)\
                        .then_inc(msplit, 1)
                    pool.wait_ge(msplit, groups * 4 + 2)
                    pool.tensor_tensor(mparts[:, :, 1, :], nrest[:], zero[:], ALU.add).then_inc(msplit, 1)
                    pool.wait_ge(msplit, groups * 4 + 3)
                    pool.tensor_tensor(mparts[:, :, 2, :], nrest[:], mparts[:, :, 1, :], ALU.subtract)\
                        .then_inc(msplit, 1)

                pool.memset(zero[:], 0.0).then_inc(set_up, 1)
                pool.wait_ge(set_up, 2 * G + 2)
                split(0)
                split(1)
                with pool.Fori(2, NG) as group:
                    split(group)

            @block.vector
            def _(dve):
                dve.memset(U[:], 0.0).then_inc(set_up, 1)

                def row_max(use, r, a, groups):
                    j, qt, c, par = cross_banks()[a]
                    if a == 0 and groups is not None:
                        dve.wait_ge(maxed, groups)
                    dve.wait_ge(filled, use + 1)
                    dve.tensor_reduce(pmax[:, par, 2 * j + qt, c:c + 1], ring[r][:, 0:CW[c]], AX.X,
                                      ALU.max).then_inc(drained, 1)
                    if a == XA - 1:
                        dve.wait_ge(drained, use + 1)
                        dve.tensor_reduce(nmax[:], pmax[:], AX.X, ALU.max, negate=True)\
                           .then_inc(maxed, 1)

                def maxima_out(use, r, last_slot, loads):
                    dve.wait_ge(filled, use + 1)
                    if loads is not None:
                        dve.wait_ge(m_in[last_slot], loads * 32)
                    dve.tensor_copy(mrows[:], ring[r][:].bitcast(BF16)[0:2 * MC, 0:P])\
                       .then_inc(drained, 1)

                for a in range(XA):
                    row_max(a, a % 3, a, None)
                maxima_out(XA, XA % 3, 0, None)
                for a in range(XA):
                    row_max(XA + 1 + a, (XA + 1 + a) % 3, a, 1)

                def batch(b, first, last):
                    use, k = base(b, first), 0
                    for g in range(G):
                        for kt in range(KT):
                            for kind, a in cross_ring(g, kt, first, last):
                                r = (start_bank(first) + k) % 3
                                if kind == "scores":
                                    row_max(use + k, r, a, b * G + g + 2)
                                elif kind == "maxima":
                                    maxima_out(use + k, r, g, b + 1)
                                elif kind == "sums":
                                    pg = (g - 1) % G
                                    vector_sums(dve, filled, normed, drained, use + k, b * G + g - 1,
                                                pg, ring[r], rec[pg % 2], y)
                                elif kind == "turn":
                                    vector_turn(dve, filled, drained, use + k, a, ring[r], yT)
                                else:
                                    vector_output(dve, filled, drained, use + k, a, ring[r], x, b - 1)
                                k += 1

                over_batches(dve, batch)
                vector_sums(dve, filled, normed, drained, AFTER, NG - 1, G - 1, ring[AFTER % 3],
                            rec[(G - 1) % 2], y)
                n = AFTER + 1
                vector_turn(dve, filled, drained, n, range(TT), ring[n % 3], yT)
                vector_output(dve, filled, drained, n + 1, range(TT), ring[(n + 1) % 3], x, B - 1)


FT = F // P
HU = E * FT


def expert_stage(nc, io, scr, banks, x, xn, xnT, ident, out):
    with ExitStack() as ctx:
        def sb(name, shape, dt=F32):
            return ctx.enter_context(nc.sbuf_tensor("e_" + name, shape, dt))
        wr, rank = sb("wr", [D, E]), sb("rank", [P, E])
        wg, wu, wd = sb("wg", [D, E, F]), sb("wu", [D, E, F]), sb("wd", [P, E, FT, D])
        names = "logit p q chosen1 chosen2 score cw"
        r = {n: sb("r_" + n, [P, NT, E]) for n in names.split()}
        s = {n: sb("s_" + n, [P, NT]) for n in "top sum inv first second best den".split()}
        cwT = sb("cwT", [E, N])
        cwb = sb("cwb", [P, E, N])
        xc = [sb(f"xc{i}", [D, CK]) for i in range(2)]
        act_out = [sb(f"silu{i}", [P, CK]) for i in range(2)]
        hid = [sb(f"hid{i}", [P, CK]) for i in range(4)]
        yT = sb("yT", [D, CK])
        res = sb("res", [P, NT, D])
        nm = Norm(nc, ctx, "e_n_")
        (w_in, logits, shifted, exped, step, cw_turned, cw_out, cw_st, scaled, up, silued, hidden,
         downed, summed, y_out, y_turned, added, stored_out) = sems(
            nc, ctx, "e_w_in e_logits e_shifted e_exped e_step e_cw_turned e_cw_out e_cw_st e_scaled "
                     "e_up e_silued e_hidden e_downed e_summed e_y_out e_y_turned e_added e_stored_out")
        cw_in = sems(nc, ctx, " ".join(f"e_cw_in{c}" for c in range(NC)))
        def tiles(a, c):
            return a[:, CT * c:CT * (c + 1), :] if isinstance(c, int) else a[:, bass.ds(c * CT, CT), :]

        gate, upb = banks[0:2], banks[2:4]
        yb, tb = banks[4], banks[5]

        with nc.Block() as block:

            @block.sync
            def _(sp):
                for dst, src in ((wr, io["wr"]), (rank, io["rank"]), (wg, io["wg"]), (wu, io["wu"]),
                                 (wd, io["wd"])):
                    sp.dma_start(dst[:], src).then_inc(w_in, 16)
                for c in range(NC):
                    o = slice(c * CK, (c + 1) * CK)
                    sp.wait_ge(cw_out, c + 1)
                    sp.dma_start(scr["cw"][:, o], cwT[:, o]).then_inc(cw_st, 16)
                    sp.wait_ge(cw_st, 16 * (c + 1))
                    sp.dma_start(cwb[:, :, o], scr["cw"][:, o].partition_broadcast(P))\
                      .then_inc(cw_in[c], 16)

                def store(c):
                    sp.wait_ge(added, c + 1)
                    dst = out[c * CK:(c + 1) * CK, :] if isinstance(c, int) else out[bass.ds(c * CK, CK), :]
                    sp.dma_start(dst.rearrange("(t p) d -> p t d", p=P), tiles(res, c))\
                      .then_inc(stored_out, 16)

                with sp.Fori(0, NC) as c:
                    store(c)
                sp.wait_ge(stored_out, 16 * NC)

            @block.tensor
            def _(pe):
                for c in range(NC):
                    norm_tensor(pe, nm, xn, ident, banks[5:7], c)
                    pe.wait_ge(nm.out, c + 1)
                    if c == 0:
                        pe.wait_ge(w_in, 16 * 5)
                    for t in range(CT * c, CT * (c + 1)):
                        mm = pe.matmul(banks[0][:, t * E:(t + 1) * E], xnT[:, t * P:(t + 1) * P], wr[:],
                                       start=True, stop=True, skip_group_check=True)
                mm.then_inc(logits, 1)
                pe.wait_ge(step, RSTEPS)
                for c in range(NC):
                    for t in range(CT):
                        mm = pe.transpose(banks[1 + c][0:E, t * P:(t + 1) * P],
                                          r["cw"][:, CT * c + t, :], ident[:])
                    mm.then_inc(cw_turned, 1)
                pe.wait_ge(cw_out, NC)

                def hidden_units(c, k, first):
                    e, f = divmod(k, FT)
                    o = slice(c * CK, (c + 1) * CK) if isinstance(c, int) else bass.ds(c * CK, CK)
                    if not (first and k < 2):
                        pe.wait_ge(hidden, c * HU + k - 1)
                    pe.matmul(gate[k % 2], wg[:, e, f * P:(f + 1) * P], xnT[:, o], start=True, stop=True)\
                      .then_inc(up, 1)
                    pe.wait_ge(scaled, c * E + e + 1)
                    pe.matmul(upb[k % 2], wu[:, e, f * P:(f + 1) * P], xc[e % 2][:], start=True, stop=True)\
                      .then_inc(up, 1)

                def down(c, k, first):
                    e, f = divmod(k, FT)
                    pe.wait_ge(hidden, c * HU + k + 1)
                    if k == 0 and not first:
                        pe.wait_ge(y_out, c)
                    mm = pe.matmul(yb, wd[:, e, f, :], hid[k % 4][:], start=(k == 0), stop=(k == HU - 1))
                    mm.then_inc(downed, 1)

                def turn_back(c):
                    pe.wait_ge(y_out, c + 1)
                    for t in range(CT):
                        mm = pe.transpose(tb[:, t * D:(t + 1) * D], yT[:, t * P:(t + 1) * P], ident[:])
                    mm.then_inc(y_turned, 1)

                def piece(c, first):
                    for k in range(HU):
                        hidden_units(c, k, first)
                        if k == 3 and not first:
                            turn_back(c - 1)
                        if k >= 2:
                            down(c, k - 2, first)
                    down(c, HU - 2, first)
                    down(c, HU - 1, first)

                piece(0, True)
                with pe.Fori(1, NC) as c:
                    piece(c, False)
                turn_back(NC - 1)

            @block.scalar
            def _(act):
                norm_scalar_root(act, nm)
                for c in range(NC):
                    norm_scalar_out(act, nm, banks[5:7], xnT, c)
                act.wait_ge(shifted, 1)
                act.activation(r["p"][:], r["p"][:], ACT.Exp).then_inc(exped, 1)
                for c in range(NC):
                    act.wait_ge(cw_turned, c + 1)
                    act.copy(cwT[:, c * CK:(c + 1) * CK], banks[1 + c][0:E, :]).then_inc(cw_out, 1)

                def piece(c, first):
                    for k in range(HU):
                        if k == 2 and not first:
                            y_evacuate(c - 1)
                        act.wait_ge(up, 2 * (c * HU + k) + 1)
                        if not (first and k < 2):
                            act.wait_ge(hidden, c * HU + k - 1)
                        act.activation(act_out[k % 2][:], gate[k % 2], ACT.Silu).then_inc(silued, 1)

                def y_evacuate(c):
                    act.wait_ge(downed, (c + 1) * HU)
                    act.copy(yT[:], yb).then_inc(y_out, 1)

                piece(0, True)
                with act.Fori(1, NC) as c:
                    piece(c, False)
                y_evacuate(NC - 1)

            @block.gpsimd
            def _(pool):
                def piece(c, first):
                    for e in range(E):
                        if not (first and e < 2):
                            pool.wait_ge(up, 2 * FT * (c * E + e - 1))
                        o = slice(c * CK, (c + 1) * CK)
                        pool.tensor_tensor(xc[e % 2][:], xnT[:, o], cwb[:, e, o], ALU.mult)\
                            .then_inc(scaled, 1)

                for c in range(NC):
                    pool.wait_ge(cw_in[c], 16)
                    piece(c, c == 0)

            @block.vector
            def _(dve):
                norm_vector(dve, nm, x, xn)
                dve.wait_ge(w_in, 16 * 5)
                dve.wait_ge(logits, 1)
                n = [0]

                def then(ins):
                    n[0] += 1
                    ins.then_inc(step, 1)
                    dve.wait_ge(step, n[0])

                def wide(a):
                    return a[:].unsqueeze(2).broadcast_to([P, NT, E])

                ranks = rank[:].unsqueeze(1).broadcast_to([P, NT, E])
                then(dve.tensor_copy(r["logit"][:], banks[0][:, 0:NT * E].rearrange("p (t e) -> p t e", e=E)))
                then(dve.tensor_reduce(s["top"][:], r["logit"][:], AX.X, ALU.max))
                dve.tensor_tensor(r["p"][:], r["logit"][:], wide(s["top"]), ALU.subtract).then_inc(shifted, 1)
                dve.wait_ge(exped, 1)
                then(dve.tensor_reduce(s["sum"][:], r["p"][:], AX.X, ALU.add))
                then(dve.reciprocal(s["inv"][:], s["sum"][:]))
                then(dve.tensor_tensor(r["p"][:], r["p"][:], wide(s["inv"]), ALU.mult))
                left = "p"
                for top, chosen in (("first", "chosen1"), ("second", "chosen2")):
                    then(dve.tensor_reduce(s[top][:], r[left][:], AX.X, ALU.max))
                    then(dve.tensor_tensor(r["score"][:], r[left][:], wide(s[top]), ALU.is_equal))
                    then(dve.tensor_tensor(r["score"][:], r["score"][:], ranks, ALU.mult))
                    then(dve.tensor_reduce(s["best"][:], r["score"][:], AX.X, ALU.max))
                    then(dve.tensor_tensor(r[chosen][:], r["score"][:], wide(s["best"]), ALU.is_equal))
                    if left == "p":
                        then(dve.scalar_tensor_tensor(out=r["q"][:], in0=r[chosen][:], scalar=-2.0,
                                                      in1=r["p"][:], op0=ALU.mult, op1=ALU.add))
                        left = "q"
                then(dve.tensor_tensor(r["score"][:], r["chosen1"][:], r["chosen2"][:], ALU.add))
                then(dve.tensor_tensor(r["score"][:], r["score"][:], r["p"][:], ALU.mult))
                then(dve.tensor_tensor(s["den"][:], s["first"][:], s["second"][:], ALU.add))
                then(dve.tensor_scalar(s["den"][:], s["den"][:], 1e-20, None, ALU.add))
                then(dve.reciprocal(s["inv"][:], s["den"][:]))
                then(dve.tensor_tensor(r["cw"][:], r["score"][:], wide(s["inv"]), ALU.mult))
                assert n[0] == RSTEPS

                def piece(c, first):
                    for k in range(HU):
                        if k == 4 and not first:
                            add_back(c - 1)
                        dve.wait_ge(silued, c * HU + k + 1)
                        dve.wait_ge(up, 2 * (c * HU + k) + 2)
                        if not (first and k < 4):
                            dve.wait_ge(downed, c * HU + k - 3)
                        dve.tensor_tensor(hid[k % 4][:], upb[k % 2], act_out[k % 2][:], ALU.mult)\
                           .then_inc(hidden, 1)

                def add_back(c):
                    dve.wait_ge(y_turned, c + 1)
                    dve.tensor_tensor(tiles(res, c), tb.rearrange("p (t d) -> p t d", d=D),
                                      tiles(x, c), ALU.add).then_inc(added, 1)

                piece(0, True)
                with dve.Fori(1, NC) as c:
                    piece(c, False)
                add_back(NC - 1)


RSTEPS = 22


def decoder_layer(nc, io, out):
    with ExitStack() as ctx:
        def sb(name, shape, dt=F32):
            return ctx.enter_context(nc.sbuf_tensor(name, shape, dt))

        def scratch(name, shape, dt):
            return nc.dram_tensor(name, shape, dt, kind="Internal").ap()
        scr = {
            "ks": scratch("scr_ks", [B, 2, KROWS, GJ, S2], BF16),
            "qs": scratch("scr_qs", [2, PROWS, GJ, N], BF16),
            "v": scratch("scr_v", [B, P, G * KT * 4 * VW], F32),
            "ks_self": scratch("scr_ks_self", [2, PROWS, GJ, N], BF16),
            "qs_self": scratch("scr_qs_self", [2, PROWS, GJ, N], BF16),
            "cw": scratch("scr_cw", [E, N], F32),
        }
        x, xn, xnT = sb("x", [P, NT, D]), sb("xn", [P, NT, D]), sb("xnT", [D, N])
        ident, identb = sb("ident", [P, P]), sb("identb", [P, P], BF16)
        v_all = sb("v_all", [P, NT, H, VW])
        S4 = ctx.enter_context(nc.psum_tensor("S4", [P, 4 * 512], F32))
        ring = [ctx.enter_context(nc.psum_tensor(f"ring{i}", [P, 512], F32)) for i in range(3)]
        U = ctx.enter_context(nc.psum_tensor("U", [P, 512], F32))
        banks = [S4[:, 512 * i:512 * (i + 1)] for i in range(4)] + [r[:] for r in ring] + [U[:]]
        cst_in, stored0, stored1, stored_log, stored_self, stored_q = sems(
            nc, ctx, "cst_in stored_context0 stored_context1 stored_log stored_self stored_q")
        with ExitStack() as held:
            kp = [[held.enter_context(nc.sbuf_tensor(f"kpart{i}_{j}", [D, S2], BF16)) for j in range(3)]
                  for i in range(2)]
            vb = [held.enter_context(nc.sbuf_tensor(f"vbuf{i}", [P, G, KT, 4 * VW], F32))
                  for i in range(2)]
            lp = [held.enter_context(nc.sbuf_tensor(f"logpart{j}", [B, S2], BF16)) for j in range(MP)]
            context_stage(nc, io, scr, banks, kp, vb, lp, [stored0, stored1], stored_log)
            self_projection_stage(nc, io, scr, banks, x, xn, xnT, v_all, ident, identb, cst_in,
                                  stored_self)
            self_attention_stage(nc, io, scr, ring, S4[:], U, x, v_all, ident, identb)
            query_stage(nc, io, scr, banks, x, xn, xnT, ident, stored_q)
            cross_attention_stage(nc, io, scr, ring, S4[:], U, x, ident, identb, [stored0, stored1],
                                  stored_log)
        expert_stage(nc, io, scr, banks, x, xn, xnT, ident, out)


def _layouts(a):
    c = np.ascontiguousarray
    perm = np.array([(4 * g + 2 * j + par) * DK + d
                     for par in range(2) for d in range(DK) for g in range(G) for j in range(2)])
    swap = np.array([(e // DK) * DK + (e % DK + DK // 2) % DK for e in perm])
    def row(b):
        return np.broadcast_to(b, (P, D))

    half = DK // 2
    freq = (1.0 / 10000.0 ** (2.0 * np.arange(half, dtype=np.float32) / DK)).astype(np.float32)
    ang = np.arange(T, dtype=np.float32)[:, None] * freq[None, :]
    d = perm % DK
    cos = np.cos(ang)[:, d % half].T.astype(np.float32)
    sin = (np.sin(ang)[:, d % half] * np.where(d < half, -1, 1)).T.astype(np.float32)
    hidden = np.where(np.arange(P)[None, :] > np.arange(P)[:, None], MASKED, 0).astype(np.float32)
    scale = np.float32(SCALE)
    return {
        "x": a["x"].reshape(N, D),
        "ctxT": c(a["ctx_1024"].transpose(2, 0, 1).reshape(D, B * S2)),
        "weights": a["fside_BxS2_0"],
        "w_q": c(a["L0_attn_WQ_w"].T[:, perm]), "w_q_swap": c(a["L0_attn_WQ_w"].T[:, swap]),
        "w_k": c(a["L0_attn_WK_w"].T[:, perm]), "w_k_swap": c(a["L0_attn_WK_w"].T[:, swap]),
        "b_q": a["L0_attn_WQ_b"][perm, None], "b_q_swap": a["L0_attn_WQ_b"][swap, None],
        "b_k": a["L0_attn_WK_b"][perm, None], "b_k_swap": a["L0_attn_WK_b"][swap, None],
        "rot_q": cos * scale, "rot_q_swap": sin * scale, "rot_k": cos, "rot_k_swap": sin,
        "swv": c(a["L0_attn_WV_w"].T), "sbv": row(a["L0_attn_WV_b"]),
        "swo": c(a["L0_attn_Wo_w"].T), "sbo": row(a["L0_attn_Wo_b"]),
        "xwq": c(a["L0_xattn_wq"][:, perm]), "xbq": a["L0_xattn_bq"][perm, None],
        "xwk": c(a["L0_xattn_wk"][:, perm]), "xbk": a["L0_xattn_bk"][perm, None],
        "xwv": a["L0_xattn_wv"], "xbv": row(a["L0_xattn_bv"]),
        "xwo": a["L0_xattn_wo"], "xbo": row(a["L0_xattn_bo"]),
        "wr": c(a["L0_ffn_gate_w"].T),
        "wg": c(a["L0_ffn_w_gate"].transpose(1, 0, 2)), "wu": c(a["L0_ffn_w_up"].transpose(1, 0, 2)),
        "wd": c(a["L0_ffn_w_down"].reshape(E, FT, P, D).transpose(2, 0, 1, 3)),
        "ident": np.eye(P, dtype=np.float32),
        "masks": np.stack([hidden, hidden.T], 1),
        "rank": np.broadcast_to(np.arange(E, 0, -1).astype(np.float32), (P, E)),
    }


def kernel(**inputs):
    import concourse.bacc as bacc
    from concourse.bass_utils import run_bass_kernel_spmd

    nc = bacc.Bacc("TRN2", target_bir_lowering=False, num_devices=1)
    arrays, io = {}, {}
    for name, a in _layouts({k: np.asarray(v) for k, v in inputs.items()}).items():
        a = np.ascontiguousarray(a)
        arrays[f"in_{name}"] = a
        io[name] = nc.dram_tensor(f"in_{name}", a.shape, mybir.dt.from_np(a.dtype),
                                  kind="ExternalInput").ap()
    out = nc.dram_tensor("out", [N, D], F32, kind="ExternalOutput").ap()
    decoder_layer(nc, io, out)
    r = run_bass_kernel_spmd(nc, [arrays], core_ids=[0])
    return r.results[0]["out"].reshape(B, T, D)
```

```python
from contextlib import ExitStack

import numpy as np

import concourse.bass as bass
from concourse import mybir

F32 = mybir.dt.float32
BF16 = mybir.dt.bfloat16
F32R = mybir.dt.float32r
ALU = mybir.AluOpType
ACT = mybir.ActivationFunctionType
AX = mybir.AxisListType

B, T, D, H = 8, 256, 128, 16
DK = D // H
S2 = 1601
E, F = 8, 256
N = B * T
P = 128
NT = N // P
TT = T // P
EPS = 1e-5
SCALE = DK ** -0.5
MASKED = -1e30

G = 4
GJ = 2 * G
KT = -(-S2 // P)
LAST = S2 - (KT - 1) * P
CH = 4
CW = [S2 // CH + (i < S2 % CH) for i in range(CH)]
CO = [sum(CW[:i]) for i in range(CH)]
VW = DK + 1

K_PART = [1, 2, 1, 2, 1, 3]
Q_PART = [1, 1, 2, 2, 3, 1]
NPROD = len(K_PART)
PROWS = NPROD * DK
MP = 3
KROWS = MP + PROWS

LOG_SHIFT = 20

CK = 512
NC = N // CK
CT = CK // P


def sems(nc, ctx, names):
    return [ctx.enter_context(nc.semaphore(n)) for n in names.split()]


class Context:

    STORES = NPROD + 1
    LOG_STEPS = 6

    def __init__(self, nc, ctx):
        def sb(name, shape, dt=F32):
            return ctx.enter_context(nc.sbuf_tensor("c_" + name, shape, dt))
        self.wk, self.wv, self.bk, self.bv = sb("wk", [D, D]), sb("wv", [D, D]), sb("bk", [D, 1]), sb("bv", [P, D])
        self.cx = [sb(f"ctx{i}", [D, S2]) for i in range(2)]
        self.keys, self.rest = sb("keys", [D, S2]), sb("rest", [D, S2])
        self.kp = [[sb(f"k{i}_{j}", [D, S2], BF16) for j in range(3)] for i in range(2)]
        self.vb = [sb(f"v{i}", [P, G, KT, 4 * VW]) for i in range(2)]
        self.lw, self.lrest = sb("lw", [B, S2]), sb("lrest", [B, S2])
        self.lp = [sb(f"lp{j}", [B, S2], BF16) for j in range(MP)]
        self.lbias = sb("lbias", [B, 1])
        (self.w_in, self.fw_in, self.ones_set, self.log_steps, self.whole, self.first, self.rested, self.second,
         self.third, self.stored_log, in0, in1, st0, st1) = sems(
            nc, ctx, "c_w_in c_fw_in c_ones_set c_log_steps c_whole c_first c_rested c_second c_third "
                     "c_stored_log c_ctx_in0 c_ctx_in1 c_stored0 c_stored1")
        self.ctx_in, self.stored = [in0, in1], [st0, st1]

    def load(self, sp, io, b, i):
        src = io["ctxT"][:, b * S2:(b + 1) * S2] if isinstance(b, int) else \
            io["ctxT"][:, bass.ds(b * S2, S2)]
        sp.dma_start(self.cx[i][:], src).then_inc(self.ctx_in[i], 16)

    def load_first(self, sp, io):
        for dst, src in ((self.wk, io["xwk"]), (self.bk, io["xbk"]), (self.wv, io["xwv"]),
                         (self.bv, io["xbv"])):
            sp.dma_start(dst[:], src).then_inc(self.w_in, 16)
        for i in range(2):
            self.load(sp, io, i, i)
            sp.sem_inc(self.stored[i], 16 * self.STORES)

    def store(self, sp, scr, b, i, drained, values_drained):
        one = slice(b, b + 1) if isinstance(b, int) else bass.ds(b, 1)
        ready = {1: self.first, 2: self.second, 3: self.third}
        for r in sorted(range(NPROD), key=lambda r: K_PART[r]):
            sp.wait_ge(ready[K_PART[r]], b + 1)
            sp.dma_start(scr["ks"][one, :, MP + DK * r:MP + DK * (r + 1), :, :]
                         .rearrange("o c r n k -> (o c) (r n) k"),
                         self.kp[i][K_PART[r] - 1][:]).then_inc(self.stored[i], 16)
        sp.wait_ge(drained, values_drained)
        sp.dma_start(scr["v"][one].rearrange("o p v -> (o p) v"),
                     self.vb[i][:].rearrange("p g t v -> p (g t v)")).then_inc(self.stored[i], 16)

    def store_log(self, sp, scr):
        sp.wait_ge(self.log_steps, self.LOG_STEPS)
        for j in range(MP):
            for par in range(2):
                sp.dma_start(scr["ks"][:, par, j, :, :],
                             self.lp[j][:].unsqueeze(1).broadcast_to([B, GJ, S2]))\
                  .then_inc(self.stored_log, 16)

    def tensor_keys(self, pe, filled, drained, use, bank, i, half, c):
        if c == 0:
            pe.wait_ge(self.ctx_in[i], half * 16 + 16)
        pe.wait_ge(drained, use - 2)
        pe.matmul(bank[:, 0:CW[c]], self.wk[:], self.cx[i][:, CO[c]:CO[c] + CW[c]],
                  start=True, stop=True).then_inc(filled, 1)

    def tensor_values(self, pe, filled, drained, use, bank, i, c):
        pe.wait_ge(drained, use - 2)
        for n, t in enumerate(range(CT * c, min(CT * (c + 1), KT))):
            m = P if t < KT - 1 else LAST
            mm = pe.matmul(bank[0:m, n * D:(n + 1) * D], self.cx[i][:, t * P:t * P + m], self.wv[:],
                           start=True, stop=True)
        mm.then_inc(filled, 1)

    def vector_keys(self, dve, filled, drained, use, bank, c, b, first):
        if c == 0 and not first:
            dve.wait_ge(self.second, b)
        dve.wait_ge(filled, use + 1)
        dve.tensor_scalar(self.keys[:, CO[c]:CO[c] + CW[c]], bank[:, 0:CW[c]], self.bk[:], None, ALU.add)\
           .then_inc(drained, 1)

    def vector_values(self, dve, filled, drained, use, bank, i, half, c):
        if c == 0:
            dve.wait_ge(self.stored[i], 16 * self.STORES * (half + 1))
        dve.wait_ge(filled, use + 1)
        nt = min(CT, KT - CT * c)
        m = P if c < CH - 1 else LAST
        for g in range(G):
            ins = dve.tensor_tensor(
                self.vb[i][0:m, g, CT * c:CT * c + nt, :]
                .rearrange("p t (h v) -> p t h v", h=4)[:, :, :, 0:DK],
                bank[0:m, 0:nt * D].rearrange("p (t e) -> p t e", e=D)[:, :, 32 * g:32 * g + 32]
                .rearrange("p t (h d) -> p t h d", h=4),
                self.bv[0:m, 32 * g:32 * g + 32].rearrange("p (h d) -> p h d", h=4)
                .unsqueeze(1).broadcast_to([m, nt, 4, DK]), ALU.add)
        ins.then_inc(drained, 1)

    def scalar_first(self, act, i, half, keys_drained, drained):
        act.wait_ge(drained, keys_drained)
        act.wait_ge(self.stored[i], 16 * self.STORES * (half + 1))
        act.copy(self.kp[i][0][:], self.keys[:]).then_inc(self.first, 1)

    def scalar_second(self, act, i, b):
        act.wait_ge(self.rested, b + 1)
        act.copy(self.kp[i][1][:], self.rest[:]).then_inc(self.second, 1)

    def pool_rest(self, pool, i, b, first):
        pool.wait_ge(self.first, b + 1)
        if not first:
            pool.wait_ge(self.third, b)
        pool.tensor_tensor(self.rest[:], self.keys[:], self.kp[i][0][:], ALU.subtract)\
           .then_inc(self.rested, 1)

    def pool_third(self, pool, i, b):
        pool.wait_ge(self.second, b + 1)
        pool.tensor_tensor(self.kp[i][2][:], self.rest[:], self.kp[i][1][:], ALU.subtract)\
           .then_inc(self.third, 1)

    def scalar_log(self, act):
        act.wait_ge(self.fw_in, 16)
        act.wait_ge(self.ones_set, 1)
        act.activation(self.lw[:], self.lw[:], ACT.Ln, bias=self.lbias[:], scale=float(2 ** LOG_SHIFT))\
           .then_inc(self.log_steps, 1)

    def pool_log(self, pool):
        for i in range(2):
            pool.memset(self.vb[i][:], 1.0).then_inc(self.ones_set, 1)
        pool.wait_ge(self.log_steps, 1)
        pool.tensor_scalar(self.lw[:], self.lw[:], -LOG_SHIFT * float(np.log(2.0)), None, ALU.add)\
            .then_inc(self.log_steps, 1)
        pool.wait_ge(self.log_steps, 3)
        pool.tensor_tensor(self.lrest[:], self.lw[:], self.lp[0][:], ALU.subtract).then_inc(self.log_steps, 1)

    def pool_log_third(self, pool):
        pool.wait_ge(self.log_steps, 5)
        pool.tensor_tensor(self.lp[2][:], self.lrest[:], self.lp[1][:], ALU.subtract)\
            .then_inc(self.log_steps, 1)

    def scalar_log_part(self, act, j):
        act.wait_ge(self.log_steps, 2 + 2 * j)
        act.copy(self.lp[j][:], (self.lrest if j else self.lw)[:]).then_inc(self.log_steps, 1)


class Stacks:

    def __init__(self, nc, ctx, tag, kb, qb):
        self.kb, self.qb = kb, qb
        self.stored = sems(nc, ctx, f"{tag}_half_stored0 {tag}_half_stored1")
        self.filled = ctx.enter_context(nc.semaphore(f"{tag}_filled"))
        self.fills = 2 * len(kb)

    def fill(self, pool):
        for k, q in zip(self.kb, self.qb):
            pool.memset(k[:], 1.0).then_inc(self.filled, 1)
            pool.memset(q[:], 0.0).then_inc(self.filled, 1)


def store_parts(sp, operands, half, stored, ready=((None, 0),) * 3):
    o = slice(half * N // 2, (half + 1) * N // 2)
    for which, (sem, value) in enumerate(ready):
        if sem is not None:
            sp.wait_ge(sem, value)
        for dst, part, parts in operands:
            for r in range(NPROD):
                if parts[r] == which + 1:
                    sp.dma_start(dst[:, DK * r:DK * (r + 1), :, o].rearrange("c r n t -> c (r n) t"),
                                 part[which][:, o]).then_inc(stored[half], 16)


class Norm:

    def __init__(self, nc, ctx, tag):
        self.st = ctx.enter_context(nc.sbuf_tensor(tag + "stats", [P, NT, 6], F32))
        self.mv = ctx.enter_context(nc.sbuf_tensor(tag + "meanvar", [P, NT, 2], F32))
        self.rs = ctx.enter_context(nc.sbuf_tensor(tag + "rstd", [P, NT, 2], F32))
        self.eps = ctx.enter_context(nc.sbuf_tensor(tag + "eps", [P, 1], F32))
        self.counted, self.stats, self.rooted, self.ready, self.turned, self.out = sems(
            nc, ctx, " ".join(tag + n for n in "counted_s stats_s rooted_s ready_s turned_s out_s".split()))


def norm_stats(dve, nm, x, b):
    for n in range(TT):
        t = slice(TT * b + n, TT * b + n + 1) if isinstance(b, int) else bass.ds(b * TT + n, 1)
        dve.bn_stats(nm.st[:, t, :].rearrange("p t s -> p (t s)"),
                     x[:, t, :].rearrange("p t d -> p (t d)")).then_inc(nm.counted, 1)


def norm_vector(dve, nm, x, xn):
    dve.memset(nm.eps[:], EPS).then_inc(nm.stats, 1)
    dve.wait_ge(nm.counted, NT)
    for t in range(NT):
        dve.bn_aggr(nm.mv[:, t, :], nm.st[:, t, :]).then_inc(nm.stats, 1)
    dve.wait_ge(nm.rooted, 1)
    dve.reciprocal(nm.rs[:, :, 1], nm.rs[:, :, 0]).then_inc(nm.rooted, 1)
    dve.wait_ge(nm.rooted, 2)
    for t in range(NT):
        dve.tensor_scalar(xn[:, t, :], x[:, t, :], nm.mv[:, t, 0:1], nm.rs[:, t, 1:2],
                          ALU.subtract, ALU.mult).then_inc(nm.ready, 1)


def norm_scalar_root(act, nm):
    act.wait_ge(nm.stats, 1 + NT)
    act.activation(nm.rs[:, :, 0], nm.mv[:, :, 1], ACT.Sqrt, bias=nm.eps[:]).then_inc(nm.rooted, 1)


def norm_scalar_out(act, nm, bank2, xnT, c):
    act.wait_ge(nm.turned, c + 1)
    act.copy(xnT[:, c * CK:(c + 1) * CK], bank2[c % 2]).then_inc(nm.out, 1)


def norm_tensor(pe, nm, xn, ident, bank2, c):
    pe.wait_ge(nm.ready, CT * (c + 1))
    if c >= 2:
        pe.wait_ge(nm.out, c - 1)
    for t in range(CT):
        mm = pe.transpose(bank2[c % 2][:, t * P:(t + 1) * P], xn[:, CT * c + t, :], ident[:])
    mm.then_inc(nm.turned, 1)


def self_projection_stage(nc, io, scr, banks, x, xn, xnT, v_all, bo, U, stacks, operands, ident, identb, context):
    with ExitStack() as ctx:
        def sb(name, shape, dt=F32):
            return ctx.enter_context(nc.sbuf_tensor("p_" + name, shape, dt))
        names = ["q", "q_swap", "k", "k_swap"]
        w = {n: sb("w" + n, [D, D]) for n in names}
        bias = {n: sb("b" + n, [D, 1]) for n in names}
        wv, bv = sb("wv", [D, D]), sb("bv", [P, D])
        rot = {n: sb("rot" + n, [D, T]) for n in names}
        turned = [[sb(f"t{n}{i}", [D, CK]) for i in range(2)] for n in "qk"]
        part = [operands[0][1], operands[1][1]]
        rest = [sb(f"rest{n}", [D, CK]) for n in "qk"]
        nm = Norm(nc, ctx, "p_n_")
        (w_in, x_in, cst_in, proj, drained, whole, first, rest_s, second, third, ones_set) = sems(
            nc, ctx, "p_w_in p_x_in p_cst_in p_proj p_drained p_whole p_first p_rest p_second p_third "
                     "p_ones_set")
        NW = 4 * 3 + 3
        PC = 5
        with nc.Block() as block:

            @block.sync
            def _(sp):
                sp.dma_start(x[:], io["x"].rearrange("(t p) d -> p t d", p=P)).then_inc(x_in, 16)
                sp.dma_start(context.lw[:], io["weights"]).then_inc(context.fw_in, 16)
                sp.dma_start(ident[:], io["ident"]).then_inc(cst_in, 16)
                for n in names:
                    sp.dma_start(w[n][:], io["w_" + n]).then_inc(w_in, 16)
                    sp.dma_start(bias[n][:], io["b_" + n]).then_inc(w_in, 16)
                    sp.dma_start(rot[n][:], io["rot_" + n]).then_inc(w_in, 16)
                sp.dma_start(wv[:], io["swv"]).then_inc(w_in, 16)
                sp.dma_start(bv[:], io["sbv"]).then_inc(w_in, 16)
                sp.dma_start(bo[:], io["sbo"]).then_inc(w_in, 16)
                context.load_first(sp, io)
                store_parts(sp, operands, 0, stacks.stored, [(n, NC) for n in (first, second, third)])

            @block.tensor
            def _(pe):
                pe.wait_ge(cst_in, 16)
                norm_tensor(pe, nm, xn, ident, banks[5:7], 0)
                for c in range(NC):
                    if c + 1 < NC:
                        norm_tensor(pe, nm, xn, ident, banks[5:7], c + 1)
                    if c == 0:
                        pe.wait_ge(w_in, 16 * NW)
                    pe.wait_ge(nm.out, c + 1)
                    for i, n in enumerate(names):
                        if c:
                            pe.wait_ge(drained, PC * (c - 1) + i + 1)
                        pe.matmul(banks[i], w[n][:], xnT[:, c * CK:(c + 1) * CK],
                                  start=True, stop=True).then_inc(proj, 1)
                    if c:
                        pe.wait_ge(drained, PC * c)
                    for t in range(CT):
                        mm = pe.matmul(banks[4][:, t * D:(t + 1) * D],
                                       xnT[:, c * CK + t * P:c * CK + (t + 1) * P], wv[:],
                                       start=True, stop=True)
                    mm.then_inc(proj, 1)

            @block.scalar
            def _(act):
                context.scalar_log(act)
                norm_scalar_root(act, nm)
                norm_scalar_out(act, nm, banks[5:7], xnT, 0)
                for c in range(NC):
                    if c + 1 < NC:
                        norm_scalar_out(act, nm, banks[5:7], xnT, c + 1)
                    o = slice(c * CK, (c + 1) * CK)
                    for i in range(2):
                        act.wait_ge(whole, 2 * c + i + 1)
                        act.copy(part[i][0][:, o], turned[i][0][:]).then_inc(first, 1)
                    if c == 0:
                        context.scalar_log_part(act, 0)
                    for i in range(2):
                        act.wait_ge(rest_s, 2 * c + i + 1)
                        act.copy(part[i][1][:, o], rest[i][:]).then_inc(second, 1)
                    if c == 1:
                        context.scalar_log_part(act, 1)

            @block.gpsimd
            def _(pool):
                pool.memset(context.lbias[:], 1e-20 * 2 ** LOG_SHIFT).then_inc(context.ones_set, 1)
                pool.memset(v_all[:], 1.0).then_inc(ones_set, 1)
                stacks.fill(pool)
                context.pool_log(pool)
                for c in range(NC):
                    for i in range(2):
                        pool.wait_ge(second, 2 * c + i + 1)
                        pool.tensor_tensor(part[i][2][:, c * CK:(c + 1) * CK], rest[i][:],
                                           part[i][1][:, c * CK:(c + 1) * CK], ALU.subtract)\
                            .then_inc(third, 1)
                    if c == 1:
                        context.pool_log_third(pool)

            @block.vector
            def _(dve):
                dve.memset(U, 0.0)
                dve.wait_ge(x_in, 16)
                for b in range(B):
                    norm_stats(dve, nm, x, b)
                norm_vector(dve, nm, x, xn)
                dve.wait_ge(cst_in, 16)
                dve.tensor_copy(identb[:], ident[:])
                dve.wait_ge(w_in, 16 * NW)
                dve.wait_ge(ones_set, 1)
                steps = 0
                for c in range(NC):
                    o = slice(c * CK, (c + 1) * CK)
                    for i in range(2):
                        if c:
                            dve.wait_ge(rest_s, 2 * (c - 1) + i + 1)
                        for s in range(2):
                            n = names[2 * i + s]
                            dve.wait_ge(proj, PC * c + 2 * i + s + 1)
                            dve.scalar_tensor_tensor(
                                out=turned[i][s][:].rearrange("p (b t) -> p b t", t=T),
                                in0=banks[2 * i + s].rearrange("p (b t) -> p b t", t=T),
                                scalar=bias[n][:],
                                in1=rot[n][:].unsqueeze(1).broadcast_to([P, CK // T, T]),
                                op0=ALU.add, op1=ALU.mult).then_inc(drained, 1)
                        dve.wait_ge(drained, PC * c + 2 * i + 2)
                        dve.tensor_tensor(turned[i][0][:], turned[i][0][:], turned[i][1][:], ALU.add)\
                           .then_inc(whole, 1)
                    dve.wait_ge(proj, PC * c + 5)
                    dve.tensor_tensor(
                        v_all[:, CT * c:CT * (c + 1), :, 0:DK],
                        banks[4].rearrange("p (t h d) -> p t h d", t=CT, h=H),
                        bv[:].rearrange("p (h d) -> p h d", h=H).unsqueeze(1)
                        .broadcast_to([P, CT, H, DK]), ALU.add).then_inc(drained, 1)
                    for i in range(2):
                        dve.wait_ge(first, 2 * c + i + 1)
                        if c:
                            dve.wait_ge(third, 2 * (c - 1) + i + 1)
                        dve.tensor_tensor(rest[i][:], turned[i][0][:], part[i][0][:, o], ALU.subtract)\
                           .then_inc(rest_s, 1)


def tensor_sums(pe, filled, evac, drained, use, bank, u, groups, ident):
    pe.wait_ge(evac, groups)
    pe.wait_ge(drained, use - 2)
    for t in range(TT):
        mm = pe.transpose(bank[:, t * P:(t + 1) * P], u[:, t * P:(t + 1) * P], ident[:])
    mm.then_inc(filled, 1)


def tensor_turn(pe, filled, drained, use, last_sums, tiles, bank, y, ident):
    pe.wait_ge(drained, last_sums + 1)
    pe.wait_ge(drained, use - 2)
    for n, t in enumerate(tiles):
        mm = pe.transpose(bank[:, n * P:(n + 1) * P], y[:, t, :], ident[:])
    mm.then_inc(filled, 1)


def tensor_output(pe, filled, drained, use, turned, tiles, bank, yT, wo):
    pe.wait_ge(drained, turned + 1)
    pe.wait_ge(drained, use - 2)
    for n, t in enumerate(tiles):
        mm = pe.matmul(bank[:, n * D:(n + 1) * D], yT[:, t, :], wo[:], start=True, stop=True)
    mm.then_inc(filled, 1)


def vector_sums(dve, filled, normed, drained, use, group, g, bank, rec, y):
    sums = bank[:, 0:TT * P].rearrange("p (q h c) -> p q h c", q=TT, h=4)
    dve.wait_ge(filled, use + 1)
    dve.reciprocal(rec[:], sums[:, :, :, DK]).then_inc(normed, 1)
    dve.wait_ge(normed, group + 1)
    dve.tensor_tensor(y[:, :, 4 * DK * g:4 * DK * (g + 1)].rearrange("p q (h d) -> p q h d", h=4),
                      sums[:, :, :, 0:DK], rec[:].unsqueeze(3).broadcast_to([P, TT, 4, DK]),
                      ALU.mult).then_inc(drained, 1)


def vector_turn(dve, filled, drained, use, tiles, bank, yT):
    dve.wait_ge(filled, use + 1)
    dve.tensor_copy(yT[:, tiles[0]:tiles[-1] + 1, :],
                    bank[:, 0:len(tiles) * P].rearrange("p (t q) -> p t q", q=P)).then_inc(drained, 1)


def vector_output(dve, filled, drained, use, tiles, bank, x, b):
    n = len(tiles)
    part = x[:, TT * b + tiles[0]:TT * b + tiles[0] + n, :] if isinstance(b, int) else \
        x[:, bass.ds(b * TT + tiles[0], n), :]
    dve.wait_ge(filled, use + 1)
    dve.tensor_tensor(part, bank[:, 0:n * D].rearrange("p (t d) -> p t d", t=n), part, ALU.add)\
       .then_inc(drained, 1)


SU = 2 * G
SA = 12
SRING = SA + 1 + G + 2 + 2 * CH


def self_banks():
    return [(par, 1, 2 * i, 2) for i in range(G) for par in range(2)] + \
           [(par, 0, 4 * i, 4) for i in range(2) for par in range(2)]


def self_ring(u, first, last):
    jobs = []
    if u in (0, 1):
        jobs += [("context keys", c) for c in (2 * u, 2 * u + 1)]
    if u == 1 and not first:
        jobs.append(("sums", G - 1))
    if u in (2, 3) and not first:
        jobs.append((("turn", "output")[u - 2], range(TT)))
    if u in (3, 5, 7):
        jobs.append(("sums", (u - 3) // 2))
    if not last and 2 <= u <= 4:
        jobs += [("scores", a) for a in range(4 * (u - 2), 4 * (u - 1))]
    if u >= 5:
        jobs += [("context values", c) for c in ([0], [1, 2], [3])[u - 5]]
    if not last and u == 5:
        jobs.append(("maxima", 0))
    return jobs


def over_pairs(eng, batch):
    batch(0, 0, 0, True, False)
    with eng.Fori(0, B // 2 - 1) as i:
        batch(i * 2 + 1, 1, i, False, False)
        batch(i * 2 + 2, 0, i + 1, False, False)
    batch(B - 1, 1, B // 2 - 1, False, True)


def self_attention_stage(nc, io, scr, ring, S4, U, x, v_all, bo, stacks, operands, next_stacks, ident, identb, context, next_norm):
    with ExitStack() as ctx:
        def sb(name, shape, dt=F32):
            return ctx.enter_context(nc.sbuf_tensor("s_" + name, shape, dt))
        kb, qb = stacks.kb, stacks.qb
        vv = [sb(f"v{i}", [P, TT, H, VW]) for i in range(2)]
        mask32 = sb("mask32", [P, 2, P])
        mask = sb("mask", [P, 2, 4, P], BF16)
        wo = sb("wo", [D, D])
        probs = sb("probs", [P, 4, 2, 2 * T])
        nmax, nrest, zero = (sb(n, [P, 2, 2 * GJ]) for n in ("nmax", "nrest", "zero"))
        mparts = sb("mparts", [P, 2, MP, 2 * GJ], BF16)
        mrows = sb("mrows", [4 * MP * GJ, P], BF16)
        ub = [sb(f"u{i}", [P, T]) for i in range(2)]
        rec = [sb(f"rec{i}", [P, TT, 4]) for i in range(2)]
        y = sb("y", [P, TT, D])
        yT = sb("yT", [D, TT, P])
        (w_in, wo_in, ones_in, biased, set_up, filled, drained, scored, exped, valued, evac, normed, msplit, m0, m1) = sems(
            nc, ctx, "s_w_in s_wo_in s_ones_in s_biased s_set_up s_ring_filled s_ring_drained s_scored s_exped s_valued s_evac "
                     "s_normed s_msplit s_max_in0 s_max_in1")
        m_in = [m0, m1]
        load_in = sems(nc, ctx, "s_load_in0 s_load_in1")
        values_in = sems(nc, ctx, "s_values_in0 s_values_in1")
        S = S4.rearrange("p (u c w) -> p u c w", u=2, c=2)
        MC = 2 * GJ * MP
        NL = 3

        def base(b, first):
            return SA + 1 if first else (b - 1) * SRING + SA + 1 + SRING - 3

        AFTER = base(B - 1, False) + SRING - SA - 1

        with nc.Block() as block:

            @block.sync
            def _(sp):
                sp.dma_start(mask32[:], io["masks"]).then_inc(w_in, 16)

                def load(b, s):
                    toks = slice(b * T, (b + 1) * T) if isinstance(b, int) else bass.ds(b * T, T)
                    sp.dma_start(kb[s][0:2 * PROWS, :, :],
                                 scr["ks_self"][:, :, :, toks].rearrange("c r n t -> (c r) n t"))\
                      .then_inc(load_in[s], 16)
                    for par in range(2):
                        sp.dma_start(qb[s][PROWS * par:PROWS * (par + 1), par, :, :],
                                     scr["qs_self"][par, :, :, toks]).then_inc(load_in[s], 16)
                    vsrc = v_all[:, TT * b:TT * (b + 1)] if isinstance(b, int) else \
                        v_all[:, bass.ds(b * TT, TT)]
                    sp.dma_start(vv[s][:].rearrange("p t h v -> p (t h v)"),
                                 vsrc.rearrange("p t h v -> p (t h v)")).then_inc(values_in[s], 16)

                def maxima_rows(use, s):
                    sp.wait_ge(drained, use + 1)
                    for par in range(2):
                        row = 2 * PROWS + MP * par
                        sp.dma_start(qb[s][row:row + MP, par, :, :].rearrange("p j q -> p (j q)"),
                                     mrows[MC * par:MC * (par + 1), :]).then_inc(m_in[s], 16)

                sp.wait_ge(stacks.stored[0], 16 * 2 * NPROD)
                load(0, 0)
                store_parts(sp, operands, 1, stacks.stored)
                load(1, 1)
                sp.dma_start(wo[:], io["swo"]).then_inc(wo_in, 16)
                maxima_rows(SA, 0)
                sp.wait_ge(stacks.stored[1], 16 * 2 * NPROD)
                sp.wait_ge(next_stacks.filled, next_stacks.fills)
                for q in next_stacks.qb:
                    for par in range(2):
                        sp.dma_start(q[KROWS * par:KROWS * par + MP, par, :, :]
                                     .rearrange("p j q -> p (j q)"), next_stacks.kb[0][0:MP, 0, 0:2 * T])\
                          .then_inc(ones_in, 16)

                def batch(b, s, half, first, last):
                    if not first and not last:
                        sp.wait_ge(valued, SU * b)
                        load(b + 1, 1 - s)
                        context.load(sp, io, b + 1, 1 - s)
                    if not first:
                        context.store(sp, scr, b - 1, 1 - s, drained, base(b, False))
                    if last:
                        context.store_log(sp, scr)
                    n = base(b, first)
                    for u in range(SU):
                        for kind, a in self_ring(u, first, last):
                            if kind == "maxima":
                                maxima_rows(n, 1 - s)
                            n = n + 1

                over_pairs(sp, batch)
                context.store(sp, scr, B - 1, 1, drained, AFTER)
                sp.wait_ge(ones_in, 16 * 2 * G)

            @block.tensor
            def _(pe):
                pe.wait_ge(set_up, 3)

                def scores_rows(use, r, s, a, wait):
                    par, qt, gj, cnt = self_banks()[a]
                    if wait:
                        pe.wait_ge(drained, use - 2)
                    keys = (qt + 1) * P
                    rows = slice(0, 2 * PROWS)
                    for n in range(cnt):
                        pe.matmul(ring[r][:, n * keys:(n + 1) * keys],
                                  qb[s][rows, par, gj + n, qt * P:(qt + 1) * P],
                                  kb[s][rows, gj + n, 0:keys],
                                  start=(n == 0), stop=False, skip_group_check=True)
                    out = ring[r][:].rearrange("p (n k) -> p n k", n=cnt)[:, :, qt * P:keys]
                    pe.matmul(out, identb[:], mask[:, 0, 0:cnt, :], start=False, stop=True,
                              skip_group_check=True).then_inc(filled, 1)

                def turn_maxima(use, r, nsplit):
                    pe.wait_ge(msplit, nsplit)
                    pe.wait_ge(drained, use - 2)
                    pe.transpose(ring[r][:].bitcast(BF16)[0:2 * MC, 0:P],
                                 mparts[:].rearrange("p c m n -> p (c m n)"), identb[:])\
                      .then_inc(filled, 1)

                def values(n, u, s, gn):
                    g, kt = u // 2, u % 2
                    pe.wait_ge(exped, n + 1)
                    if kt == 0 and gn is not None:
                        pe.wait_ge(evac, gn)
                    for par in range(2):
                        for j in range(2):
                            t, w = 2 * j + par, T - kt * P
                            mm = pe.matmul(U[32 * t:32 * t + VW, kt * P:T],
                                           vv[s][:, kt, 4 * g + t, :],
                                           probs[:, u % 4, j, par * w:(par + 1) * w],
                                           start=(kt == 0), stop=(kt == 1), skip_group_check=True)
                    mm.then_inc(valued, 1)

                pe.wait_ge(load_in[0], 16 * NL)
                for a in range(SA):
                    scores_rows(a, a % 3, 0, a, a >= 3)
                turn_maxima(SA, SA % 3, 4)

                def batch(b, s, half, first, last):
                    n0, rb = b * SU, (SA + 1 if first else SA + 1 + SRING - 3)
                    use, k = base(b, first), 0
                    for u in range(SU):
                        g, kt = u // 2, u % 2
                        if u == 0:
                            pe.wait_ge(load_in[s], (half + 1) * 16 * NL)
                            pe.wait_ge(m_in[s], (half + 1) * 32)
                        if not (first and u < 2):
                            pe.wait_ge(exped, n0 + u - 1)
                        w = T - kt * P
                        rows = slice(0, 2 * (PROWS + MP))
                        for j in range(2):
                            pe.matmul(S[:, u % 2, j, 0:2 * w],
                                      kb[s][rows, 2 * g + j, kt * P:(kt + 1) * P],
                                      qb[s][rows, :, 2 * g + j, kt * P:T],
                                      start=True, stop=False, skip_group_check=True)
                            mm = pe.matmul(
                                S[:, u % 2, j, 0:2 * w].rearrange("p (c q) -> p c q", c=2)[:, :, 0:P],
                                identb[:], mask[:, 1, 0:2, :], start=False, stop=True,
                                skip_group_check=True)
                        mm.then_inc(scored, 1)
                        if u == 0 and not first:
                            values(n0 - 1, SU - 1, 1 - s, None)
                        for kind, a in self_ring(u, first, last):
                            r = (rb + k) % 3
                            if kind == "scores":
                                if a == 0:
                                    pe.wait_ge(load_in[1 - s], (half + (1 + s)) * 16 * NL)
                                scores_rows(use + k, r, 1 - s, a, True)
                            elif kind == "maxima":
                                turn_maxima(use + k, r, (b + 2) * 4)
                            elif kind == "context keys":
                                context.tensor_keys(pe, filled, drained, use + k, ring[r], s, half, a)
                            elif kind == "context values":
                                context.tensor_values(pe, filled, drained, use + k, ring[r], s, a)
                            elif kind == "sums":
                                if u == 1:
                                    last_sums = use + k
                                tensor_sums(pe, filled, evac, drained, use + k, ring[r], ub[a % 2],
                                            b * G + a + 1 - (G if u == 1 else 0), ident)
                            elif kind == "turn":
                                turned = use + k
                                tensor_turn(pe, filled, drained, use + k, last_sums, a, ring[r], y, ident)
                            else:
                                tensor_output(pe, filled, drained, use + k, turned, a, ring[r],
                                              yT, wo)
                            k += 1
                        if u == 1:
                            pe.wait_ge(values_in[s], (half + 1) * 16)
                        if u > 0:
                            values(n0 + u - 1, u - 1, s, None if first and u == 1 else b * G + (u - 1) // 2)

                pe.wait_ge(wo_in, 16)
                over_pairs(pe, batch)
                values(B * SU - 1, SU - 1, 1, None)
                tensor_sums(pe, filled, evac, drained, AFTER, ring[AFTER % 3],
                            ub[(G - 1) % 2], B * G, ident)
                n = AFTER + 1
                tensor_turn(pe, filled, drained, n, AFTER, range(TT), ring[n % 3], y, ident)
                tensor_output(pe, filled, drained, n + 1, n, range(TT), ring[(n + 1) % 3], yT, wo)

            @block.scalar
            def _(act):
                def evacuate(group, gn, wait):
                    act.wait_ge(valued, gn * 2 + 2)
                    if wait:
                        act.wait_ge(normed, gn - 1)
                    act.copy(ub[group % 2][:], U[:, 0:T]).then_inc(evac, 1)

                def batch(b, s, half, first, last):
                    for u in range(SU):
                        n = b * SU + u
                        act.wait_ge(scored, n + 1)
                        if not (first and u < 4):
                            act.wait_ge(valued, n - 3)
                        w = 2 * (T - (u % 2) * P)
                        act.activation(probs[:, u % 4, :, 0:w], S[:, u % 2, :, 0:w], ACT.Exp)\
                           .then_inc(exped, 1)
                        if u % 2 == 0 and not (first and u == 0):
                            group = u // 2 - 1
                            evacuate(group % G, b * G + group, not (first and u < 6))
                        if u == 2:
                            context.scalar_first(act, s, half, base(b, first) + (4 if first else 5), drained)
                        if u == 4:
                            context.scalar_second(act, s, b)

                over_pairs(act, batch)
                evacuate(G - 1, B * G - 1, True)

            @block.gpsimd
            def _(pool):
                def split(b, use):
                    pool.wait_ge(drained, use)
                    pool.tensor_tensor(mparts[:, :, 0, :], nmax[:], zero[:], ALU.add).then_inc(msplit, 1)
                    pool.wait_ge(msplit, b * 4 + 1)
                    pool.tensor_tensor(nrest[:], nmax[:], mparts[:, :, 0, :], ALU.subtract)\
                        .then_inc(msplit, 1)
                    pool.wait_ge(msplit, b * 4 + 2)
                    pool.tensor_tensor(mparts[:, :, 1, :], nrest[:], zero[:], ALU.add).then_inc(msplit, 1)
                    pool.wait_ge(msplit, b * 4 + 3)
                    pool.tensor_tensor(mparts[:, :, 2, :], nrest[:], mparts[:, :, 1, :], ALU.subtract)\
                        .then_inc(msplit, 1)

                pool.memset(zero[:], 0.0).then_inc(set_up, 1)
                pool.tensor_tensor(x[:], x[:], bo[:].unsqueeze(1).broadcast_to([P, NT, D]), ALU.add)\
                    .then_inc(biased, 1)
                pool.wait_ge(set_up, 3)
                split(0, SA)
                for half in range(2):
                    pool.wait_ge(stacks.stored[half], 16 * 2 * NPROD)
                next_stacks.fill(pool)

                def batch(b, s, half, first, last):
                    context.pool_rest(pool, s, b, first)
                    n = base(b, first)
                    for u in range(SU):
                        for kind, a in self_ring(u, first, last):
                            n = n + 1
                            if kind == "scores" and a == SA - 1:
                                split(b + 1, n)
                    context.pool_third(pool, s, b)

                over_pairs(pool, batch)

            @block.vector
            def _(dve):
                dve.wait_ge(w_in, 16)
                for i in range(2):
                    dve.tensor_copy(mask[:, i, :, :], mask32[:, i, :].unsqueeze(1)
                                    .broadcast_to([P, 4, P])).then_inc(set_up, 1)

                def row_max(use, r, a):
                    par, qt, gj, cnt = self_banks()[a]
                    dve.wait_ge(filled, use + 1)
                    out = nmax[:, par, :].rearrange("p (n q) -> p n q", q=TT)[:, gj:gj + cnt, qt]
                    dve.tensor_reduce(out, ring[r][:].rearrange("p (n k) -> p n k", n=cnt), AX.X,
                                      ALU.max, negate=True).then_inc(drained, 1)

                def maxima_out(use, r, s, half, wait):
                    dve.wait_ge(filled, use + 1)
                    if wait:
                        dve.wait_ge(m_in[s], (half + 1) * 32)
                    dve.tensor_copy(mrows[:], ring[r][:].bitcast(BF16)[0:2 * MC, 0:P])\
                       .then_inc(drained, 1)

                for a in range(SA):
                    row_max(a, a % 3, a)
                maxima_out(SA, SA % 3, 0, 0, False)

                def batch(b, s, half, first, last):
                    use, rb, k = base(b, first), (SA + 1 if first else SA + 1 + SRING - 3), 0
                    for u in range(SU):
                        for kind, a in self_ring(u, first, last):
                            r = (rb + k) % 3
                            if kind == "scores":
                                row_max(use + k, r, a)
                            elif kind == "maxima":
                                maxima_out(use + k, r, s, half, True)
                            elif kind == "context keys":
                                context.vector_keys(dve, filled, drained, use + k, ring[r], a, b, first)
                            elif kind == "context values":
                                context.vector_values(dve, filled, drained, use + k, ring[r], s, half, a)
                            elif kind == "sums":
                                vector_sums(dve, filled, normed, drained, use + k,
                                            b * G + a - (G if u == 1 else 0), a, ring[r], rec[a % 2], y)
                            elif kind == "turn":
                                vector_turn(dve, filled, drained, use + k, a, ring[r], yT)
                            else:
                                vector_output(dve, filled, drained, use + k, a, ring[r], x, b - 1)
                                done = use + k + 1
                            k += 1
                        if u == 6 and not first:
                            dve.wait_ge(drained, done)
                            norm_stats(dve, next_norm, x, b - 1)

                dve.wait_ge(biased, 1)
                for half in range(2):
                    dve.wait_ge(stacks.stored[half], 16 * 2 * NPROD)
                over_pairs(dve, batch)
                vector_sums(dve, filled, normed, drained, AFTER, B * G - 1, G - 1, ring[AFTER % 3],
                            rec[(G - 1) % 2], y)
                n = AFTER + 1
                vector_turn(dve, filled, drained, n, range(TT), ring[n % 3], yT)
                vector_output(dve, filled, drained, n + 1, range(TT), ring[(n + 1) % 3], x, B - 1)
                dve.wait_ge(drained, n + 2)
                norm_stats(dve, next_norm, x, B - 1)


def query_stage(nc, io, scr, banks, x, xn, xnT, stacks, operands, ident, nm):
    with ExitStack() as ctx:
        def sb(name, shape, dt=F32):
            return ctx.enter_context(nc.sbuf_tensor("q_" + name, shape, dt))
        w, bias, sbias, bo = sb("w", [D, D]), sb("b", [D, 1]), sb("sb", [D, 1]), sb("bo", [P, D])
        whole = sb("whole", [D, N])
        part = operands[0][1]
        rest = [sb(f"rest{i}", [D, CK]) for i in range(NC)]

        def piece(c):
            return slice(c * CK, (c + 1) * CK)

        (w_in, scaled, proj, first, whole_s, rest_s, second, third, biased) = sems(
            nc, ctx, "q_w_in q_scaled q_proj q_first q_whole q_rest q_second q_third q_biased")
        with nc.Block() as block:

            @block.sync
            def _(sp):
                for dst, src in ((w, io["xwq"]), (bias, io["xbq"]), (bo, io["xbo"])):
                    sp.dma_start(dst[:], src).then_inc(w_in, 16)
                store_parts(sp, operands, 0, stacks.stored, [(n, NC // 2) for n in (first, second, third)])

            @block.tensor
            def _(pe):
                norm_tensor(pe, nm, xn, ident, banks[5:7], 0)
                for c in range(NC):
                    if c + 1 < NC:
                        norm_tensor(pe, nm, xn, ident, banks[5:7], c + 1)
                    if c == 0:
                        pe.wait_ge(w_in, 48)
                    pe.wait_ge(nm.out, c + 1)
                    pe.matmul(banks[c], w[:], xnT[:, c * CK:(c + 1) * CK],
                              start=True, stop=True).then_inc(proj, 1)

            @block.scalar
            def _(act):
                norm_scalar_root(act, nm)
                norm_scalar_out(act, nm, banks[5:7], xnT, 0)
                for c in range(NC + 1):
                    if c + 1 < NC:
                        norm_scalar_out(act, nm, banks[5:7], xnT, c + 1)
                    if c < NC:
                        act.wait_ge(whole_s, c + 1)
                        act.copy(part[0][:, piece(c)], whole[:, piece(c)]).then_inc(first, 1)
                    if c > 0:
                        act.wait_ge(rest_s, c)
                        act.copy(part[1][:, piece(c - 1)], rest[c - 1][:]).then_inc(second, 1)

            @block.gpsimd
            def _(pool):
                pool.wait_ge(nm.ready, NT)
                pool.wait_ge(w_in, 48)
                pool.tensor_tensor(x[:], x[:], bo[:].unsqueeze(1).broadcast_to([P, NT, D]), ALU.add)\
                    .then_inc(biased, 1)

            @block.vector
            def _(dve):
                norm_vector(dve, nm, x, xn)
                dve.wait_ge(w_in, 48)
                dve.tensor_scalar(sbias[:], bias[:], SCALE, None, ALU.mult).then_inc(scaled, 1)
                dve.wait_ge(scaled, 1)
                for c in range(NC + 2):
                    if c < NC:
                        dve.wait_ge(proj, c + 1)
                        dve.tensor_scalar(whole[:, piece(c)], banks[c], SCALE, sbias[:], ALU.mult, ALU.add)\
                           .then_inc(whole_s, 1)
                    if 0 < c <= NC:
                        dve.wait_ge(first, c)
                        dve.tensor_tensor(rest[c - 1][:], whole[:, piece(c - 1)],
                                          part[0][:, piece(c - 1)], ALU.subtract).then_inc(rest_s, 1)
                    if c > 1:
                        dve.wait_ge(second, c - 1)
                        dve.tensor_tensor(part[2][:, piece(c - 2)], rest[c - 2][:],
                                          part[1][:, piece(c - 2)], ALU.subtract).then_inc(third, 1)


XA = 2 * 2 * TT * CH
NG = B * G
EARLY = 8


def cross_banks():
    return [(j, qt, c, par) for j in range(2) for qt in range(TT) for c in range(CH) for par in range(2)]


def first_scores(tile):
    one, total = EARLY + 3 * KT, (G + 1) * XA
    return EARLY + 3 * tile if tile <= KT else one + (total - one) * (tile - KT) // ((G - 1) * KT)


def cross_ring(g, kt, first, last):
    jobs = []
    if first:
        jobs += [("scores", (n % XA, 1 + n // XA - g))
                 for n in range(first_scores(g * KT + kt), first_scores(g * KT + kt + 1))]
    elif not (last and g >= G - 2):
        jobs += [("scores", (a, 2)) for a in range(XA * kt // KT, XA * (kt + 1) // KT)]
    if kt == (10 - 2 * g if first else 9) and not (last and g == G - 1):
        jobs.append(("maxima", 0))
    if kt == 3 and not (first and g == 0):
        jobs.append(("sums", 0))
    if kt in (5, 7) and g == 0 and not first:
        jobs.append((("turn", "output")[(kt - 5) // 2], range(TT)))
    return jobs


def cross_early():
    return range(EARLY)


def cross_uses(first, last):
    return sum(len(cross_ring(g, kt, first, last)) for g in range(G) for kt in range(KT))


def over_batches(eng, batch):
    batch(0, True, False)
    with eng.Fori(1, B - 1) as b:
        batch(b, False, False)
    batch(B - 1, False, True)


def cross_attention_stage(nc, io, scr, ring, S4, U, x, stacks, operands, ident, identb, context, next_norm,
                          experts):
    with ExitStack() as ctx:
        def sb(name, shape, dt=F32):
            return ctx.enter_context(nc.sbuf_tensor("x_" + name, shape, dt))
        kb, qb = stacks.kb, stacks.qb
        vv = [sb(f"v{i}", [P, KT, 4, VW]) for i in range(G)]
        wo = sb("wo", [D, D])
        probs = sb("probs", [P, 4, 2, 2 * T])
        pmax = sb("pmax", [P, 2, 2 * TT, CH])
        nmax, nrest, zero = (sb(n, [P, 2, 2 * TT]) for n in ("nmax", "nrest", "zero"))
        mparts = sb("mparts", [P, 2, MP, 2 * TT], BF16)
        mrows = sb("mrows", [4 * MP * TT, P], BF16)
        ub = [sb(f"u{i}", [P, T]) for i in range(2)]
        rec = [sb(f"rec{i}", [P, TT, 4]) for i in range(2)]
        y = sb("y", [P, TT, D])
        yT = sb("yT", [D, TT, P])
        (w_in, set_up, filled, drained, maxed, scored, exped, valued, evac, normed, msplit) = sems(
            nc, ctx, "x_w_in x_set_up x_ring_filled x_ring_drained x_maxed x_scored x_exped x_valued "
                     "x_evac x_normed x_msplit")
        m_in = sems(nc, ctx, "x_max_in0 x_max_in1 x_max_in2 x_max_in3")
        load_in = sems(nc, ctx, "x_load_in0 x_load_in1 x_load_in2 x_load_in3")
        S = S4.rearrange("p (u c w) -> p u c w", u=2, c=2)
        MC = 2 * TT * MP
        NL = 4
        UNITS = G * KT

        PRO = XA + 1 + EARLY
        U0, UM, UL = cross_uses(True, False), cross_uses(False, False), cross_uses(False, True)
        assert UM % 3 == 0

        def base(b, first):
            return PRO if first else (b - 1) * UM + PRO + U0

        def start_bank(first):
            return PRO if first else PRO + U0

        AFTER = PRO + U0 + (B - 2) * UM + UL

        with nc.Block() as block:

            @block.sync
            def _(sp):
                for i in range(2):
                    sp.wait_ge(context.stored[i], 16 * context.STORES * (B // 2 + 1))
                sp.wait_ge(context.stored_log, 16 * 2 * MP)

                def load(b, g):
                    one = slice(b, b + 1) if isinstance(b, int) else bass.ds(b, 1)
                    toks = slice(b * T, (b + 1) * T) if isinstance(b, int) else bass.ds(b * T, T)
                    sp.dma_start(kb[g][0:2 * KROWS, :, :],
                                 scr["ks"][one, :, :, 2 * g:2 * g + 2, :]
                                 .rearrange("o c r j k -> (o c r) j k")).then_inc(load_in[g], 16)
                    for par in range(2):
                        sp.dma_start(qb[g][KROWS * par + MP:KROWS * (par + 1), par, :, :],
                                     scr["qs"][par, :, 2 * g:2 * g + 2, toks])\
                          .then_inc(load_in[g], 16)
                    sp.dma_start(vv[g][:].rearrange("p t h v -> p (t h v)"),
                                 scr["v"][one, :, g * KT * 4 * VW:(g + 1) * KT * 4 * VW]
                                 .rearrange("o p v -> (o p) v")).then_inc(load_in[g], 16)

                def maxima_rows(use, g):
                    sp.wait_ge(drained, use + 1)
                    for par in range(2):
                        row = 2 * KROWS + MP * par
                        sp.dma_start(qb[g][row:row + MP, par, :, :].rearrange("p j q -> p (j q)"),
                                     mrows[MC * par:MC * (par + 1), :]).then_inc(m_in[g], 16)

                sp.wait_ge(stacks.stored[0], 16 * NPROD)
                for g in range(G):
                    load(0, g)
                store_parts(sp, operands, 1, stacks.stored)
                sp.dma_start(wo[:], io["xwo"]).then_inc(w_in, 16)
                maxima_rows(XA, 0)
                experts.load(sp, io)
                sp.wait_ge(stacks.stored[1], 16 * NPROD)

                def batch(b, first, last):
                    n = base(b, first)
                    for g in range(G):
                        if not (first and g == 0) and not (last and g > 0):
                            sp.wait_ge(valued, b * UNITS + g * KT)
                            load(b if g == 0 else b + 1, (g - 1) % G)
                        for kt in range(KT):
                            for kind, a in cross_ring(g, kt, first, last):
                                if kind == "maxima":
                                    maxima_rows(n, (g + 1) % G)
                                n = n + 1

                over_batches(sp, batch)

            @block.tensor
            def _(pe):
                def scores_rows(use, r, g, a, wait):
                    j, qt, c, par = cross_banks()[a]
                    if wait:
                        pe.wait_ge(drained, use - 2)
                    rows = slice(0, 2 * KROWS)
                    pe.matmul(ring[r][:, 0:CW[c]], qb[g][rows, par, j, qt * P:(qt + 1) * P],
                              kb[g][rows, j, CO[c]:CO[c] + CW[c]], start=True, stop=True)\
                      .then_inc(filled, 1)

                def turn_maxima(use, r, groups):
                    pe.wait_ge(msplit, groups * 4)
                    pe.wait_ge(drained, use - 2)
                    pe.transpose(ring[r][:].bitcast(BF16)[0:2 * MC, 0:P],
                                 mparts[:].rearrange("p c m n -> p (c m n)"), identb[:])\
                      .then_inc(filled, 1)

                def values(n, g, kt, groups):
                    pe.wait_ge(exped, n + 1)
                    if kt == 0 and groups is not None:
                        pe.wait_ge(evac, groups)
                    m = P if kt < KT - 1 else LAST
                    for par in range(2):
                        for j in range(2):
                            t = 2 * j + par
                            mm = pe.matmul(U[32 * t:32 * t + VW, 0:T], vv[g][0:m, kt, t, :],
                                           probs[0:m, (g * KT + kt) % 4, j, par * T:(par + 1) * T],
                                           start=(kt == 0), stop=(kt == KT - 1), skip_group_check=True)
                    mm.then_inc(valued, 1)

                pe.wait_ge(load_in[0], 16 * NL)
                for a in range(XA):
                    scores_rows(a, a % 3, 0, a, a >= 3)
                turn_maxima(XA, XA % 3, 1)
                pe.wait_ge(load_in[1], 16 * NL)
                for a in cross_early():
                    scores_rows(XA + 1 + a, (XA + 1 + a) % 3, 1, a, True)

                def batch(b, first, last):
                    use, k = base(b, first), 0
                    for g in range(G):
                        pe.wait_ge(m_in[g], (b + 1) * 32)
                        for kt in range(KT):
                            u = g * KT + kt
                            if not (first and u < 2):
                                pe.wait_ge(exped, b * UNITS + u - 1)
                            m = P if kt < KT - 1 else LAST
                            rows = slice(0, 2 * (KROWS + MP))
                            for j in range(2):
                                mm = pe.matmul(S[0:m, u % 2, j, :], kb[g][rows, j, kt * P:kt * P + m],
                                               qb[g][rows, :, j, :], start=True, stop=True)
                            mm.then_inc(scored, 1)
                            jobs = cross_ring(g, kt, first, last)
                            for kind, a in jobs:
                                if kind != "scores":
                                    break
                                a, ahead = a
                                if a == 0:
                                    pe.wait_ge(load_in[(g + ahead) % G],
                                               (b + 1 + (g + ahead) // G) * (16 * NL))
                                scores_rows(use + k, (start_bank(first) + k) % 3, (g + ahead) % G, a, True)
                                k += 1
                            if u > 0:
                                pg, pk = divmod(u - 1, KT)
                                values(b * UNITS + u - 1, pg, pk, None if first and pg == 0 else b * G + pg)
                            elif not first:
                                values(b * UNITS - 1, G - 1, KT - 1, None)
                            for kind, a in jobs:
                                r = (start_bank(first) + k) % 3
                                if kind == "scores":
                                    continue
                                elif kind == "maxima":
                                    turn_maxima(use + k, r, b * G + g + 2)
                                elif kind == "sums":
                                    last_sums = use + k
                                    tensor_sums(pe, filled, evac, drained, use + k, ring[r],
                                                ub[(g - 1) % 2], b * G + g, ident)
                                elif kind == "turn":
                                    turned = use + k
                                    tensor_turn(pe, filled, drained, use + k, last_sums, a, ring[r], y,
                                                ident)
                                else:
                                    tensor_output(pe, filled, drained, use + k, turned, a, ring[r],
                                                  yT, wo)
                                k += 1

                pe.wait_ge(w_in, 16)
                over_batches(pe, batch)
                values(B * UNITS - 1, G - 1, KT - 1, None)
                tensor_sums(pe, filled, evac, drained, AFTER, ring[AFTER % 3],
                            ub[(G - 1) % 2], NG, ident)
                n = AFTER + 1
                tensor_turn(pe, filled, drained, n, AFTER, range(TT), ring[n % 3], y, ident)
                tensor_output(pe, filled, drained, n + 1, n, range(TT), ring[(n + 1) % 3], yT, wo)

            @block.scalar
            def _(act):
                def evacuate(g, units, groups):
                    act.wait_ge(valued, units)
                    if groups is not None:
                        act.wait_ge(normed, groups)
                    act.copy(ub[g % 2][:], U[:, 0:T]).then_inc(evac, 1)

                def batch(b, first, last):
                    for u in range(UNITS):
                        g, kt = divmod(u, KT)
                        m = P if kt < KT - 1 else LAST
                        act.wait_ge(scored, b * UNITS + u + 1)
                        if not (first and u < 4):
                            act.wait_ge(valued, b * UNITS + u - 3)
                        act.activation(probs[0:m, u % 4, :, :], S[0:m, u % 2, :, :], ACT.Exp)\
                           .then_inc(exped, 1)
                        if kt == 0 and not (first and g == 0):
                            evacuate((g - 1) % G, b * UNITS + u, None if first and g < 3 else b * G + g - 2)

                over_batches(act, batch)
                evacuate(G - 1, B * UNITS, NG - 2)

            @block.gpsimd
            def _(pool):
                def split(groups):
                    pool.wait_ge(maxed, groups + 1)
                    pool.tensor_tensor(mparts[:, :, 0, :], nmax[:], zero[:], ALU.add).then_inc(msplit, 1)
                    pool.wait_ge(msplit, groups * 4 + 1)
                    pool.tensor_tensor(nrest[:], nmax[:], mparts[:, :, 0, :], ALU.subtract)\
                        .then_inc(msplit, 1)
                    pool.wait_ge(msplit, groups * 4 + 2)
                    pool.tensor_tensor(mparts[:, :, 1, :], nrest[:], zero[:], ALU.add).then_inc(msplit, 1)
                    pool.wait_ge(msplit, groups * 4 + 3)
                    pool.tensor_tensor(mparts[:, :, 2, :], nrest[:], mparts[:, :, 1, :], ALU.subtract)\
                        .then_inc(msplit, 1)

                pool.memset(zero[:], 0.0).then_inc(set_up, 1)
                pool.wait_ge(set_up, 1)
                split(0)
                split(1)
                with pool.Fori(2, NG) as group:
                    split(group)

            @block.vector
            def _(dve):
                def row_max(use, r, a, groups):
                    j, qt, c, par = cross_banks()[a]
                    if a == 0 and groups is not None:
                        dve.wait_ge(maxed, groups)
                    dve.wait_ge(filled, use + 1)
                    dve.tensor_reduce(pmax[:, par, 2 * j + qt, c:c + 1], ring[r][:, 0:CW[c]], AX.X,
                                      ALU.max).then_inc(drained, 1)
                    if a == XA - 1:
                        dve.wait_ge(drained, use + 1)
                        dve.tensor_reduce(nmax[:], pmax[:], AX.X, ALU.max, negate=True)\
                           .then_inc(maxed, 1)

                def maxima_out(use, r, last_slot, loads):
                    dve.wait_ge(filled, use + 1)
                    if loads is not None:
                        dve.wait_ge(m_in[last_slot], loads * 32)
                    dve.tensor_copy(mrows[:], ring[r][:].bitcast(BF16)[0:2 * MC, 0:P])\
                       .then_inc(drained, 1)

                for a in range(XA):
                    row_max(a, a % 3, a, None)
                maxima_out(XA, XA % 3, 0, None)
                for a in cross_early():
                    row_max(XA + 1 + a, (XA + 1 + a) % 3, a, 1)

                def batch(b, first, last):
                    use, k = base(b, first), 0
                    for g in range(G):
                        for kt in range(KT):
                            for kind, a in cross_ring(g, kt, first, last):
                                r = (start_bank(first) + k) % 3
                                if kind == "scores":
                                    row_max(use + k, r, a[0], b * G + g + a[1])
                                elif kind == "maxima":
                                    maxima_out(use + k, r, g, b + 1)
                                elif kind == "sums":
                                    pg = (g - 1) % G
                                    vector_sums(dve, filled, normed, drained, use + k, b * G + g - 1,
                                                pg, ring[r], rec[pg % 2], y)
                                elif kind == "turn":
                                    vector_turn(dve, filled, drained, use + k, a, ring[r], yT)
                                else:
                                    vector_output(dve, filled, drained, use + k, a, ring[r], x, b - 1)
                                    done = use + k + 1
                                k += 1
                        if g == 1 and not first:
                            dve.wait_ge(drained, done)
                            norm_stats(dve, next_norm, x, b - 1)

                over_batches(dve, batch)
                vector_sums(dve, filled, normed, drained, AFTER, NG - 1, G - 1, ring[AFTER % 3],
                            rec[(G - 1) % 2], y)
                n = AFTER + 1
                vector_turn(dve, filled, drained, n, range(TT), ring[n % 3], yT)
                vector_output(dve, filled, drained, n + 1, range(TT), ring[(n + 1) % 3], x, B - 1)
                dve.wait_ge(drained, n + 2)
                norm_stats(dve, next_norm, x, B - 1)


FT = F // P
HU = E * FT


class Experts:

    def __init__(self, nc, ctx):
        def sb(name, shape):
            return ctx.enter_context(nc.sbuf_tensor("e_" + name, shape, F32))
        self.wr, self.rank = sb("wr", [D, E]), sb("rank", [P, E])
        self.wg, self.wu, self.wd = sb("wg", [D, E, F]), sb("wu", [D, E, F]), sb("wd", [P, E, FT, D])
        self.w_in, = sems(nc, ctx, "e_w_in")

    def load(self, sp, io):
        for dst, src in ((self.wr, io["wr"]), (self.rank, io["rank"]), (self.wg, io["wg"]),
                         (self.wu, io["wu"]), (self.wd, io["wd"])):
            sp.dma_start(dst[:], src).then_inc(self.w_in, 16)

    def self_stacks(self):
        keys = self.wd[:].rearrange("p e f d -> p (e f d)").bitcast(BF16)
        queries = [w[:].rearrange("p e f -> p (e f)").bitcast(BF16) for w in (self.wg, self.wu)]
        return ([keys[:, i * GJ * T:(i + 1) * GJ * T].rearrange("p (n t) -> p n t", n=GJ) for i in range(2)],
                [q[:, 0:2 * GJ * T].rearrange("p (c n t) -> p c n t", c=2, n=GJ) for q in queries])


def expert_stage(nc, io, banks, x, xn, xnT, ident, out, nm, experts):
    with ExitStack() as ctx:
        def sb(name, shape, dt=F32):
            return ctx.enter_context(nc.sbuf_tensor("e_" + name, shape, dt))
        wr, rank, wg, wu, wd, w_in = (experts.wr, experts.rank, experts.wg, experts.wu, experts.wd,
                                      experts.w_in)
        names = "logit p q chosen1 chosen2 score cw"
        r = {n: sb("r_" + n, [P, NT, E]) for n in names.split()}
        s = {n: sb("s_" + n, [P, NT]) for n in "top sum inv first second best den".split()}
        wg_p, wu_p = ([sb(f"{n}_part{j}", [P, E, F], F32R) for j in range(2)] for n in ("wg", "wu"))
        x_p = [sb(f"x_part{j}", [D, N], F32R) for j in range(2)]
        weights = [(wg, wg_p), (wu, wu_p)]
        act_out = [sb(f"silu{i}", [P, CK]) for i in range(2)]
        hid = [sb(f"hid{i}", [P, CK]) for i in range(4)]
        res = sb("res", [P, NT, D])
        (logits, shifted, exped, step, up, silued, hidden, downed, added, stored_out, w_first, w_second,
         x_first, x_second) = sems(
            nc, ctx, "e_logits e_shifted e_exped e_step e_up e_silued e_hidden e_downed e_added "
                     "e_stored_out e_w_first e_w_second e_x_first e_x_second")
        PAIRS = ((0, 0), (0, 1), (1, 0))
        AHEAD = 3

        def tiles(a, c):
            return a[:, CT * c:CT * (c + 1), :] if isinstance(c, int) else a[:, bass.ds(c * CT, CT), :]

        gate, upb = banks[0:2], banks[2:4]
        yb = banks[4:6]

        with nc.Block() as block:

            @block.sync
            def _(sp):
                def store(c):
                    sp.wait_ge(added, (c + 1) * E * CT)
                    dst = out[c * CK:(c + 1) * CK, :] if isinstance(c, int) else out[bass.ds(c * CK, CK), :]
                    sp.dma_start(dst.rearrange("(t p) d -> p t d", p=P), tiles(res, c))\
                      .then_inc(stored_out, 16)

                with sp.Fori(0, NC) as c:
                    store(c)
                sp.wait_ge(stored_out, 16 * NC)

            @block.tensor
            def _(pe):
                norm_tensor(pe, nm, xn, ident, banks[5:7], 0)
                for c in range(NC):
                    if c + 1 < NC:
                        norm_tensor(pe, nm, xn, ident, banks[5:7], c + 1)
                    pe.wait_ge(nm.out, c + 1)
                    if c == 0:
                        pe.wait_ge(w_in, 16 * 5)
                    for t in range(CT * c, CT * (c + 1)):
                        mm = pe.matmul(banks[7][:, t * E:(t + 1) * E], xnT[:, t * P:(t + 1) * P], wr[:],
                                       start=True, stop=True, skip_group_check=True)
                mm.then_inc(logits, 1)

                def product(out, stationary, moving):
                    for n, (i, j) in enumerate(PAIRS):
                        mm = pe.matmul(out, stationary(i), moving(j), start=(n == 0),
                                       stop=(n == len(PAIRS) - 1))
                    return mm

                def hidden_units(c, k, first):
                    e, f = divmod(k, FT)
                    o = slice(c * CK, (c + 1) * CK) if isinstance(c, int) else bass.ds(c * CK, CK)
                    if not (first and k < 2):
                        pe.wait_ge(hidden, c * HU + k - 1)
                    if first and f == 0:
                        pe.wait_ge(w_second, 2 * e + 2)
                    for bank, w in ((gate[k % 2], wg_p), (upb[k % 2], wu_p)):
                        product(bank, lambda i: w[i][:, e, f * P:(f + 1) * P], lambda j: x_p[j][:, o])\
                            .then_inc(up, 1)

                def down(c, e, first):
                    pe.wait_ge(hidden, c * HU + FT * (e + 1))
                    if not (first and e < 2):
                        pe.wait_ge(added, (c * E + e - 1) * CT)
                    for t in range(CT):
                        for f in range(FT):
                            mm = pe.matmul(yb[e % 2][:, t * D:(t + 1) * D],
                                           hid[(FT * e + f) % 4][:, t * P:(t + 1) * P], wd[:, e, f, :],
                                           start=(f == 0), stop=(f == FT - 1), skip_group_check=True)
                    mm.then_inc(downed, 1)

                def piece(c, first):
                    for e in range(E):
                        for f in range(FT):
                            hidden_units(c, FT * e + f, first)
                        if e > 0:
                            down(c, e - 1, first)
                        elif not first:
                            down(c - 1, E - 1, False)

                pe.wait_ge(x_second, 1)
                piece(0, True)
                pe.wait_ge(x_second, NC)
                with pe.Fori(1, NC) as c:
                    piece(c, False)
                down(NC - 1, E - 1, False)

            @block.scalar
            def _(act):
                def split_weights(e):
                    for whole, parts in weights:
                        act.copy(parts[0][:, e, :], whole[:, e, :]).then_inc(w_first, 1)

                norm_scalar_root(act, nm)
                act.wait_ge(w_in, 16 * 5)
                for c in range(NC):
                    if c < AHEAD:
                        split_weights(c)
                    act.wait_ge(nm.turned, c + 1)
                    act.copy(x_p[0][:, c * CK:(c + 1) * CK], banks[5 + c % 2]).then_inc(x_first, 1)
                    norm_scalar_out(act, nm, banks[5:7], xnT, c)
                act.wait_ge(shifted, 1)
                act.activation(r["p"][:], r["p"][:], ACT.Exp).then_inc(exped, 1)

                def piece(c, first):
                    for k in range(HU):
                        act.wait_ge(up, 2 * (c * HU + k) + 1)
                        if not (first and k < 2):
                            act.wait_ge(hidden, c * HU + k - 1)
                        act.activation(act_out[k % 2][:], gate[k % 2], ACT.Silu).then_inc(silued, 1)
                        if first and k % FT == 0 and k // FT + AHEAD < E:
                            split_weights(k // FT + AHEAD)

                piece(0, True)
                with act.Fori(1, NC) as c:
                    piece(c, False)

            @block.gpsimd
            def _(pool):
                def split_weights(e):
                    for n, (whole, parts) in enumerate(weights):
                        pool.wait_ge(w_first, 2 * e + n + 1)
                        pool.tensor_tensor(parts[1][:, e, :], whole[:, e, :],
                                           parts[0][:, e, :].bitcast(F32), ALU.subtract).then_inc(w_second, 1)

                for c in range(NC):
                    if c < AHEAD:
                        split_weights(c)
                    o = slice(c * CK, (c + 1) * CK)
                    pool.wait_ge(x_first, c + 1)
                    pool.wait_ge(nm.out, c + 1)
                    pool.tensor_tensor(x_p[1][:, o], xnT[:, o], x_p[0][:, o].bitcast(F32), ALU.subtract)\
                        .then_inc(x_second, 1)

                for e in range(AHEAD, E):
                    split_weights(e)

            @block.vector
            def _(dve):
                norm_vector(dve, nm, x, xn)
                dve.wait_ge(w_in, 16 * 5)
                dve.wait_ge(logits, 1)
                n = [0]

                def then(ins):
                    n[0] += 1
                    ins.then_inc(step, 1)
                    dve.wait_ge(step, n[0])

                def wide(a):
                    return a[:].unsqueeze(2).broadcast_to([P, NT, E])

                ranks = rank[:].unsqueeze(1).broadcast_to([P, NT, E])
                then(dve.tensor_copy(r["logit"][:], banks[7][:, 0:NT * E].rearrange("p (t e) -> p t e", e=E)))
                then(dve.tensor_reduce(s["top"][:], r["logit"][:], AX.X, ALU.max))
                dve.tensor_tensor(r["p"][:], r["logit"][:], wide(s["top"]), ALU.subtract).then_inc(shifted, 1)
                dve.wait_ge(exped, 1)
                then(dve.tensor_reduce(s["sum"][:], r["p"][:], AX.X, ALU.add))
                then(dve.reciprocal(s["inv"][:], s["sum"][:]))
                then(dve.tensor_tensor(r["p"][:], r["p"][:], wide(s["inv"]), ALU.mult))
                left = "p"
                for top, chosen in (("first", "chosen1"), ("second", "chosen2")):
                    then(dve.tensor_reduce(s[top][:], r[left][:], AX.X, ALU.max))
                    then(dve.tensor_tensor(r["score"][:], r[left][:], wide(s[top]), ALU.is_equal))
                    then(dve.tensor_tensor(r["score"][:], r["score"][:], ranks, ALU.mult))
                    then(dve.tensor_reduce(s["best"][:], r["score"][:], AX.X, ALU.max))
                    then(dve.tensor_tensor(r[chosen][:], r["score"][:], wide(s["best"]), ALU.is_equal))
                    if left == "p":
                        then(dve.scalar_tensor_tensor(out=r["q"][:], in0=r[chosen][:], scalar=-2.0,
                                                      in1=r["p"][:], op0=ALU.mult, op1=ALU.add))
                        left = "q"
                then(dve.tensor_tensor(r["score"][:], r["chosen1"][:], r["chosen2"][:], ALU.add))
                then(dve.tensor_tensor(r["score"][:], r["score"][:], r["p"][:], ALU.mult))
                then(dve.tensor_tensor(s["den"][:], s["first"][:], s["second"][:], ALU.add))
                then(dve.tensor_scalar(s["den"][:], s["den"][:], 1e-20, None, ALU.add))
                then(dve.reciprocal(s["inv"][:], s["den"][:]))
                then(dve.tensor_tensor(r["cw"][:], r["score"][:], wide(s["inv"]), ALU.mult))
                assert n[0] == RSTEPS

                def add_expert(c, e):
                    dve.wait_ge(downed, c * E + e + 1)
                    if e > 0:
                        dve.wait_ge(added, (c * E + e) * CT)
                    for t in range(CT):
                        one = slice(CT * c + t, CT * c + t + 1) if isinstance(c, int) else \
                            bass.ds(c * CT + t, 1)
                        so_far = (x if e == 0 else res)[:, one, :].rearrange("p t d -> p (t d)")
                        dve.scalar_tensor_tensor(
                            out=res[:, one, :].rearrange("p t d -> p (t d)"),
                            in0=yb[e % 2][:, t * D:(t + 1) * D],
                            scalar=r["cw"][:, one, e:e + 1].rearrange("p t e -> p (t e)"), in1=so_far,
                            op0=ALU.mult, op1=ALU.add).then_inc(added, 1)

                def piece(c, first):
                    for e in range(E):
                        for f in range(FT):
                            k = FT * e + f
                            dve.wait_ge(silued, c * HU + k + 1)
                            dve.wait_ge(up, 2 * (c * HU + k) + 2)
                            if not (first and e < 2):
                                dve.wait_ge(downed, c * E + e - 1)
                            dve.tensor_tensor(hid[k % 4][:], upb[k % 2], act_out[k % 2][:], ALU.mult)\
                               .then_inc(hidden, 1)
                        if e > 0:
                            add_expert(c, e - 1)
                        elif not first:
                            add_expert(c - 1, E - 1)

                piece(0, True)
                with dve.Fori(1, NC) as c:
                    piece(c, False)
                add_expert(NC - 1, E - 1)


RSTEPS = 22


def decoder_layer(nc, io, out):
    with ExitStack() as ctx:
        def sb(name, shape, dt=F32):
            return ctx.enter_context(nc.sbuf_tensor(name, shape, dt))

        def scratch(name, shape, dt):
            return nc.dram_tensor(name, shape, dt, kind="Internal").ap()
        scr = {
            "ks": scratch("scr_ks", [B, 2, KROWS, GJ, S2], BF16),
            "qs": scratch("scr_qs", [2, PROWS, GJ, N], BF16),
            "v": scratch("scr_v", [B, P, G * KT * 4 * VW], F32),
            "ks_self": scratch("scr_ks_self", [2, PROWS, GJ, N], BF16),
            "qs_self": scratch("scr_qs_self", [2, PROWS, GJ, N], BF16),
        }
        x, xn, xnT = sb("x", [P, NT, D]), sb("xn", [P, NT, D]), sb("xnT", [D, N])
        ident, identb = sb("ident", [P, P]), sb("identb", [P, P], BF16)
        v_all, bo = sb("v_all", [P, NT, H, VW]), sb("self_bo", [P, D])
        query_norm, expert_norm = Norm(nc, ctx, "q_n_"), Norm(nc, ctx, "e_n_")
        experts = Experts(nc, ctx)
        self_stacks = Stacks(nc, ctx, "s", *experts.self_stacks())
        S4 = ctx.enter_context(nc.psum_tensor("S4", [P, 4 * 512], F32))
        ring = [ctx.enter_context(nc.psum_tensor(f"ring{i}", [P, 512], F32)) for i in range(3)]
        U = ctx.enter_context(nc.psum_tensor("U", [P, 512], F32))
        banks = [S4[:, 512 * i:512 * (i + 1)] for i in range(4)] + [r[:] for r in ring] + [U[:]]
        with ExitStack() as held:
            context = Context(nc, held)
            cross_stacks = Stacks(
                nc, held, "x",
                [held.enter_context(nc.sbuf_tensor(f"x_k{i}", [P, 2, S2], BF16)) for i in range(G)],
                [held.enter_context(nc.sbuf_tensor(f"x_q{i}", [P, 2, 2, T], BF16)) for i in range(G)])
            lent = [k[:].rearrange("p j k -> p (j k)")[:, 0:N] for k in cross_stacks.kb] + \
                   [k[:].bitcast(BF16)[:, 0:N] for k in (context.keys, context.rest)]
            self_operands = [(scr["qs_self"], [lent[0], lent[1], lent[4]], Q_PART),
                             (scr["ks_self"], [lent[2], lent[3], lent[5]], K_PART)]
            v_lent = v_all[:].rearrange("p t h v -> p (t h v)").bitcast(BF16)
            query_operands = [(scr["qs"], [v_lent[:, 0:N], v_lent[:, N:2 * N], lent[4]], Q_PART)]
            self_projection_stage(nc, io, scr, banks, x, xn, xnT, v_all, bo, U[:], self_stacks,
                                  self_operands, ident, identb, context)
            self_attention_stage(nc, io, scr, ring, S4[:], U, x, v_all, bo, self_stacks, self_operands,
                                 cross_stacks, ident, identb, context, query_norm)
            query_stage(nc, io, scr, banks, x, xn, xnT, cross_stacks, query_operands, ident, query_norm)
            cross_attention_stage(nc, io, scr, ring, S4[:], U, x, cross_stacks, query_operands, ident,
                                  identb, context, expert_norm, experts)
        expert_stage(nc, io, banks, x, xn, xnT, ident, out, expert_norm, experts)


def _layouts(a):
    c = np.ascontiguousarray
    perm = np.array([(4 * g + 2 * j + par) * DK + d
                     for par in range(2) for d in range(DK) for g in range(G) for j in range(2)])
    swap = np.array([(e // DK) * DK + (e % DK + DK // 2) % DK for e in perm])
    def row(b):
        return np.broadcast_to(b, (P, D))

    half = DK // 2
    freq = (1.0 / 10000.0 ** (2.0 * np.arange(half, dtype=np.float32) / DK)).astype(np.float32)
    ang = np.arange(T, dtype=np.float32)[:, None] * freq[None, :]
    d = perm % DK
    cos = np.cos(ang)[:, d % half].T.astype(np.float32)
    sin = (np.sin(ang)[:, d % half] * np.where(d < half, -1, 1)).T.astype(np.float32)
    hidden = np.where(np.arange(P)[None, :] > np.arange(P)[:, None], MASKED, 0).astype(np.float32)
    scale = np.float32(SCALE)
    return {
        "x": a["x"].reshape(N, D),
        "ctxT": c(a["ctx_1024"].transpose(2, 0, 1).reshape(D, B * S2)),
        "weights": a["fside_BxS2_0"],
        "w_q": c(a["L0_attn_WQ_w"].T[:, perm]), "w_q_swap": c(a["L0_attn_WQ_w"].T[:, swap]),
        "w_k": c(a["L0_attn_WK_w"].T[:, perm]), "w_k_swap": c(a["L0_attn_WK_w"].T[:, swap]),
        "b_q": a["L0_attn_WQ_b"][perm, None], "b_q_swap": a["L0_attn_WQ_b"][swap, None],
        "b_k": a["L0_attn_WK_b"][perm, None], "b_k_swap": a["L0_attn_WK_b"][swap, None],
        "rot_q": cos * scale, "rot_q_swap": sin * scale, "rot_k": cos, "rot_k_swap": sin,
        "swv": c(a["L0_attn_WV_w"].T), "sbv": row(a["L0_attn_WV_b"]),
        "swo": c(a["L0_attn_Wo_w"].T), "sbo": row(a["L0_attn_Wo_b"]),
        "xwq": c(a["L0_xattn_wq"][:, perm]), "xbq": a["L0_xattn_bq"][perm, None],
        "xwk": c(a["L0_xattn_wk"][:, perm]), "xbk": a["L0_xattn_bk"][perm, None],
        "xwv": a["L0_xattn_wv"], "xbv": row(a["L0_xattn_bv"]),
        "xwo": a["L0_xattn_wo"], "xbo": row(a["L0_xattn_bo"]),
        "wr": c(a["L0_ffn_gate_w"].T),
        "wg": c(a["L0_ffn_w_gate"].transpose(1, 0, 2)), "wu": c(a["L0_ffn_w_up"].transpose(1, 0, 2)),
        "wd": c(a["L0_ffn_w_down"].reshape(E, FT, P, D).transpose(2, 0, 1, 3)),
        "ident": np.eye(P, dtype=np.float32),
        "masks": np.stack([hidden, hidden.T], 1),
        "rank": np.broadcast_to(np.arange(E, 0, -1).astype(np.float32), (P, E)),
    }


def kernel(**inputs):
    import concourse.bacc as bacc
    from concourse.bass_utils import run_bass_kernel_spmd

    nc = bacc.Bacc("TRN2", target_bir_lowering=False, num_devices=1)
    arrays, io = {}, {}
    for name, a in _layouts({k: np.asarray(v) for k, v in inputs.items()}).items():
        a = np.ascontiguousarray(a)
        arrays[f"in_{name}"] = a
        io[name] = nc.dram_tensor(f"in_{name}", a.shape, mybir.dt.from_np(a.dtype),
                                  kind="ExternalInput").ap()
    out = nc.dram_tensor("out", [N, D], F32, kind="ExternalOutput").ap()
    decoder_layer(nc, io, out)
    r = run_bass_kernel_spmd(nc, [arrays], core_ids=[0])
    return r.results[0]["out"].reshape(B, T, D)
```
